# Optimizing a Trainium2 kernel written in Bass

```python
import numpy as np
import jax
import jax.numpy as jnp

def _softmax(x, axis=-1):
    return jax.nn.softmax(x, axis=axis)

def _gelu(x):
    return jax.nn.gelu(x, approximate=True)

def _silu(x):
    return jax.nn.silu(x)

def _sigmoid(x):
    return jax.nn.sigmoid(x)

def _layernorm(x, axis=-1, eps=1e-05):
    m = jnp.mean(x, axis=axis, keepdims=True)
    v = jnp.var(x, axis=axis, keepdims=True)
    return (x - m) / jnp.sqrt(v + eps)

def _scatter_add(tgt, idx, src, axis=0):
    return tgt.at[idx].add(src)

def _segment_sum(src, seg, n):
    return jax.ops.segment_sum(src, seg, n)
kernel_name = 'mk_perceiver_d4_seqx_r4_76f787'

def setup_inputs(seed: int=0):
    np.random.seed(seed)
    _w = jnp.asarray

    def _rec_inputs():
        import jax
        import jax.numpy as jnp
        _rk = jax.random.key(seed)
        x = -0.0002928 + 1 * jax.random.normal(jax.random.fold_in(_rk, 1), (1, 128, 256), jnp.float32)
        _lenS = 128 - jax.random.randint(jax.random.fold_in(_rk, 7), (1,), 0, max(1, 128 // 4) + 1, jnp.int32)
        _lenS2 = 12544 - jax.random.randint(jax.random.fold_in(_rk, 8), (1,), 0, max(1, 12544 // 4) + 1, jnp.int32)
        _ctx_1024P = jax.random.normal(jax.random.fold_in(_rk, 11), (1, 16, 256), jnp.float32)
        _ctx_1024c = jax.random.dirichlet(jax.random.fold_in(_rk, 511), 0.3 * jnp.ones((16,), jnp.float32), (1, 12544))
        _ctx_1024t = jnp.einsum('bsk,bkd->bsd', _ctx_1024c, _ctx_1024P)
        _ctx_1024t = _ctx_1024t * jax.lax.rsqrt(jnp.mean(jnp.square(_ctx_1024t)) + 1e-12) * 0.953939
        ctx_1024 = -1.39393e-06 + 0.999914 * (_ctx_1024t + 0.3 * jax.random.normal(jax.random.fold_in(_rk, 611), (1, 12544, 256), jnp.float32))
        _validS = jnp.arange(128)[None, :] < _lenS[:, None]
        _validS2 = jnp.arange(12544)[None, :] < _lenS2[:, None]
        _causal = jnp.tril(jnp.ones((128, 128), dtype=bool))
        mask_BxS2_bf1 = jnp.ones((1, 12544), dtype=bool)
        return (x, ctx_1024, mask_BxS2_bf1)
    x, ctx_1024, mask_BxS2_bf1 = _rec_inputs()

    def _L0_xattn_setup():
        import jax, jax.numpy as jnp
        import numpy as np
        B, N, D = (2, 512, 256)
        H = 16
        DH = D // H
        key = jax.random.key(seed)
        ks = jax.random.split(key, 10)
        s = 0.02
        return {'x_q': jax.random.normal(ks[0], (B, N, D), dtype=jnp.float32), 'x_kv': jax.random.normal(ks[1], (B, N, D), dtype=jnp.float32), 'Wq': jax.random.normal(ks[2], (D, D), dtype=jnp.float32) * s, 'bq': jnp.zeros((D,), dtype=jnp.float32), 'Wk': jax.random.normal(ks[3], (D, D), dtype=jnp.float32) * s, 'bk': jnp.zeros((D,), dtype=jnp.float32), 'Wv': jax.random.normal(ks[4], (D, D), dtype=jnp.float32) * s, 'bv': jnp.zeros((D,), dtype=jnp.float32), 'Wo': jax.random.normal(ks[5], (D, D), dtype=jnp.float32) * s, 'bo': jnp.zeros((D,), dtype=jnp.float32)}
    _L0_xattn_all = _L0_xattn_setup()
    _L0_xattn_in = {k: v for k, v in _L0_xattn_all.items() if k in ('Wq', 'bq', 'Wk', 'bk', 'Wv', 'bv', 'Wo', 'bo')}
    del _L0_xattn_all

    def _L0_attn_setup():
        import jax, jax.numpy as jnp
        import numpy as np
        D_MODEL = 256
        N_HEADS = 16
        HEAD_DIM = D_MODEL // N_HEADS
        KV_LATENT = 64
        LN_EPS = 1e-05

        def apply_rope(x):
            b, h, t, d = x.shape
            half = d // 2
            pos = jnp.arange(t, dtype=x.dtype)[:, None]
            inv_freq = 1.0 / 10000.0 ** (jnp.arange(half, dtype=x.dtype) / half)
            angles = pos * inv_freq[None, :]
            sin = jnp.sin(angles)[None, None]
            cos = jnp.cos(angles)[None, None]
            x1, x2 = (x[..., :half], x[..., half:])
            return jnp.concatenate([x1 * cos - x2 * sin, x1 * sin + x2 * cos], axis=-1)
        key = jax.random.key(seed)
        ks = jax.random.split(key, 6)
        d, L = (D_MODEL, KV_LATENT)
        s = 1.0 / np.sqrt(d)
        sl = 1.0 / np.sqrt(L)
        return {'x': jax.random.normal(ks[0], (2, 512, d), dtype=jnp.float32), 'W_q': jax.random.uniform(ks[1], (d, d), jnp.float32, -s, s), 'W_dkv': jax.random.uniform(ks[2], (d, L), jnp.float32, -s, s), 'W_uk': jax.random.uniform(ks[3], (L, d), jnp.float32, -sl, sl), 'W_uv': jax.random.uniform(ks[4], (L, d), jnp.float32, -sl, sl), 'W_o': jax.random.uniform(ks[5], (d, d), jnp.float32, -s, s), 'ln_gamma': jnp.ones((L,), jnp.float32), 'ln_beta': jnp.zeros((L,), jnp.float32)}
    _L0_attn_all = _L0_attn_setup()
    _L0_attn_in = {k: v for k, v in _L0_attn_all.items() if k in ('W_q', 'W_dkv', 'W_uk', 'W_uv', 'W_o', 'ln_gamma', 'ln_beta')}
    del _L0_attn_all

    def _L0_ffn_setup():
        import jax, jax.numpy as jnp
        import numpy as np
        BLOCK = 32
        W_BITS = 4
        ACT_BITS = 16

        def act_qdq(x):
            qmax = 2.0 ** (ACT_BITS - 1) - 1.0
            scale = jnp.maximum(jnp.max(jnp.abs(x)) / qmax, 1e-12)
            return jnp.clip(jnp.round(x / scale), -qmax - 1.0, qmax) * scale

        def fixed_qdq_u16(x):
            scale = 1.0 / 65536.0
            return jnp.clip(jnp.round(x / scale), 0.0, 65535.0) * scale

        def lpbq_dequant(w):
            O, I = w.shape
            qmax = 2.0 ** (W_BITS - 1) - 1.0
            wb = w.reshape(O, I // BLOCK, BLOCK)
            s = jnp.maximum(jnp.max(jnp.abs(wb), axis=-1, keepdims=True) / qmax, 1e-12)
            wq = jnp.clip(jnp.round(wb / s), -qmax - 1.0, qmax) * s
            return wq.reshape(O, I)
        key = jax.random.key(seed)
        k1, k2, k3, k4 = jax.random.split(key, 4)
        B, S, H, I = (2, 1024, 256, 768)
        x = jax.random.normal(k1, (B, S, H), jnp.float32)
        w_gate = jax.random.normal(k2, (I, H), jnp.float32) * 0.02
        w_up = jax.random.normal(k3, (I, H), jnp.float32) * 0.02
        w_down = jax.random.normal(k4, (H, I), jnp.float32) * 0.02
        return {'x': x, 'w_gate': w_gate, 'w_up': w_up, 'w_down': w_down}
    _L0_ffn_all = _L0_ffn_setup()
    _L0_ffn_in = {k: v for k, v in _L0_ffn_all.items() if k in ('w_gate', 'w_up', 'w_down')}
    del _L0_ffn_all

    def _L1_xattn_setup():
        import jax, jax.numpy as jnp
        import numpy as np
        N_HEADS = 16
        D_MODEL = 256
        HEAD_DIM = D_MODEL // N_HEADS
        MASK_FILL = -100000000.0

        def _split_heads(x):
            B, S, _ = x.shape
            return x.reshape(B, S, N_HEADS, HEAD_DIM).transpose(0, 2, 1, 3)
        key = jax.random.key(seed)
        ks = jax.random.split(key, 12)
        B, L, P = (2, 512, 512)
        s = 1.0 / np.sqrt(D_MODEL).astype(np.float32)
        inp = {'q': jax.random.normal(ks[0], (B, L, D_MODEL), dtype=jnp.float32), 'k': jax.random.normal(ks[1], (B, P, D_MODEL), dtype=jnp.float32), 'v': jax.random.normal(ks[2], (B, P, D_MODEL), dtype=jnp.float32), 'attention_mask': jnp.ones((B, P), dtype=bool), 'Wq': jax.random.normal(ks[3], (D_MODEL, D_MODEL), dtype=jnp.float32) * s, 'bq': jnp.zeros((D_MODEL,), dtype=jnp.float32), 'Wk': jax.random.normal(ks[4], (D_MODEL, D_MODEL), dtype=jnp.float32) * s, 'bk': jnp.zeros((D_MODEL,), dtype=jnp.float32), 'Wv': jax.random.normal(ks[5], (D_MODEL, D_MODEL), dtype=jnp.float32) * s, 'bv': jnp.zeros((D_MODEL,), dtype=jnp.float32), 'Wo': jax.random.normal(ks[6], (D_MODEL, D_MODEL), dtype=jnp.float32) * s, 'bo': jnp.zeros((D_MODEL,), dtype=jnp.float32)}
        return inp
    _L1_xattn_all = _L1_xattn_setup()
    _L1_xattn_in = {k: v for k, v in _L1_xattn_all.items() if k in ('Wq', 'bq', 'Wk', 'bk', 'Wv', 'bv', 'Wo', 'bo')}
    del _L1_xattn_all

    def _L1_attn_setup():
        import jax, jax.numpy as jnp
        import numpy as np
        HEADS = 32
        DIM_HEAD = 32
        EPS = 1e-06
        key = jax.random.key(seed)
        k1, k2, k3 = jax.random.split(key, 3)
        b, n, dim = (2, 512, 256)
        x = jax.random.normal(k1, (b, n, dim), dtype=jnp.float32)
        w_qkv = jax.random.normal(k2, (dim, 3 * HEADS * DIM_HEAD), dtype=jnp.float32) * dim ** (-0.5)
        w_out = jax.random.normal(k3, (HEADS * DIM_HEAD, dim), dtype=jnp.float32) * dim ** (-0.5)
        b_out = jnp.zeros((dim,), dtype=jnp.float32)
        ln_gamma = jnp.ones((dim,), dtype=jnp.float32)
        ln_beta = jnp.zeros((dim,), dtype=jnp.float32)
        return {'x': x, 'w_qkv': w_qkv, 'w_out': w_out, 'b_out': b_out, 'ln_gamma': ln_gamma, 'ln_beta': ln_beta}
    _L1_attn_all = _L1_attn_setup()
    _L1_attn_in = {k: v for k, v in _L1_attn_all.items() if k in ('w_qkv', 'w_out', 'b_out', 'ln_gamma', 'ln_beta')}
    del _L1_attn_all

    def _L1_ffn_setup():
        import jax, jax.numpy as jnp
        import numpy as np
        from jax import lax
        D = 256
        H = 1024
        E = 8
        TOPK = 2
        key = jax.random.key(seed)
        ks = jax.random.split(key, 7)
        s = 0.02
        return {'x': jax.random.normal(ks[0], (2, 512, D), dtype=jnp.float32), 'W1': jax.random.normal(ks[1], (E, D, H), dtype=jnp.float32) * s, 'b1': jnp.zeros((E, H), dtype=jnp.float32), 'W2': jax.random.normal(ks[2], (E, H, D), dtype=jnp.float32) * s, 'b2': jnp.zeros((E, D), dtype=jnp.float32), 'Wr': jax.random.normal(ks[3], (D, E), dtype=jnp.float32) * s, 'br': jnp.zeros((E,), dtype=jnp.float32)}
    _L1_ffn_all = _L1_ffn_setup()
    _L1_ffn_in = {k: v for k, v in _L1_ffn_all.items() if k in ('W1', 'b1', 'W2', 'b2', 'Wr', 'br')}
    del _L1_ffn_all

    def _L2_xattn_setup():
        import jax, jax.numpy as jnp
        import numpy as np
        import math
        B, L, D = (4, 1024, 256)
        M = 64
        EPS = 1e-06
        key = jax.random.key(seed)
        kq, kk, kv, kp = jax.random.split(key, 4)
        Q = jax.random.normal(kq, (B, L, D), dtype=jnp.float32)
        K = jax.random.normal(kk, (B, L, D), dtype=jnp.float32)
        V = jax.random.normal(kv, (B, L, D), dtype=jnp.float32)
        projection = jax.random.normal(kp, (M, D), dtype=jnp.float32)
        return {'Q': Q, 'K': K, 'V': V, 'projection': projection}
    _L2_xattn_all = _L2_xattn_setup()
    _L2_xattn_in = {k: v for k, v in _L2_xattn_all.items() if k in ('projection',)}
    del _L2_xattn_all

    def _L2_attn_setup():
        import jax, jax.numpy as jnp
        import numpy as np
        import math
        DIM = 256
        N_HEADS = 16
        HEAD_DIM = DIM // N_HEADS
        B, S = (2, 512)
        key = jax.random.key(seed)
        k_x, k_wqkv, k_bqkv, k_wout, k_bout = jax.random.split(key, 5)
        scale_in = 1.0 / math.sqrt(DIM)
        x = jax.random.normal(k_x, (B, S, DIM), dtype=jnp.float32)
        Wqkv = jax.random.uniform(k_wqkv, (N_HEADS, DIM, 3 * HEAD_DIM), dtype=jnp.float32, minval=-scale_in, maxval=scale_in)
        bqkv = jax.random.uniform(k_bqkv, (N_HEADS, 3 * HEAD_DIM), dtype=jnp.float32, minval=-scale_in, maxval=scale_in)
        Wout = jax.random.uniform(k_wout, (DIM, DIM), dtype=jnp.float32, minval=-scale_in, maxval=scale_in)
        bout = jax.random.uniform(k_bout, (DIM,), dtype=jnp.float32, minval=-scale_in, maxval=scale_in)
        return {'x': x, 'Wqkv': Wqkv, 'bqkv': bqkv, 'Wout': Wout, 'bout': bout}
    _L2_attn_all = _L2_attn_setup()
    _L2_attn_in = {k: v for k, v in _L2_attn_all.items() if k in ('Wqkv', 'bqkv', 'Wout', 'bout')}
    del _L2_attn_all

    def _L2_ffn_setup():
        import jax, jax.numpy as jnp
        import numpy as np
        FP8_MAX = 448.0

        def quant_fp8(x):
            amax = jnp.max(jnp.abs(x)).astype(jnp.float32)
            scale = jnp.minimum(FP8_MAX / jnp.maximum(amax, 1e-12), FP8_MAX)
            x_fp8 = jnp.clip(x * scale, -FP8_MAX, FP8_MAX).astype(jnp.float8_e4m3fn)
            return (x_fp8, 1.0 / scale)
        key = jax.random.key(seed)
        k1, k2, k3 = jax.random.split(key, 3)
        B, S, IN, OUT = (4, 2048, 256, 256)
        input = jax.random.normal(k1, (B, S, IN), dtype=jnp.float32)
        bound = 1.0 / np.sqrt(IN)
        weight = jax.random.uniform(k2, (OUT, IN), dtype=jnp.float32, minval=-bound, maxval=bound)
        bias = jax.random.uniform(k3, (OUT,), dtype=jnp.float32, minval=-bound, maxval=bound)
        return {'input': input, 'weight': weight, 'bias': bias}
    _L2_ffn_all = _L2_ffn_setup()
    _L2_ffn_in = {k: v for k, v in _L2_ffn_all.items() if k in ('weight', 'bias')}
    del _L2_ffn_all

    def _L3_xattn_setup():
        import jax, jax.numpy as jnp
        import numpy as np
        D_MODEL = 256
        N_HEADS = 16
        D_K = D_MODEL // N_HEADS
        key = jax.random.key(seed)
        ks = jax.random.split(key, 16)
        B, S = (2, 512)
        sc = 1.0 / np.sqrt(D_MODEL)
        inp = {'query': jax.random.normal(ks[0], (B, S, D_MODEL), jnp.float32), 'key': jax.random.normal(ks[1], (B, S, D_MODEL), jnp.float32), 'value': jax.random.normal(ks[2], (B, S, D_MODEL), jnp.float32), 'Wq': jax.random.normal(ks[3], (D_MODEL, D_MODEL), jnp.float32) * sc, 'bq': jnp.zeros((D_MODEL,), jnp.float32), 'Wk': jax.random.normal(ks[4], (D_MODEL, D_MODEL), jnp.float32) * sc, 'bk': jnp.zeros((D_MODEL,), jnp.float32), 'Wv': jax.random.normal(ks[5], (D_MODEL, D_MODEL), jnp.float32) * sc, 'bv': jnp.zeros((D_MODEL,), jnp.float32), 'Wo': jax.random.normal(ks[6], (D_MODEL, D_MODEL), jnp.float32) * sc, 'bo': jnp.zeros((D_MODEL,), jnp.float32), 'theta': jax.random.normal(ks[7], (N_HEADS,), jnp.float32) * 0.1, 'gate': jax.random.normal(ks[8], (D_MODEL,), jnp.float32) * 0.1}
        return inp
    _L3_xattn_all = _L3_xattn_setup()
    _L3_xattn_in = {k: v for k, v in _L3_xattn_all.items() if k in ('Wq', 'bq', 'Wk', 'bk', 'Wv', 'bv', 'Wo', 'bo', 'theta', 'gate')}
    del _L3_xattn_all

    def _L3_attn_setup():
        import jax, jax.numpy as jnp
        import numpy as np
        D_IN = 256
        D_ATT = 256
        D_OUT = 256
        N, S = (8, 1024)
        key = jax.random.key(seed)
        ks = jax.random.split(key, 5)
        sc_in = 1.0 / np.sqrt(D_IN)
        sc_att = 1.0 / np.sqrt(D_ATT)
        return {'x': jax.random.normal(ks[0], (N, S, D_IN), dtype=jnp.float32), 'Wq': jax.random.normal(ks[1], (D_IN, D_ATT), dtype=jnp.float32) * sc_in, 'bq': jnp.zeros((D_ATT,), dtype=jnp.float32), 'Wk': jax.random.normal(ks[2], (D_IN, D_ATT), dtype=jnp.float32) * sc_in, 'bk': jnp.zeros((D_ATT,), dtype=jnp.float32), 'Wv': jax.random.normal(ks[3], (D_IN, D_ATT), dtype=jnp.float32) * sc_in, 'bv': jnp.zeros((D_ATT,), dtype=jnp.float32), 'Wo': jax.random.normal(ks[4], (D_ATT, D_OUT), dtype=jnp.float32) * sc_att, 'bo': jnp.zeros((D_OUT,), dtype=jnp.float32)}
    _L3_attn_all = _L3_attn_setup()
    _L3_attn_in = {k: v for k, v in _L3_attn_all.items() if k in ('Wq', 'bq', 'Wk', 'bk', 'Wv', 'bv', 'Wo', 'bo')}
    del _L3_attn_all

    def _L3_ffn_setup():
        import jax, jax.numpy as jnp
        import numpy as np
        TOP_K = 2
        key = jax.random.key(seed)
        ks = jax.random.split(key, 7)
        B_, S, D, F, E, R = (2, 512, 256, 1024, 4, 4)
        x = jax.random.normal(ks[0], (B_, S, D), dtype=jnp.float32)
        Wg = jax.random.normal(ks[1], (E, D), dtype=jnp.float32) * (1.0 / np.sqrt(D))
        bg = jnp.zeros((E,), dtype=jnp.float32)
        Wi = jax.random.normal(ks[2], (F, D), dtype=jnp.float32) * (1.0 / np.sqrt(D))
        Wo = jax.random.normal(ks[3], (D, F), dtype=jnp.float32) * (1.0 / np.sqrt(F))
        A = jax.random.normal(ks[4], (E, R, D), dtype=jnp.float32) * (1.0 / np.sqrt(D))
        Bm = jax.random.normal(ks[5], (E, F, R), dtype=jnp.float32) * 0.01
        return {'x': x, 'Wg': Wg, 'bg': bg, 'Wi': Wi, 'Wo': Wo, 'A': A, 'B': Bm}
    _L3_ffn_all = _L3_ffn_setup()
    _L3_ffn_in = {k: v for k, v in _L3_ffn_all.items() if k in ('Wg', 'bg', 'Wi', 'Wo', 'A', 'B')}
    del _L3_ffn_all
    return {'x': x, 'ctx_1024': ctx_1024, 'mask_BxS2_bf1': mask_BxS2_bf1, 'L0_xattn_Wq': _L0_xattn_in['Wq'], 'L0_xattn_bq': _L0_xattn_in['bq'], 'L0_xattn_Wk': _L0_xattn_in['Wk'], 'L0_xattn_bk': _L0_xattn_in['bk'], 'L0_xattn_Wv': _L0_xattn_in['Wv'], 'L0_xattn_bv': _L0_xattn_in['bv'], 'L0_xattn_Wo': _L0_xattn_in['Wo'], 'L0_xattn_bo': _L0_xattn_in['bo'], 'L0_attn_W_q': _L0_attn_in['W_q'], 'L0_attn_W_dkv': _L0_attn_in['W_dkv'], 'L0_attn_W_uk': _L0_attn_in['W_uk'], 'L0_attn_W_uv': _L0_attn_in['W_uv'], 'L0_attn_W_o': _L0_attn_in['W_o'], 'L0_attn_ln_gamma': _L0_attn_in['ln_gamma'], 'L0_attn_ln_beta': _L0_attn_in['ln_beta'], 'L0_ffn_w_gate': _L0_ffn_in['w_gate'], 'L0_ffn_w_up': _L0_ffn_in['w_up'], 'L0_ffn_w_down': _L0_ffn_in['w_down'], 'L1_xattn_Wq': _L1_xattn_in['Wq'], 'L1_xattn_bq': _L1_xattn_in['bq'], 'L1_xattn_Wk': _L1_xattn_in['Wk'], 'L1_xattn_bk': _L1_xattn_in['bk'], 'L1_xattn_Wv': _L1_xattn_in['Wv'], 'L1_xattn_bv': _L1_xattn_in['bv'], 'L1_xattn_Wo': _L1_xattn_in['Wo'], 'L1_xattn_bo': _L1_xattn_in['bo'], 'L1_attn_w_qkv': _L1_attn_in['w_qkv'], 'L1_attn_w_out': _L1_attn_in['w_out'], 'L1_attn_b_out': _L1_attn_in['b_out'], 'L1_attn_ln_gamma': _L1_attn_in['ln_gamma'], 'L1_attn_ln_beta': _L1_attn_in['ln_beta'], 'L1_ffn_W1': _L1_ffn_in['W1'], 'L1_ffn_b1': _L1_ffn_in['b1'], 'L1_ffn_W2': _L1_ffn_in['W2'], 'L1_ffn_b2': _L1_ffn_in['b2'], 'L1_ffn_Wr': _L1_ffn_in['Wr'], 'L1_ffn_br': _L1_ffn_in['br'], 'L2_xattn_projection': _L2_xattn_in['projection'], 'L2_attn_Wqkv': _L2_attn_in['Wqkv'], 'L2_attn_bqkv': _L2_attn_in['bqkv'], 'L2_attn_Wout': _L2_attn_in['Wout'], 'L2_attn_bout': _L2_attn_in['bout'], 'L2_ffn_weight': _L2_ffn_in['weight'], 'L2_ffn_bias': _L2_ffn_in['bias'], 'L3_xattn_Wq': _L3_xattn_in['Wq'], 'L3_xattn_bq': _L3_xattn_in['bq'], 'L3_xattn_Wk': _L3_xattn_in['Wk'], 'L3_xattn_bk': _L3_xattn_in['bk'], 'L3_xattn_Wv': _L3_xattn_in['Wv'], 'L3_xattn_bv': _L3_xattn_in['bv'], 'L3_xattn_Wo': _L3_xattn_in['Wo'], 'L3_xattn_bo': _L3_xattn_in['bo'], 'L3_xattn_theta': _L3_xattn_in['theta'], 'L3_xattn_gate': _L3_xattn_in['gate'], 'L3_attn_Wq': _L3_attn_in['Wq'], 'L3_attn_bq': _L3_attn_in['bq'], 'L3_attn_Wk': _L3_attn_in['Wk'], 'L3_attn_bk': _L3_attn_in['bk'], 'L3_attn_Wv': _L3_attn_in['Wv'], 'L3_attn_bv': _L3_attn_in['bv'], 'L3_attn_Wo': _L3_attn_in['Wo'], 'L3_attn_bo': _L3_attn_in['bo'], 'L3_ffn_Wg': _L3_ffn_in['Wg'], 'L3_ffn_bg': _L3_ffn_in['bg'], 'L3_ffn_Wi': _L3_ffn_in['Wi'], 'L3_ffn_Wo': _L3_ffn_in['Wo'], 'L3_ffn_A': _L3_ffn_in['A'], 'L3_ffn_B': _L3_ffn_in['B']}

def reference(x, ctx_1024, mask_BxS2_bf1, L0_xattn_Wq, L0_xattn_bq, L0_xattn_Wk, L0_xattn_bk, L0_xattn_Wv, L0_xattn_bv, L0_xattn_Wo, L0_xattn_bo, L0_attn_W_q, L0_attn_W_dkv, L0_attn_W_uk, L0_attn_W_uv, L0_attn_W_o, L0_attn_ln_gamma, L0_attn_ln_beta, L0_ffn_w_gate, L0_ffn_w_up, L0_ffn_w_down, L1_xattn_Wq, L1_xattn_bq, L1_xattn_Wk, L1_xattn_bk, L1_xattn_Wv, L1_xattn_bv, L1_xattn_Wo, L1_xattn_bo, L1_attn_w_qkv, L1_attn_w_out, L1_attn_b_out, L1_attn_ln_gamma, L1_attn_ln_beta, L1_ffn_W1, L1_ffn_b1, L1_ffn_W2, L1_ffn_b2, L1_ffn_Wr, L1_ffn_br, L2_xattn_projection, L2_attn_Wqkv, L2_attn_bqkv, L2_attn_Wout, L2_attn_bout, L2_ffn_weight, L2_ffn_bias, L3_xattn_Wq, L3_xattn_bq, L3_xattn_Wk, L3_xattn_bk, L3_xattn_Wv, L3_xattn_bv, L3_xattn_Wo, L3_xattn_bo, L3_xattn_theta, L3_xattn_gate, L3_attn_Wq, L3_attn_bq, L3_attn_Wk, L3_attn_bk, L3_attn_Wv, L3_attn_bv, L3_attn_Wo, L3_attn_bo, L3_ffn_Wg, L3_ffn_bg, L3_ffn_Wi, L3_ffn_Wo, L3_ffn_A, L3_ffn_B):
    import jax
    import jax.numpy as jnp

    def _L0_xattn_ref(x_q, x_kv, Wq, bq, Wk, bk, Wv, bv, Wo, bo):
        import jax, jax.numpy as jnp
        import numpy as np
        B, N, D = (2, 512, 256)
        H = 16
        DH = D // H
        dp_scale = DH ** (-0.5)

        def split_heads(x):
            b, n, _ = x.shape
            return x.reshape(b, n, H, DH).transpose(0, 2, 1, 3)
        q = split_heads(x_q @ Wq + bq) * dp_scale
        k = split_heads(x_kv @ Wk + bk)
        v = split_heads(x_kv @ Wv + bv)
        i, j = (q.shape[2], k.shape[2])
        causal_mask = jnp.triu(jnp.ones((i, j), dtype=bool), j - i + 1)
        attn = jnp.einsum('bhic,bhjc->bhij', q, k)
        neg = -jnp.finfo(attn.dtype).max
        attn = jnp.where(causal_mask, neg, attn)
        attn = jax.nn.softmax(attn, axis=-1)
        o = jnp.einsum('bhij,bhjc->bhic', attn, v)
        o = o.transpose(0, 2, 1, 3).reshape(x_q.shape[0], i, H * DH)
        return o @ Wo + bo

    def _L0_attn_ref(x, W_q, W_dkv, W_uk, W_uv, W_o, ln_gamma, ln_beta):
        import jax, jax.numpy as jnp
        import numpy as np
        D_MODEL = 256
        N_HEADS = 16
        HEAD_DIM = D_MODEL // N_HEADS
        KV_LATENT = 64
        LN_EPS = 1e-05

        def apply_rope(x):
            b, h, t, d = x.shape
            half = d // 2
            pos = jnp.arange(t, dtype=x.dtype)[:, None]
            inv_freq = 1.0 / 10000.0 ** (jnp.arange(half, dtype=x.dtype) / half)
            angles = pos * inv_freq[None, :]
            sin = jnp.sin(angles)[None, None]
            cos = jnp.cos(angles)[None, None]
            x1, x2 = (x[..., :half], x[..., half:])
            return jnp.concatenate([x1 * cos - x2 * sin, x1 * sin + x2 * cos], axis=-1)
        b, t, _ = x.shape
        q = (x @ W_q).reshape(b, t, N_HEADS, HEAD_DIM).transpose(0, 2, 1, 3)
        lat = x @ W_dkv
        mu = jnp.mean(lat, axis=-1, keepdims=True)
        var = jnp.mean(jnp.square(lat - mu), axis=-1, keepdims=True)
        lat = (lat - mu) * jax.lax.rsqrt(var + LN_EPS) * ln_gamma + ln_beta
        k = (lat @ W_uk).reshape(b, t, N_HEADS, HEAD_DIM).transpose(0, 2, 1, 3)
        v = (lat @ W_uv).reshape(b, t, N_HEADS, HEAD_DIM).transpose(0, 2, 1, 3)
        q = apply_rope(q)
        k = apply_rope(k)
        scores = jnp.einsum('bhqd,bhkd->bhqk', q, k) / jnp.sqrt(jnp.float32(HEAD_DIM))
        causal = jnp.tril(jnp.ones((t, t), dtype=bool))
        scores = jnp.where(causal[None, None], scores, -jnp.inf)
        attn = jax.nn.softmax(scores, axis=-1)
        out = jnp.einsum('bhqk,bhkd->bhqd', attn, v)
        out = out.transpose(0, 2, 1, 3).reshape(b, t, D_MODEL)
        return out @ W_o

    def _L0_ffn_ref(x, w_gate, w_up, w_down):
        import jax, jax.numpy as jnp
        import numpy as np
        BLOCK = 32
        W_BITS = 4
        ACT_BITS = 16

        def act_qdq(x):
            qmax = 2.0 ** (ACT_BITS - 1) - 1.0
            scale = jnp.maximum(jnp.max(jnp.abs(x)) / qmax, 1e-12)
            return jnp.clip(jnp.round(x / scale), -qmax - 1.0, qmax) * scale

        def fixed_qdq_u16(x):
            scale = 1.0 / 65536.0
            return jnp.clip(jnp.round(x / scale), 0.0, 65535.0) * scale

        def lpbq_dequant(w):
            O, I = w.shape
            qmax = 2.0 ** (W_BITS - 1) - 1.0
            wb = w.reshape(O, I // BLOCK, BLOCK)
            s = jnp.maximum(jnp.max(jnp.abs(wb), axis=-1, keepdims=True) / qmax, 1e-12)
            wq = jnp.clip(jnp.round(wb / s), -qmax - 1.0, qmax) * s
            return wq.reshape(O, I)
        x = act_qdq(x)
        up = act_qdq(x @ lpbq_dequant(w_up).T)
        gate = act_qdq(x @ lpbq_dequant(w_gate).T)
        sig = fixed_qdq_u16(jax.nn.sigmoid(gate))
        gate = act_qdq(gate * sig)
        o = act_qdq(gate * up)
        return o @ lpbq_dequant(w_down).T

    def _L1_xattn_ref(q, k, v, attention_mask, Wq, bq, Wk, bk, Wv, bv, Wo, bo):
        import jax, jax.numpy as jnp
        import numpy as np
        N_HEADS = 16
        D_MODEL = 256
        HEAD_DIM = D_MODEL // N_HEADS
        MASK_FILL = -100000000.0

        def _split_heads(x):
            B, S, _ = x.shape
            return x.reshape(B, S, N_HEADS, HEAD_DIM).transpose(0, 2, 1, 3)
        qm = _split_heads(q @ Wq.T + bq)
        km = _split_heads(k @ Wk.T + bk)
        vm = _split_heads(v @ Wv.T + bv)
        scores = jnp.einsum('bnlh,bnph->bnlp', qm, km) / np.sqrt(HEAD_DIM).astype(np.float32)
        mask = attention_mask[:, None, None, :]
        scores = jnp.where(mask, scores, MASK_FILL)
        attn = jax.nn.softmax(scores, axis=-1)
        out = jnp.einsum('bnlp,bnph->bnlh', attn, vm)
        B, _, L, _ = out.shape
        out = out.transpose(0, 2, 1, 3).reshape(B, L, D_MODEL)
        return out @ Wo.T + bo

    def _L1_attn_ref(x, w_qkv, w_out, b_out, ln_gamma, ln_beta):
        import jax, jax.numpy as jnp
        import numpy as np
        HEADS = 32
        DIM_HEAD = 32
        EPS = 1e-06
        b, n, dim = x.shape
        scale = DIM_HEAD ** (-0.5)
        qkv = x @ w_qkv
        qkv = qkv.reshape(b, n, 3, HEADS, DIM_HEAD)
        qkv = jnp.transpose(qkv, (2, 0, 3, 1, 4))
        q, k, v = (qkv[0], qkv[1], qkv[2])
        dots = jnp.einsum('bhnd,bhmd->bhnm', q, k) * scale
        attn = jax.nn.softmax(dots, axis=-1)
        out = jnp.einsum('bhnm,bhmd->bhnd', attn, v)
        out = jnp.transpose(out, (0, 2, 1, 3)).reshape(b, n, HEADS * DIM_HEAD)
        out = out @ w_out + b_out
        mu = jnp.mean(out, axis=-1, keepdims=True)
        var = jnp.mean((out - mu) ** 2, axis=-1, keepdims=True)
        out = (out - mu) / jnp.sqrt(var + EPS) * ln_gamma + ln_beta
        return out

    def _L1_ffn_ref(x, W1, b1, W2, b2, Wr, br):
        import jax, jax.numpy as jnp
        import numpy as np
        from jax import lax
        D = 256
        H = 1024
        E = 8
        TOPK = 2
        B, S, _ = x.shape
        xf = x.reshape(-1, D)
        logits = xf @ Wr + br
        topv, _ = lax.top_k(logits, TOPK)
        thresh = topv[:, TOPK - 1:TOPK]
        masked = jnp.where(logits >= thresh, logits, -jnp.inf)
        weights = jax.nn.softmax(masked, axis=-1)
        h = jax.nn.gelu(jnp.einsum('td,edh->eth', xf, W1) + b1[:, None, :], approximate=False)
        expert_out = jnp.einsum('eth,ehd->etd', h, W2) + b2[:, None, :]
        out = jnp.einsum('etd,te->td', expert_out, weights)
        return out.reshape(B, S, D)

    def _L2_xattn_ref(Q, K, V, projection):
        import jax, jax.numpy as jnp
        import numpy as np
        import math
        B, L, D = (4, 1024, 256)
        M = 64
        EPS = 1e-06
        d_model = Q.shape[-1]
        m = projection.shape[0]
        inv_sqrt_d = 1.0 / math.sqrt(d_model)
        rf_q = jnp.exp(jnp.einsum('bld,md->blm', Q * inv_sqrt_d, projection)) / math.sqrt(m)
        rf_k = jnp.exp(jnp.einsum('bld,md->blm', K * inv_sqrt_d, projection))
        KV = jnp.einsum('blm,bld->bmd', rf_k, V)
        Z = jnp.sum(rf_k, axis=1)
        out = jnp.einsum('blm,bmd->bld', rf_q, KV)
        normalizer = jnp.einsum('blm,bm->bl', rf_q, Z) + EPS
        return out / normalizer[..., None]

    def _L2_attn_ref(x, Wqkv, bqkv, Wout, bout):
        import jax, jax.numpy as jnp
        import numpy as np
        import math
        DIM = 256
        N_HEADS = 16
        HEAD_DIM = DIM // N_HEADS
        B, S = (2, 512)
        b, s, d = x.shape
        qkv = jnp.einsum('bsd,hde->bhse', x, Wqkv) + bqkv[None, :, None, :]
        q, k, v = jnp.split(qkv, 3, axis=-1)
        score = jnp.einsum('bhsd,bhtd->bhst', q, k)
        causal = jnp.tril(jnp.ones((s, s), dtype=bool))
        score = jnp.where(causal[None, None], score, -jnp.inf)
        attn = jax.nn.softmax(score / jnp.sqrt(jnp.asarray(HEAD_DIM, x.dtype)), axis=-1)
        y = jnp.einsum('bhst,bhtd->bhsd', attn, v)
        y = jnp.transpose(y, (0, 2, 1, 3)).reshape(b, s, d)
        out = y @ Wout + bout
        return out

    def _L2_ffn_ref(input, weight, bias):
        import jax, jax.numpy as jnp
        import numpy as np
        FP8_MAX = 448.0

        def quant_fp8(x):
            amax = jnp.max(jnp.abs(x)).astype(jnp.float32)
            scale = jnp.minimum(FP8_MAX / jnp.maximum(amax, 1e-12), FP8_MAX)
            x_fp8 = jnp.clip(x * scale, -FP8_MAX, FP8_MAX).astype(jnp.float8_e4m3fn)
            return (x_fp8, 1.0 / scale)
        prev_shape = input.shape
        x2d = input.reshape(-1, weight.shape[1])
        w_fp8, w_scale = quant_fp8(weight)
        x_fp8, x_scale = quant_fp8(x2d)
        acc = jnp.matmul(x_fp8.astype(jnp.float32), w_fp8.astype(jnp.float32).T)
        out2d = (acc * (x_scale * w_scale) + bias).astype(jnp.bfloat16)
        out = out2d.reshape(*prev_shape[:-1], weight.shape[0]).astype(input.dtype)
        return out

    def _L3_xattn_ref(query, key, value, Wq, bq, Wk, bk, Wv, bv, Wo, bo, theta, gate):
        import jax, jax.numpy as jnp
        import numpy as np
        D_MODEL = 256
        N_HEADS = 16
        D_K = D_MODEL // N_HEADS
        B, Sq, D = query.shape
        Sk = key.shape[1]
        Q = (query @ Wq.T + bq).reshape(B, Sq, N_HEADS, D_K).transpose(0, 2, 1, 3)
        K = (key @ Wk.T + bk).reshape(B, Sk, N_HEADS, D_K).transpose(0, 2, 1, 3)
        V = (value @ Wv.T + bv).reshape(B, Sk, N_HEADS, D_K).transpose(0, 2, 1, 3)
        inv_sqrt_dk = 1.0 / jnp.sqrt(jnp.float32(D_K))
        scores = jnp.einsum('bhqd,bhkd->bhqk', Q, K) * inv_sqrt_dk
        cos_t = jnp.cos(theta)[None, :, None, None]
        sin_t = jnp.sin(theta)[None, :, None, None]
        q_rot = jnp.concatenate([cos_t * Q[..., :1] - sin_t * Q[..., 1:2], sin_t * Q[..., :1] + cos_t * Q[..., 1:2], Q[..., 2:]], axis=-1)
        scores_q = jnp.einsum('bhqd,bhkd->bhqk', q_rot, K) * inv_sqrt_dk
        g_scalar = jax.nn.sigmoid(gate.mean())
        scores = g_scalar * scores_q + (1.0 - g_scalar) * scores
        attn = jax.nn.softmax(scores, axis=-1)
        out = jnp.einsum('bhqk,bhkd->bhqd', attn, V)
        out = out.transpose(0, 2, 1, 3).reshape(B, Sq, D)
        return out @ Wo.T + bo

    def _L3_attn_ref(x, Wq, bq, Wk, bk, Wv, bv, Wo, bo):
        import jax, jax.numpy as jnp
        import numpy as np
        D_IN = 256
        D_ATT = 256
        D_OUT = 256
        N, S = (8, 1024)
        query = jnp.einsum('nsd,dh->nsh', x, Wq) + bq
        keyp = jnp.einsum('nsd,dh->nsh', x, Wk) + bk
        value = jnp.einsum('nsd,dh->nsh', x, Wv) + bv
        fmap = lambda t: jax.nn.elu(t) + 1.0
        Q = fmap(query)
        K = fmap(keyp)
        KV = jnp.sum(K * value, axis=1)
        Ksum = jnp.sum(K, axis=1)
        Z = 1.0 / (Q * Ksum[:, None, :] + 1e-06)
        V = Q * KV[:, None, :] * Z
        out = jnp.einsum('nsh,ho->nso', V, Wo) + bo
        return jax.nn.gelu(out)

    def _L3_ffn_ref(x, Wg, bg, Wi, Wo, A, B):
        import jax, jax.numpy as jnp
        import numpy as np
        TOP_K = 2
        E = Wg.shape[0]
        logits = jnp.einsum('bsd,ed->bse', x, Wg) + bg
        scores = jax.nn.softmax(logits, axis=-1)
        topv, topi = jax.lax.top_k(scores, TOP_K)
        w = jnp.sum(jax.nn.one_hot(topi, E, dtype=x.dtype) * topv[..., None], axis=-2)
        base = jnp.einsum('bsd,fd->bsf', x, Wi)
        lora_low = jnp.einsum('bsd,erd->bser', x, A)
        lora = jnp.einsum('bser,efr->bsef', lora_low, B)
        h = jax.nn.relu(base[:, :, None, :] + lora)
        expert_out = jnp.einsum('bsef,df->bsed', h, Wo)
        out = jnp.einsum('bse,bsed->bsd', w, expert_out)
        return out
    x = x + _L0_xattn_ref(_layernorm(x, axis=-1), ctx_1024, L0_xattn_Wq, L0_xattn_bq, L0_xattn_Wk, L0_xattn_bk, L0_xattn_Wv, L0_xattn_bv, L0_xattn_Wo, L0_xattn_bo)
    x = x + _L0_attn_ref(_layernorm(x, axis=-1), L0_attn_W_q, L0_attn_W_dkv, L0_attn_W_uk, L0_attn_W_uv, L0_attn_W_o, L0_attn_ln_gamma, L0_attn_ln_beta)
    x = x + _L0_ffn_ref(_layernorm(x, axis=-1), L0_ffn_w_gate, L0_ffn_w_up, L0_ffn_w_down)
    x = x + _L1_xattn_ref(_layernorm(x, axis=-1), ctx_1024, ctx_1024, mask_BxS2_bf1, L1_xattn_Wq, L1_xattn_bq, L1_xattn_Wk, L1_xattn_bk, L1_xattn_Wv, L1_xattn_bv, L1_xattn_Wo, L1_xattn_bo)
    x = x + _L1_attn_ref(_layernorm(x, axis=-1), L1_attn_w_qkv, L1_attn_w_out, L1_attn_b_out, L1_attn_ln_gamma, L1_attn_ln_beta)
    x = x + _L1_ffn_ref(_layernorm(x, axis=-1), L1_ffn_W1, L1_ffn_b1, L1_ffn_W2, L1_ffn_b2, L1_ffn_Wr, L1_ffn_br)
    x = x + _L2_xattn_ref(_layernorm(x, axis=-1), ctx_1024, ctx_1024, L2_xattn_projection)
    x = x + _L2_attn_ref(_layernorm(x, axis=-1), L2_attn_Wqkv, L2_attn_bqkv, L2_attn_Wout, L2_attn_bout)
    x = x + _L2_ffn_ref(_layernorm(x, axis=-1), L2_ffn_weight, L2_ffn_bias)
    x = x + _L3_xattn_ref(_layernorm(x, axis=-1), ctx_1024, ctx_1024, L3_xattn_Wq, L3_xattn_bq, L3_xattn_Wk, L3_xattn_bk, L3_xattn_Wv, L3_xattn_bv, L3_xattn_Wo, L3_xattn_bo, L3_xattn_theta, L3_xattn_gate)
    x = x + _L3_attn_ref(_layernorm(x, axis=-1), L3_attn_Wq, L3_attn_bq, L3_attn_Wk, L3_attn_bk, L3_attn_Wv, L3_attn_bv, L3_attn_Wo, L3_attn_bo)
    x = x + _L3_ffn_ref(_layernorm(x, axis=-1), L3_ffn_Wg, L3_ffn_bg, L3_ffn_Wi, L3_ffn_Wo, L3_ffn_A, L3_ffn_B)
    return x

_drawn_inputs = setup_inputs


def setup_inputs(seed=0):
    import zlib

    import numpy as np

    out = dict(_drawn_inputs(seed))
    spreads = {'L0_xattn_bq': (0.0, 0.8),
     'L0_xattn_bk': (0.0, 2.0),
     'L0_xattn_bv': (0.0, 0.1),
     'L0_xattn_bo': (0.0, 0.1),
     'L0_attn_ln_gamma': (1.0, 0.6),
     'L0_attn_ln_beta': (0.0, 0.1),
     'L1_xattn_bq': (0.0, 0.336),
     'L1_xattn_bk': (0.0, 2.0),
     'L1_xattn_bv': (0.0, 0.1),
     'L1_xattn_bo': (0.0, 0.1),
     'L1_attn_b_out': (0.0, 0.1),
     'L1_attn_ln_gamma': (1.0, 0.2),
     'L1_attn_ln_beta': (0.0, 0.1),
     'L1_ffn_b1': (0.0, 0.466),
     'L1_ffn_b2': (0.0, 0.1),
     'L1_ffn_br': (0.0, 0.36),
     'L3_xattn_bq': (0.0, 0.713),
     'L3_xattn_bk': (0.0, 2.0),
     'L3_xattn_bv': (0.0, 0.1),
     'L3_xattn_bo': (0.0, 0.1),
     'L3_attn_bq': (0.0, 2.0),
     'L3_attn_bk': (0.0, 2.0),
     'L3_attn_bv': (0.0, 0.278),
     'L3_attn_bo': (0.0, 0.289),
     'L3_ffn_bg': (0.0, 0.8)}
    factors = {'L0_xattn_Wq': 8.0,
     'L0_xattn_Wk': 8.0,
     'L0_attn_W_q': 3.335,
     'L0_attn_W_uk': 3.344,
     'L2_attn_bqkv': 4.149,
     'L2_ffn_bias': 2.847,
     'L3_xattn_theta': 34.879,
     'L3_attn_Wq': 8.0,
     'L3_attn_Wk': 5.224,
     'L3_ffn_A': 8.0,
     'L3_ffn_B': 8.0}
    for name, (base, spread) in spreads.items():
        noise = np.random.default_rng([zlib.crc32(name.encode()), seed]).standard_normal(out[name].shape)
        drawn = base * np.exp(spread * noise) if base else spread * noise
        out[name] = jnp.asarray(drawn.astype(out[name].dtype))
    for name, factor in factors.items():
        out[name] = (out[name] * factor).astype(out[name].dtype)
    return out
```

```python
from contextlib import ExitStack

import numpy as np

import concourse.bass as bass
from concourse import mybir

ALU = mybir.AluOpType
ACT = mybir.ActivationFunctionType
F32 = mybir.dt.float32
F32R = mybir.dt.float32r
BF16 = mybir.dt.bfloat16
U8 = mybir.dt.uint8
U32 = mybir.dt.uint32
AX_X = mybir.AxisListType.X
ABSMAX = bass.bass_isa.ReduceOp.absmax

P = 128
S = 128
D = 256
DC = D // P
T = 12544
H = 16
DH = D // H
HPB = P // DH
NT = T // P
BANK = 512
LARGEST = 3.0e38
NEG = -1.0e30
ROUND = 12582912.0

XATTN_PACK = [("Wq", DC * D), ("Wk", DC * D), ("Wv", DC * D), ("Wo", DC * D), ("bq", DC), ("bk", DC),
              ("bv", D), ("bo", D)]
PACKS = {
    "L0_xattn": XATTN_PACK,
    "L0_attn": [("W_q", DC * D), ("W_q_swapped", DC * D), ("W_dkv", DC * 64), ("W_uk", D), ("W_uk_swapped", D),
                ("W_uv", D), ("W_o", DC * D), ("ln_gamma", 64), ("ln_beta", 64)],
    "L0_ffn": [("w_gate", 6 * D), ("w_up", 6 * D), ("w_down", 2 * 768)],
    "L1_xattn": XATTN_PACK,
    "L1_attn": [("w_qkv", DC * 3072), ("w_out", 8 * D), ("b_out", D), ("ln_gamma", D), ("ln_beta", D)],
    "L1_ffn": [("Wr", DC * 8), ("br", 8), ("b1", 64), ("b2", D)],
    "L2_xattn": [("projection", DC * 64)],
    "L2_attn": [("Wqk", DC * 2 * D), ("Wv", DC * D), ("Wout", DC * D), ("bqk", 4), ("bv", D), ("bout", D)],
    "L2_ffn": [("weight", DC * D), ("bias", D)],
    "L3_xattn": XATTN_PACK + [("Wq_swapped", DC * D), ("bq_swapped", DC), ("theta", DC), ("gate", D)],
    "L3_attn": [("Wq", DC * D), ("Wk", DC * D), ("Wv", DC * D), ("Wo", DC * D), ("bqkv", 3 * DC), ("bo", D)],
    "L3_ffn": [("Wg", DC * 4), ("bg", 4), ("Wi", DC * 1024), ("Wo", 8 * D), ("A", DC * P), ("B", 1024)],
}
LAYERS = list(PACKS)
CONSTS = [("identity", P), ("ones", P), ("causal", P), ("causal_T", P), ("rope_cos", S), ("rope_sin", S),
          ("head16", 8), ("head32", 4), ("neg_half", 1), ("fill", P), ("turned", 1), ("turn_sign", 1)]


def columns(pack):
    at, out = 0, {}
    for name, n in pack:
        out[name] = (at, at + n)
        at += n
    return out, at


def constants():
    p = np.arange(P)
    half = DH // 2
    inv_freq = (np.float32(1.0) / np.float32(10000.0) ** (np.arange(half, dtype=np.float32) / np.float32(half)))
    angle = np.arange(S, dtype=np.float32)[None, :] * inv_freq.astype(np.float32)[(p % DH) % half][:, None]
    sign = np.where(p % DH < half, -1.0, 1.0)[:, None]
    fill = np.zeros((P, P), np.float32)
    rest = -1e8
    for row in range(3):
        part = float((np.array([rest], np.float32).view(np.uint32) & np.uint32(0xFFFF0000)).view(np.float32)[0])
        fill[row] = part
        rest -= part
    assert rest == 0.0
    made = {
        "identity": np.eye(P), "ones": np.ones((P, P)), "fill": fill,
        "causal": np.where(p[None, :] > p[:, None], NEG, 0.0), "causal_T": np.where(p[:, None] > p[None, :], NEG, 0.0),
        "rope_cos": np.cos(angle), "rope_sin": np.sin(angle) * sign,
        "head16": p[:, None] // 16 == np.arange(8)[None, :], "head32": p[:, None] // 32 == np.arange(4)[None, :],
        "neg_half": np.full((P, 1), -0.5),
        "turned": (p % DH < 2)[:, None], "turn_sign": np.where(p % DH == 0, -1.0, np.where(p % DH == 1, 1.0, 0.0))[:, None],
    }
    return np.concatenate([np.asarray(made[n], np.float32) for n, _ in CONSTS], axis=1)


class Order:

    def __init__(self, eng, sem):
        self.eng, self.sem, self.n = eng, sem, 0

    def after(self, ins):
        self.n += 1
        ins.then_inc(self.sem, 1)
        self.eng.wait_ge(self.sem, self.n)


class Layer:

    def __init__(self, net, name):
        self.net, self.nc, self.name = net, net.nc, name
        self.sems = {}
        self.ctx = ExitStack()

    def __getitem__(self, name):
        if name not in self.sems:
            self.sems[name] = self.nc.alloc_semaphore(f"{self.name}_{name}")
        return self.sems[name]

    def sb(self, name, shape, dt=F32):
        return self.ctx.enter_context(self.nc.sbuf_tensor(f"{self.name}_{name}", shape, dt))

    def order(self, eng, name):
        return Order(eng, self[name])

    def __enter__(self):
        self.ps = self.ctx.enter_context(self.nc.psum_tensor(f"{self.name}_ps", [P, 8, BANK], F32))
        return self

    def __exit__(self, *exc):
        self.ctx.close()
        if exc[0] is None:
            self.nc.clear_and_free_semaphores(list(self.sems.values()))
            self.nc.all_engine_barrier()


class Net:

    def __init__(self, nc, ctx, ins):
        self.nc, self.ins = nc, ins
        self.const_at, n = columns(CONSTS)
        self.const_sb = ctx.enter_context(nc.sbuf_tensor("consts", [P, n], F32))
        self.ident_bf = ctx.enter_context(nc.sbuf_tensor("ident_bf", [P, P], BF16))
        self.causal_bf = ctx.enter_context(nc.sbuf_tensor("causal_bf", [P, 4, P], BF16))
        self.causal_T_bf = ctx.enter_context(nc.sbuf_tensor("causal_T_bf", [P, 4, P], BF16))
        self.fill_bf = ctx.enter_context(nc.sbuf_tensor("fill_bf", [P, P], BF16))
        self.zeros_bf = ctx.enter_context(nc.sbuf_tensor("zeros_bf", [P, BANK], BF16))
        self.x = ctx.enter_context(nc.sbuf_tensor("x_rows", [S, D], F32))
        sizes = [columns(PACKS[n])[1] for n in LAYERS]
        self.arena = [ctx.enter_context(nc.sbuf_tensor(f"weights_{k}", [P, max(sizes[k::2])], F32)) for k in range(2)]
        self.loaded = [nc.alloc_semaphore(f"{n}_weights_loaded") for n in LAYERS]
        self.first_loaded = nc.alloc_semaphore("x_and_consts_loaded")

    def const(self, name):
        a, b = self.const_at[name]
        return self.const_sb[:, a:b]

    def w(self, layer, name, **split):
        k = LAYERS.index(layer)
        a, b = columns(PACKS[layer])[0][name]
        v = self.arena[k % 2][:, a:b]
        return v.rearrange("p (c n) -> p c n", **split) if split else v

    def load_weights(self, eng, k):
        if k < len(LAYERS):
            n = columns(PACKS[LAYERS[k]])[1]
            eng.dma_start(self.arena[k % 2][:, 0:n], self.ins[f"pack_{LAYERS[k]}"]).then_inc(self.loaded[k], 16)

    def wait_weights(self, eng, layer):
        eng.wait_ge(self.loaded[LAYERS.index(layer)], 16)




class NormRows:

    def __init__(self, L, bank=7):
        self.L, self.net, self.bank = L, L.net, bank
        self.stats = L.sb("stats", [S, 6])
        self.mv = L.sb("mean_var", [S, 2])
        self.rstd = L.sb("rstd", [S, 2])
        self.xn = L.sb("xn", [S, D])
        self.xnT = L.sb("xnT", [P, DC, S])

    def vector(self, dve):
        L, x = self.L, self.net.x
        o = L.order(dve, "norm_dve")
        o.after(dve.bn_stats(self.stats[:, :], x[:, :]))
        dve.bn_aggr(self.mv[:, :], self.stats[:, :]).then_inc(L["var_ready"], 1)
        dve.wait_ge(L["rstd_ready"], 2)
        dve.tensor_scalar(self.xn[:, :], x[:, :], self.mv[:, 0:1], self.rstd[:, 1:2], ALU.subtract,
                          ALU.mult).then_inc(L["xn_ready"], 1)

    def gpsimd(self, pool):
        L = self.L
        pool.wait_ge(L["var_ready"], 1)
        pool.tensor_scalar(self.rstd[:, 0:1], self.mv[:, 1:2], 1e-5, None, ALU.add).then_inc(L["rstd_ready"], 1)
        pool.wait_ge(L["rstd_ready"], 1)
        pool.tensor_tensor(self.rstd[:, 1:2], self.rstd[:, 0:1], self.net.const("neg_half"),
                           ALU.pow).then_inc(L["rstd_ready"], 1)

    def tensor(self, pe):
        L = self.L
        pe.wait_ge(L["xn_ready"], 1)
        for c in range(DC):
            last = pe.transpose(L.ps[:, self.bank, c * P:(c + 1) * P], self.xn[:, c * P:(c + 1) * P],
                                self.net.const("identity"))
        last.then_inc(L["xnT_in_psum"], 1)

    def scalar(self, act):
        L = self.L
        act.wait_ge(L["xnT_in_psum"], 1)
        act.activation(self.xnT[:, :, :], L.ps[:, self.bank, 0:DC * P].rearrange("p (c n) -> p c n", c=DC),
                       ACT.Copy).then_inc(L["xnT_ready"], 1)


class Transposed:

    def __init__(self, L, tag, src, C, dst, bank):
        self.L, self.tag, self.src, self.C, self.dst, self.bank = L, tag, src, C, dst, bank

    def tensor(self, pe, ready, n=1):
        L, C = self.L, self.C
        pe.wait_ge(ready, n)
        for c in range(C):
            last = pe.transpose(L.ps[:, self.bank + c // 4, c % 4 * P:(c % 4 + 1) * P],
                                self.src[:, c * P:(c + 1) * P], L.net.const("identity"))
        last.then_inc(L[f"{self.tag}_in_psum"], 1)

    def scalar(self, act):
        L, C = self.L, self.C
        act.wait_ge(L[f"{self.tag}_in_psum"], 1)
        for b in range(0, C, 4):
            k = min(4, C - b)
            last = act.activation(self.dst[:, b:b + k, :],
                                  L.ps[:, self.bank + b // 4, 0:k * P].rearrange("p (c n) -> p c n", c=k), ACT.Copy)
            last.then_inc(L[f"{self.tag}_ready"], 1)

    def wait(self, eng):
        eng.wait_ge(self.L[f"{self.tag}_ready"], -(-self.C // 4))


def project(pe, out, xT, W, cols, start=True, stop=True):
    C = W.shape[1]
    for c in range(C):
        last = pe.matmul(out, xT[:, c, :], W[:, c, cols], start=start and c == 0, stop=stop and c == C - 1)
    return last


def project_T(pe, out, xT, W, cols):
    C = W.shape[1]
    for c in range(C):
        last = pe.matmul(out, W[:, c, cols], xT[:, c, :], start=c == 0, stop=c == C - 1, skip_group_check=True)
    return last


def wide(ap, n):
    return ap.unsqueeze(2).broadcast_to([ap.shape[0], ap.shape[1], n])


def times(ap, m):
    return ap.unsqueeze(1).broadcast_to([ap.shape[0], m, ap.shape[1]])


class SelfAttention:

    def __init__(self, L, dh, scale, causal, sets, kT, v, out):
        self.L, self.dh, self.scale, self.causal, self.sets = L, dh, scale, causal, sets
        self.kT, self.v, self.out = kT, v, out
        self.q_heads = L.sb("q_heads", [P, H, S])
        self.p = L.sb("p", [S, H, S])
        self.pT = L.sb("pT", [S, H, S])
        self.mx = L.sb("score_max", [S, H])
        self.den = L.sb("den", [S, 2, H])

    def scores_psum(self):
        return self.L.ps[:, 0:4, :].rearrange("p b (h n) -> p (b h) n", h=4)

    def spread_vector(self, dve, s, qT):
        L, per = self.L, P // self.dh
        if s == 0:
            self.order = L.order(dve, "attention_dve")
        if s:
            dve.wait_ge(L["scores_ready"], s)
        mask = L.net.const("head16" if self.dh == 16 else "head32")
        for b in range(H // per):
            dve.tensor_tensor(self.q_heads[:, b * per:(b + 1) * per, :], times(qT[:, s * (H // per) + b, :], per),
                              wide(mask, S), ALU.mult).then_inc(L["q_heads_ready"], 1)

    def tensor_scores(self, pe, s):
        L, per = self.L, P // self.dh
        pe.wait_ge(L["q_heads_ready"], (s + 1) * (H // per))
        if s:
            pe.wait_ge(L["attended"], s)
        for g in range(4):
            if self.causal:
                pe.matmul(L.ps[:, g, :], L.net.ident_bf[:, :], L.net.causal_bf[:, :, :].rearrange("p a b -> p (a b)"),
                          start=True, stop=False, skip_group_check=True)
            for h in range(4 * g, 4 * g + 4):
                last = pe.matmul(L.ps[:, g, h % 4 * S:(h % 4 + 1) * S], self.q_heads[:, h, :],
                                 self.kT[:, s * (H // per) + h // per, :], start=h % 4 == 0 and not self.causal,
                                 stop=h % 4 == 3, skip_group_check=True)
        last.then_inc(L["scores_ready"], 1)

    def tensor_output(self, pe, s):
        L, dh = self.L, self.dh
        pe.wait_ge(L["p_ready"], s + 1)
        for h in range(H):
            last = pe.transpose(L.ps[:, 4 + h // 4, h % 4 * S:(h % 4 + 1) * S], self.p[:, h, :],
                                L.net.const("identity"))
        last.then_inc(L["pT_in_psum"], 1)
        pe.wait_ge(L["pT_ready"], 2 * (s + 1))
        for h in range(H):
            at = (s * H + h) * dh
            last = pe.matmul(L.ps[:, 0, h * dh:(h + 1) * dh], self.pT[:, h, :], self.v[:, at:at + dh],
                             start=h == 0, stop=h == H - 1, skip_group_check=True)
        last.then_inc(L["out_in_psum"], 1)

    def scalar(self, act, s):
        L = self.L
        act.wait_ge(L["centred"], s + 1)
        act.activation(self.p[:, :, :], self.p[:, :, :], ACT.Exp, scale=self.scale).then_inc(L["p_ready"], 1)
        act.wait_ge(L["pT_in_psum"], s + 1)
        act.activation(self.pT[:, 0:8, :], L.ps[:, 4:6, :].rearrange("p b (h n) -> p (b h) n", h=4),
                       ACT.Copy).then_inc(L["pT_ready"], 1)

    def vector(self, dve, s):
        L, dh = self.L, self.dh
        o = self.order
        dve.wait_ge(L["scores_ready"], s + 1)
        o.after(dve.tensor_reduce(self.mx[:, :], self.scores_psum(), AX_X, ALU.max))
        dve.tensor_tensor(self.p[:, :, :], self.scores_psum(), wide(self.mx[:, :], S),
                          ALU.subtract).then_inc(L["centred"], 1)
        dve.wait_ge(L["p_ready"], s + 1)
        o.after(dve.tensor_reduce(self.den[:, 0, :], self.p[:, :, :], AX_X, ALU.add))
        o.after(dve.reciprocal(self.den[:, 1, :], self.den[:, 0, :]))
        dve.wait_ge(L["pT_in_psum"], s + 1)
        dve.tensor_copy(self.pT[:, 8:16, :], L.ps[:, 6:8, :].rearrange("p b (h n) -> p (b h) n", h=4))\
           .then_inc(L["pT_ready"], 1)
        dve.wait_ge(L["out_in_psum"], s + 1)
        dve.tensor_tensor(self.out[:, s * H * dh:(s + 1) * H * dh].rearrange("p (h n) -> p h n", h=H),
                          L.ps[:, 0, 0:H * dh].rearrange("p (h n) -> p h n", h=H), wide(self.den[:, 1, :], dh),
                          ALU.mult).then_inc(L["attended"], 1)




CHUNK = 448
NCHUNK = T // CHUNK
BODY = 14
SLOTS = 7
assert NCHUNK * CHUNK == T and NT % BODY == 0 and BODY % SLOTS == 0 and NCHUNK % 2 == 0


def turns(eng, count, body):
    with eng.Fori(0, count - 1) as i:
        body(i, False)
    body(count - 1, True)


class CrossAttention:

    def __init__(self, L, causal=False, masked=False, turned=False):
        self.L, self.net, self.nc = L, L.net, L.nc
        self.causal, self.masked, self.turned = causal, masked, turned
        self.norm = NormRows(L)
        sb = L.sb
        self.qT = sb("qT", [P, DC, S])
        self.q_hi = sb("q_hi", [P, H, S], F32R)
        self.q_lo = sb("q_lo", [P, H, S], F32R)
        self.ctx_chunk = [sb(f"ctx_chunk{c}", [P, DC, CHUNK]) for c in range(2)]
        self.k_chunk = [sb(f"k_chunk{c}", [P, DC, CHUNK]) for c in range(2)]
        self.kr_chunk = [sb(f"kr_chunk{c}", [P, DC, CHUNK], F32R) for c in range(2)]
        self.chunk_max = [sb(f"chunk_max{c}", [S, H]) for c in range(2)]
        self.row_max = sb("row_max", [S, H])
        self.max_bc = sb("max_bc", [P, H, S])
        self.ctx_tile = sb("ctx_tile", [P, SLOTS, DC, P])
        self.k_tile = sb("k_tile", [P, SLOTS, DC, P])
        self.k_halves = [sb(f"k_halves{c}", [P, 2, DC, P], F32R) for c in range(2)]
        self.v = [sb(f"v{c}", [P, H, DH + 1]) for c in range(2)]
        self.p = [sb(f"p{c}", [P, H, S]) for c in range(2)]
        self.sums = sb("sums", [P, 4, S])
        self.rden = sb("rden", [S, 4, 4])
        self.o = sb("o", [S, D])
        self.oT = sb("oT", [P, DC, S])
        self.attended = Transposed(L, "oT", self.o, DC, self.oT, 1)
        if masked:
            self.mask_chunk = [sb(f"mask_chunk{c}", [P, CHUNK], U8) for c in range(2)]
            self.mask_wide = [sb(f"mask_wide{c}", [P, CHUNK]) for c in range(2)]
            self.unmask = [sb(f"unmask{c}", [P, CHUNK], BF16) for c in range(2)]
            self.mask_cols = sb("mask_cols", [P, NT], U8)
            self.fill_cols = sb("fill_cols", [P, NT])
            self.fill = [sb(f"fill{c}", [P, 1]) for c in range(2)]
        if turned:
            self.turn = sb("turn", [P, 24])
            self.qT_swapped = sb("qT_swapped", [P, DC, S])
            self.gate_sum = sb("gate_sum", [P, D])
        self.kT = self.nc.dram_tensor(f"{L.name}_kT", [D, T], F32, kind="Internal").ap()\
            .rearrange("(c p) t -> p c t", p=P)

    def w(self, name, **split):
        return self.net.w(self.L.name, name, **split)


    def sync(self, sp):
        L, ins = self.L, self.net.ins
        ctxT = ins["ctxT"].rearrange("(c p) t -> p c t", p=P)
        if self.masked:
            sp.dma_start(self.mask_cols[:, :], ins["mask_cols"]).then_inc(L["mask_cols_loaded"], 16)

        def chunk_loads(i, last):
            for c in range(2):
                at = (2 * i + c) * CHUNK
                sp.wait_ge(L["k_in_psum"], 2 * (2 * i + c) + 2)
                sp.dma_start(self.ctx_chunk[c][:, :, :], ctxT[:, :, bass.ds(at, CHUNK)])\
                  .then_inc(L[f"ctx_chunk_loaded{c}"], 16)
                if self.masked:
                    sp.wait_ge(L["kr_ready"], 2 * i + c + 1)
                    sp.dma_start(self.mask_chunk[c][:, :], ins["mask_row"][:, bass.ds(at, CHUNK)]
                                 .broadcast_to([P, CHUNK])).then_inc(L[f"mask_chunk_loaded{c}"], 16)
        turns(sp, NCHUNK // 2, chunk_loads)
        self.net.load_weights(sp, LAYERS.index(L.name) + 1)
        for c in range(2):
            sp.wait_ge(L[f"k_stored{c}"], 16 * (NCHUNK // 2 + 1))

        def tile_loads(i, last):
            for j in range(BODY):
                t, slot = BODY * i + j, j % SLOTS
                sp.wait_ge(L["v_in_psum"], t + 1)
                sp.dma_start(self.ctx_tile[:, slot, :, :], ctxT[:, :, bass.ds(t * P, P)])\
                  .then_inc(L[f"tile_loaded{slot}"], 16)
                sp.wait_ge(L["k_halves_ready"], t + 1)
                sp.dma_start(self.k_tile[:, slot, :, :], self.kT[:, :, bass.ds(t * P, P)])\
                  .then_inc(L[f"tile_loaded{slot}"], 16)
        turns(sp, NT // BODY, tile_loads)


    def pe_queries(self, pe):
        L, xnT = self.L, self.norm.xnT
        pe.wait_ge(L["xnT_ready"], 1)
        for c in range(DC):
            last = project_T(pe, L.ps[:, 0, c * S:(c + 1) * S], xnT, self.w("Wq", c=DC), slice(c * P, (c + 1) * P))
        if self.turned:
            for c in range(DC):
                last = project_T(pe, L.ps[:, 1, c * S:(c + 1) * S], xnT, self.w("Wq_swapped", c=DC),
                                 slice(c * P, (c + 1) * P))
        last.then_inc(L["q_in_psum"], 1)

    def pe_keys(self, pe, n, c, i):
        L = self.L
        pe.wait_ge(L[f"ctx_chunk_loaded{c}"], 16 * (i + 1))
        for d in range(DC):
            pe.wait_ge(L["k_chunk_ready"], 2 * n + d + 1)
            for e in range(DC):
                last = pe.matmul(L.ps[:, 6 + d, 0:CHUNK], self.w("Wk", c=DC)[:, e, d * P:(d + 1) * P],
                                 self.ctx_chunk[c][:, e, :], start=e == 0, stop=e == DC - 1)
            last.then_inc(L["k_in_psum"], 1)

    def pe_chunk_scores(self, pe, n, c, last_chunk):
        L = self.L
        pe.wait_ge(L["kr_ready"], n + 3)
        if self.masked:
            pe.wait_ge(L["unmask_ready"], n + 1)
        for pair in range(8):
            before = pair - 3 if pair >= 3 else {0: 6, 1: 7, 2: 5}[pair] - 8
            pe.wait_ge(L["pair_max_ready"], 8 * n + before + 4)
            for h in (2 * pair, 2 * pair + 1):
                bank = pair % 3 * 2 + h % 2
                last = pe.matmul(L.ps[:, bank, 0:CHUNK], self.q_hi[:, h, :], self.kr_chunk[c][:, h // HPB, :],
                                 start=True, stop=not (self.masked or last_chunk), skip_group_check=True)
                if self.masked:
                    last = pe.matmul(L.ps[:, bank, 0:CHUNK], self.net.fill_bf[0:3, :], self.unmask[c][0:3, :],
                                     start=False, stop=not last_chunk, skip_group_check=True)
                if last_chunk:
                    last = pe.matmul(L.ps[:, bank, CHUNK - P:CHUNK], self.net.ident_bf[:, :],
                                     self.net.causal_bf[:, 0, :], start=False, stop=True, skip_group_check=True)
            last.then_inc(L["pair_scored"], 1)

    def pe_broadcast_max(self, pe):
        L = self.L
        pe.wait_ge(L["max_diagonals"], 1)
        for b in range(4):
            last = pe.matmul(L.ps[:, b, :], self.net.const("ones"),
                             self.p[0][:, 4 * b:4 * b + 4, :].rearrange("p h n -> p (h n)"), start=True, stop=True)
        last.then_inc(L["max_in_psum"], 1)
        pe.matmul(L.ps[:, 6, :], self.net.zeros_bf[:, 0:P], self.net.zeros_bf[:, :], start=True, stop=True,
                  skip_group_check=True)


    def pe_tile_scores(self, pe, t, par, masked_tile):
        L, k = self.L, self.k_halves[par]
        pe.wait_ge(L["k_halves_ready"], t + 1 + SLOTS)
        for pair in range(2):
            pe.wait_ge(L["centred"], 2 * t + pair + 1)
            banks = (2 * pair, 2 * pair + 1)
            if masked_tile:
                for b in banks:
                    pe.matmul(L.ps[:, b, :], self.net.ident_bf[:, :],
                              self.net.causal_T_bf[:, :, :].rearrange("p a b -> p (a b)"), start=True, stop=False,
                              skip_group_check=True)
            for n, (half, q) in enumerate(((0, self.q_hi), (0, self.q_lo), (1, self.q_hi))):
                for b in banks:
                    last = pe.matmul(L.ps[:, b, :], k[:, half, pair, :],
                                     q[:, 4 * b:4 * b + 4, :].rearrange("p h n -> p (h n)"),
                                     start=n == 0 and not masked_tile, stop=n == 2, skip_group_check=True)
            last.then_inc(L["pair_in_psum"], 1)

    def pe_values(self, pe, t, slot, ring, par):
        L = self.L
        pe.wait_ge(L[f"tile_loaded{slot}"], 32 * (ring + 1))
        pe.wait_ge(L["v_ready"], t + 1)
        for c in range(DC):
            last = pe.matmul(L.ps[:, 4 + par, 0:D], self.ctx_tile[:, slot, c, :], self.w("Wv", c=DC)[:, c, :],
                             start=c == 0, stop=c == DC - 1)
        last.then_inc(L["v_in_psum"], 1)

    def pe_attend(self, pe, t, par):
        L = self.L
        pe.wait_ge(L["v_ready"], t + 3)
        pe.wait_ge(L["p_ready"], t + 1)
        for h in range(H):
            q, i = h % 4 * 32, h // 4 * S
            last = pe.matmul(L.ps[q:q + DH + 1, 6, i:i + S], self.v[par][:, h, :], self.p[par][:, h, :],
                             start=False, stop=True, skip_group_check=True)
        last.then_inc(L["tile_attended"], 1)

    def tensor(self, pe):
        L = self.L
        self.norm.tensor(pe)
        self.net.wait_weights(pe, L.name)
        pe.sem_inc(L["k_in_psum"], 4)
        pe.sem_inc(L["v_in_psum"], SLOTS)
        pe.sem_inc(L["pair_in_psum"], 4)
        pe.sem_inc(L["tile_attended"], 2)
        pe.sem_inc(L["pair_scored"], 16)
        self.pe_queries(pe)
        self.pe_keys(pe, 0, 0, 0)
        pe.wait_ge(L["q_heads_ready"], 1)

        def chunk_turn(i, last):
            for c in range(2):
                n = 2 * i + c
                if not (last and c == 1):
                    self.pe_keys(pe, n + 1, 1 - c, i + c)
                self.pe_chunk_scores(pe, n, c, last and c == 1 and self.causal)
        turns(pe, NCHUNK // 2, chunk_turn)
        self.pe_broadcast_max(pe)
        pe.wait_ge(L["max_bc_ready"], 2)
        self.pe_tile_scores(pe, 0, 0, False)
        self.pe_values(pe, 0, 0, 0, 0)

        def tile_turn(i, last):
            for j in range(BODY):
                t, nxt = BODY * i + j, j + 1
                if not (last and nxt == BODY):
                    self.pe_tile_scores(pe, t + 1, nxt % 2, self.causal and last and nxt == BODY - 1)
                    self.pe_values(pe, t + 1, nxt % SLOTS, BODY // SLOTS * i + nxt // SLOTS, nxt % 2)
                self.pe_attend(pe, t, j % 2)
        turns(pe, NT // BODY, tile_turn)
        pe.wait_ge(L["sums_ready"], 1)
        for i in range(4):
            last = pe.transpose(L.ps[:, 0, i * S:(i + 1) * S], self.sums[:, i, :], self.net.const("identity"))
        last.then_inc(L["sums_in_psum"], 1)
        self.attended.tensor(pe, L["o_ready"])
        self.attended.wait(pe)
        project(pe, L.ps[:, 2, 0:D], self.oT, self.w("Wo", c=DC), slice(0, D)).then_inc(L["y_in_psum"], 1)

    def scalar(self, act):
        L = self.L
        for c in range(2):
            act.sem_inc(L[f"k_stored{c}"], 16)
        act.sem_inc(L["k_chunk_ready"], 2)
        self.norm.scalar(act)
        self.net.wait_weights(act, L.name)
        if self.turned:
            act.wait_ge(L["turn_angles"], 1)
            act.activation(self.turn[:, 4:8], self.turn[:, 0:4], ACT.Sin).then_inc(L["sines_ready"], 1)
            act.wait_ge(L["gate_mean_ready"], 1)
            act.activation(self.turn[:, 9:10], self.turn[:, 8:9], ACT.Exp, scale=-1.0 / D)\
               .then_inc(L["gate_exp_ready"], 1)

        def chunk_turn(i, last):
            for c in range(2):
                n = 2 * i + c
                act.wait_ge(L["kr_ready"], n + 1)
                if self.masked:
                    act.wait_ge(L[f"mask_chunk_loaded{c}"], 16 * (i + 1))
                    act.activation(self.mask_wide[c][:, :], self.mask_chunk[c][:, :], ACT.Copy)\
                       .then_inc(L["mask_wide_ready"], 1)
                act.wait_ge(L[f"k_stored{c}"], 16 * (i + 1))
                for d in range(DC):
                    act.wait_ge(L["k_in_psum"], 4 + 2 * n + d + 1)
                    act.activation(self.k_chunk[c][:, d, :], L.ps[:, 6 + d, 0:CHUNK], ACT.Identity,
                                   bias=self.w("bk")[:, d:d + 1]).then_inc(L["k_chunk_ready"], 1)
                if self.masked:
                    act.wait_ge(L["k_masked"], n + 1)
                else:
                    act.wait_ge(L["k_chunk_ready"], 2 * n + 4)
                act.dma_start(self.kT[:, :, bass.ds(n * CHUNK, CHUNK)], self.k_chunk[c][:, :, :])\
                   .then_inc(L[f"k_stored{c}"], 16)
        turns(act, NCHUNK // 2, chunk_turn)
        act.wait_ge(L["max_in_psum"], 1)
        act.activation(self.max_bc[:, 0:8, :], L.ps[:, 0:2, :].rearrange("p b (h n) -> p (b h) n", h=4),
                       ACT.Copy).then_inc(L["max_bc_ready"], 1)

        def tile_turn(i, last):
            for j in range(BODY):
                t = BODY * i + j
                act.wait_ge(L["centred"], 2 * t + 4)
                act.activation(self.p[j % 2][:, :, :], self.p[j % 2][:, :, :], ACT.Exp).then_inc(L["p_ready"], 1)
        turns(act, NT // BODY, tile_turn)
        self.attended.scalar(act)

    def gpsimd(self, pool):
        L, ones = self.L, self.net.const("ones")
        self.norm.gpsimd(pool)
        pool.sem_inc(L["kr_ready"], 2)
        pool.sem_inc(L["k_halves_ready"], SLOTS)
        for c in range(2):
            last = pool.memset(self.v[c][:, :, DH:DH + 1], 1.0)
        last.then_inc(L["ones_ready"], 1)
        if self.masked:
            pool.wait_ge(L["mask_cols_loaded"], 16)
            pool.tensor_scalar(self.fill_cols[:, :], self.mask_cols[:, :], -1.0, 1e8, ALU.add,
                               ALU.mult).then_inc(L["fill_cols_ready"], 1)

        def chunk_turn(i, last):
            for c in range(2):
                n = 2 * i + c
                pool.wait_ge(L["k_chunk_ready"], 2 * n + 4)
                pool.wait_ge(L["pair_scored"], 8 * n + 8)
                if self.masked:
                    pool.wait_ge(L["mask_wide_ready"], n + 1)
                    pool.tensor_tensor(self.unmask[c][0:3, :], ones[0:3, 0:1].broadcast_to([3, CHUNK]), self.mask_wide[c][0:3, :],
                                       ALU.subtract).then_inc(L["unmask_ready"], 1)
                    pool.tensor_tensor(self.k_chunk[c][:, :, :], self.k_chunk[c][:, :, :],
                                       times(self.mask_wide[c][:, :], DC), ALU.mult).then_inc(L["k_masked"], 1)
                    pool.wait_ge(L["k_masked"], n + 1)
                pool.tensor_tensor(self.kr_chunk[c][:, :, :], self.k_chunk[c][:, :, :], wide(ones[:, 0:DC], CHUNK),
                                   ALU.mult).then_inc(L["kr_ready"], 1)
        turns(pool, NCHUNK // 2, chunk_turn)
        if self.masked:
            pool.wait_ge(L["fill_cols_ready"], 1)

        def tile_turn(i, last):
            for j in range(BODY):
                t, par, slot = BODY * i + j, j % 2, j % SLOTS
                pool.wait_ge(L[f"tile_loaded{slot}"], 32 * (BODY // SLOTS * i + j // SLOTS + 1))
                pool.wait_ge(L["pair_in_psum"], 2 * t + 2)
                hi, lo = self.k_halves[par][:, 0, :, :], self.k_halves[par][:, 1, :, :]
                pool.tensor_tensor(hi, self.k_tile[:, slot, :, :], times(ones, DC), ALU.mult)\
                    .then_inc(L["k_hi_ready"], 1)
                if self.masked:
                    pool.wait_ge(L["centred"], 2 * t + 1)
                    pool.tensor_tensor(self.fill[par][:, :], self.fill_cols[:, bass.ds(t, 1)], ones[:, 0:1],
                                       ALU.mult)\
                        .then_inc(L["fill_ready"], 1)
                pool.wait_ge(L["k_hi_ready"], t + 1)
                pool.tensor_tensor(lo, self.k_tile[:, slot, :, :], hi.bitcast(F32), ALU.subtract)\
                    .then_inc(L["k_halves_ready"], 1)
        turns(pool, NT // BODY, tile_turn)

    def turned_queries(self, dve, o):
        L, tn, net = self.L, self.turn, self.net
        two_pi = 2.0 * np.pi
        hi = float(np.float32(6.28125))
        mid = float(np.float32(two_pi - hi))
        lo = float(two_pi - hi - mid)
        theta = self.w("theta")
        dve.tensor_reduce(tn[:, 8:9], self.w("gate"), AX_X, ALU.add).then_inc(L["gate_mean_ready"], 1)
        for k, quarter in ((0, 0.0), (2, 0.25)):
            o.after(dve.tensor_scalar(tn[:, 12 + k:14 + k], theta, 1.0 / two_pi, quarter, ALU.mult, ALU.add))
            o.after(dve.tensor_scalar(tn[:, 12 + k:14 + k], tn[:, 12 + k:14 + k], ROUND, -ROUND, ALU.add, ALU.add))
            o.after(dve.tensor_scalar(tn[:, k:k + 2], tn[:, 12 + k:14 + k], -hi, None, ALU.mult))
            o.after(dve.tensor_tensor(tn[:, k:k + 2], tn[:, k:k + 2], theta, ALU.add))
            for part in (-mid, -lo):
                o.after(dve.tensor_scalar(tn[:, 16:18], tn[:, 12 + k:14 + k], part, None, ALU.mult))
                o.after(dve.tensor_tensor(tn[:, k:k + 2], tn[:, k:k + 2], tn[:, 16:18], ALU.add))
            if k:
                o.after(dve.tensor_scalar(tn[:, 2:4], tn[:, 2:4], float(np.pi / 2), None, ALU.add))
        dve.tensor_scalar(tn[:, 0:4], tn[:, 0:4], 3.1415925, -3.1415925, ALU.min, ALU.max)\
           .then_inc(L["turn_angles"], 1)
        dve.wait_ge(L["gate_exp_ready"], 1)
        o.after(dve.tensor_scalar(tn[:, 10:11], tn[:, 9:10], 1.0, None, ALU.add))
        o.after(dve.reciprocal(tn[:, 10:11], tn[:, 10:11]))
        dve.wait_ge(L["sines_ready"], 1)
        o.after(dve.tensor_scalar(tn[:, 20:22], tn[:, 4:6], tn[:, 10:11], net.const("turn_sign"), ALU.mult, ALU.mult))
        o.after(dve.tensor_scalar(tn[:, 22:24], tn[:, 6:8], -1.0, tn[:, 10:11], ALU.add, ALU.mult))
        o.after(dve.tensor_scalar(tn[:, 22:24], tn[:, 22:24], net.const("turned"), 1.0, ALU.mult, ALU.add))
        for c in range(DC):
            o.after(dve.tensor_scalar(self.qT_swapped[:, c, :], self.qT_swapped[:, c, :], tn[:, 20 + c:21 + c], None,
                                      ALU.mult))
            o.after(dve.scalar_tensor_tensor(self.qT[:, c, :], self.qT[:, c, :], tn[:, 22 + c:23 + c],
                                             self.qT_swapped[:, c, :], ALU.mult, ALU.add))

    def vector(self, dve):
        L, net = self.L, self.net
        dve.sem_inc(L["pair_max_ready"], 3)
        dve.sem_inc(L["centred"], 2)
        dve.sem_inc(L["v_ready"], 2)
        self.norm.vector(dve)
        self.net.wait_weights(dve, L.name)
        o = L.order(dve, "mid_dve")
        dve.memset(self.row_max[:, :], -LARGEST).then_inc(L["row_max_ready"], 1)
        dve.wait_ge(L["q_in_psum"], 1)
        for c in range(DC):
            o.after(dve.tensor_scalar(self.qT[:, c, :], L.ps[:, 0, c * S:(c + 1) * S], self.w("bq")[:, c:c + 1],
                                      DH ** -0.5, ALU.add, ALU.mult))
        if self.turned:
            for c in range(DC):
                o.after(dve.tensor_scalar(self.qT_swapped[:, c, :], L.ps[:, 1, c * S:(c + 1) * S],
                                          self.w("bq_swapped")[:, c:c + 1], DH ** -0.5, ALU.add, ALU.mult))
            self.turned_queries(dve, o)
        q_full = self.p[0]
        for c in range(DC):
            o.after(dve.tensor_tensor(q_full[:, c * HPB:(c + 1) * HPB, :], times(self.qT[:, c, :], HPB),
                                      wide(net.const("head16"), S), ALU.mult))
        o.after(dve.tensor_copy(self.q_hi[:, :, :], q_full[:, :, :]))
        dve.tensor_tensor(self.q_lo[:, :, :], q_full[:, :, :], self.q_hi[:, :, :].bitcast(F32), ALU.subtract)\
           .then_inc(L["q_heads_ready"], 1)

        def chunk_turn(i, last):
            for c in range(2):
                n = 2 * i + c
                for pair in range(8):
                    dve.wait_ge(L["pair_scored"], 16 + 8 * n + pair + 1)
                    b = pair % 3 * 2
                    dve.tensor_reduce(self.chunk_max[c][:, 2 * pair:2 * pair + 2], L.ps[:, b:b + 2, 0:CHUNK], AX_X,
                                      ALU.max).then_inc(L["pair_max_ready"], 1)
                dve.wait_ge(L["pair_max_ready"], 8 * n + 11)
                dve.wait_ge(L["row_max_ready"], n + 1)
                dve.tensor_tensor(self.row_max[:, :], self.row_max[:, :], self.chunk_max[c][:, :], ALU.max)\
                   .then_inc(L["row_max_ready"], 1)
        turns(dve, NCHUNK // 2, chunk_turn)
        dve.wait_ge(L["row_max_ready"], NCHUNK + 1)
        dve.tensor_tensor(self.p[0][:, :, :], times(net.const("identity"), H), wide(self.row_max[:, :], S),
                          ALU.mult).then_inc(L["max_diagonals"], 1)
        dve.wait_ge(L["max_in_psum"], 1)
        dve.tensor_copy(self.max_bc[:, 8:16, :], L.ps[:, 2:4, :].rearrange("p b (h n) -> p (b h) n", h=4))\
           .then_inc(L["max_bc_ready"], 1)
        dve.wait_ge(L["max_bc_ready"], 2)
        dve.wait_ge(L["ones_ready"], 1)

        def tile_turn(i, last):
            for j in range(BODY):
                t, par = BODY * i + j, j % 2
                dve.wait_ge(L["tile_attended"], t + 1)
                if self.masked:
                    dve.wait_ge(L["fill_ready"], t + 1)
                for pair in range(2):
                    dve.wait_ge(L["pair_in_psum"], 4 + 2 * t + pair + 1)
                    out = self.p[par][:, 8 * pair:8 * pair + 8, :].rearrange("p h n -> p (h n)")
                    in0 = L.ps[:, 2 * pair:2 * pair + 2, :].rearrange("p b n -> p (b n)")
                    in1 = self.max_bc[:, 8 * pair:8 * pair + 8, :].rearrange("p h n -> p (h n)")
                    if self.masked:
                        ins = dve.scalar_tensor_tensor(out, in0, self.fill[par][:, 0:1], in1, ALU.add, ALU.subtract)
                    else:
                        ins = dve.tensor_tensor(out, in0, in1, ALU.subtract)
                    ins.then_inc(L["centred"], 1)
                dve.wait_ge(L["v_in_psum"], t + 1 + SLOTS)
                dve.tensor_tensor(self.v[par][:, :, 0:DH], L.ps[:, 4 + par, 0:D].rearrange("p (h n) -> p h n", h=H),
                                  self.w("bv").rearrange("p (h n) -> p h n", h=H), ALU.add)\
                   .then_inc(L["v_ready"], 1)
        turns(dve, NT // BODY, tile_turn)
        dve.wait_ge(L["tile_attended"], NT + 2)
        dve.tensor_copy(self.sums[:, :, :], L.ps[:, 6, :].rearrange("p (i n) -> p i n", i=4))\
           .then_inc(L["sums_ready"], 1)
        dve.wait_ge(L["sums_in_psum"], 1)
        sums = L.ps[:, 0, :].rearrange("p (i q n) -> p i q n", i=4, q=4)
        o.after(dve.reciprocal(self.rden[:, :, :], sums[:, :, :, DH]))
        for i in range(4):
            last = dve.tensor_tensor(self.o[:, i * 64:(i + 1) * 64].rearrange("p (q n) -> p q n", q=4),
                                     sums[:, i, :, 0:DH], wide(self.rden[:, i, :], DH), ALU.mult)
        last.then_inc(L["o_ready"], 1)
        dve.wait_ge(L["y_in_psum"], 1)
        o.after(dve.tensor_tensor(net.x[:, :], net.x[:, :], L.ps[:, 2, 0:D], ALU.add))
        o.after(dve.tensor_tensor(net.x[:, :], net.x[:, :], self.w("bo"), ALU.add))





class LatentAttention:

    RANK = 64

    def __init__(self, L):
        self.L, self.net, self.norm = L, L.net, NormRows(L)
        sb = L.sb
        self.qT, self.kT = sb("qT", [P, DC, S]), sb("kT", [P, DC, S])
        self.turned_part = sb("turned_part", [P, DC, S])
        self.lat = sb("lat", [S, self.RANK])
        self.latT = sb("latT", [self.RANK, S])
        self.lat_stats = sb("lat_stats", [S, 12])
        self.v, self.o = sb("v", [S, D]), sb("o", [S, D])
        self.oT = sb("oT", [P, DC, S])
        self.att = SelfAttention(L, DH, DH ** -0.5, True, 1, self.kT, self.v, self.o)
        self.attended = Transposed(L, "oT", self.o, DC, self.oT, 5)

    def w(self, name, **split):
        return self.net.w(self.L.name, name, **split)

    def sync(self, sp):
        self.net.load_weights(sp, LAYERS.index(self.L.name) + 1)

    def tensor(self, pe):
        L, xnT, n = self.L, self.norm.xnT, self.RANK
        self.norm.tensor(pe)
        self.net.wait_weights(pe, L.name)
        pe.wait_ge(L["xnT_ready"], 1)
        project(pe, L.ps[:, 0, 0:n], xnT, self.w("W_dkv", c=DC), slice(0, n)).then_inc(L["lat_in_psum"], 1)
        for bank, name in ((1, "W_q"), (2, "W_q_swapped")):
            for c in range(DC):
                last = project_T(pe, L.ps[:, bank, c * S:(c + 1) * S], xnT, self.w(name, c=DC),
                                 slice(c * P, (c + 1) * P))
            last.then_inc(L["q_in_psum"], 1)
        pe.wait_ge(L["lat_ready"], 1)
        pe.transpose(L.ps[0:n, 3, 0:S], self.lat[:, :], self.net.const("identity")).then_inc(L["latT_in_psum"], 1)
        pe.wait_ge(L["latT_ready"], 1)
        for bank, name in ((4, "W_uk"), (5, "W_uk_swapped")):
            for c in range(DC):
                last = pe.matmul(L.ps[:, bank, c * S:(c + 1) * S], self.w(name)[0:n, c * P:(c + 1) * P],
                                 self.latT[:, :], start=c == 0, stop=c == 1, skip_group_check=True)
            last.then_inc(L["k_in_psum"], 1)
        pe.matmul(L.ps[:, 6, 0:D], self.latT[:, :], self.w("W_uv")[0:n, :], start=True, stop=True)\
          .then_inc(L["v_in_psum"], 1)
        pe.wait_ge(L["qk_ready"], 2)
        pe.wait_ge(L["v_ready"], 1)
        self.att.tensor_scores(pe, 0)
        self.att.tensor_output(pe, 0)
        self.attended.tensor(pe, L["attended"])
        self.attended.wait(pe)
        project(pe, L.ps[:, 6, 0:D], self.oT, self.w("W_o", c=DC), slice(0, D)).then_inc(L["y_in_psum"], 1)

    def scalar(self, act):
        L = self.L
        self.norm.scalar(act)
        act.wait_ge(L["latT_in_psum"], 1)
        act.activation(self.latT[:, :], L.ps[0:self.RANK, 3, 0:S], ACT.Copy).then_inc(L["latT_ready"], 1)
        act.wait_ge(L["v_in_psum"], 1)
        act.activation(self.v[:, :], L.ps[:, 6, 0:D], ACT.Copy).then_inc(L["v_ready"], 1)
        self.att.scalar(act, 0)
        self.attended.scalar(act)

    def gpsimd(self, pool):
        L, st = self.L, self.lat_stats
        self.norm.gpsimd(pool)
        pool.wait_ge(L["lat_var_ready"], 1)
        pool.tensor_scalar(st[:, 8:9], st[:, 7:8], 1e-5, None, ALU.add).then_inc(L["lat_rstd_ready"], 1)
        pool.wait_ge(L["lat_rstd_ready"], 1)
        pool.tensor_tensor(st[:, 9:10], st[:, 8:9], self.net.const("neg_half"), ALU.pow)\
            .then_inc(L["lat_rstd_ready"], 1)

    def rotate(self, dve, o, out, banks):
        ps, net = self.L.ps, self.net
        straight = ps[:, banks[0], 0:DC * S].rearrange("p (c n) -> p c n", c=DC)
        swapped = ps[:, banks[1], 0:DC * S].rearrange("p (c n) -> p c n", c=DC)
        o.after(dve.tensor_tensor(self.turned_part[:, :, :], swapped, times(net.const("rope_sin"), DC), ALU.mult))
        o.after(dve.tensor_tensor(out[:, :, :], straight, times(net.const("rope_cos"), DC), ALU.mult))
        return dve.tensor_tensor(out[:, :, :], out[:, :, :], self.turned_part[:, :, :], ALU.add)

    def vector(self, dve):
        L, net, st = self.L, self.net, self.lat_stats
        self.norm.vector(dve)
        net.wait_weights(dve, L.name)
        o = L.order(dve, "latent_dve")
        dve.wait_ge(L["lat_in_psum"], 1)
        o.after(dve.tensor_copy(self.lat[:, :], L.ps[:, 0, 0:self.RANK]))
        o.after(dve.bn_stats(st[:, 0:6], self.lat[:, :]))
        dve.bn_aggr(st[:, 6:8], st[:, 0:6]).then_inc(L["lat_var_ready"], 1)
        dve.wait_ge(L["lat_rstd_ready"], 2)
        o.after(dve.tensor_scalar(self.lat[:, :], self.lat[:, :], st[:, 6:7], st[:, 9:10], ALU.subtract, ALU.mult))
        o.after(dve.tensor_tensor(self.lat[:, :], self.lat[:, :], self.w("ln_gamma"), ALU.mult))
        dve.tensor_tensor(self.lat[:, :], self.lat[:, :], self.w("ln_beta"), ALU.add).then_inc(L["lat_ready"], 1)
        dve.wait_ge(L["q_in_psum"], 2)
        self.rotate(dve, o, self.qT, (1, 2)).then_inc(L["qk_ready"], 1)
        dve.wait_ge(L["qk_ready"], 1)
        self.att.spread_vector(dve, 0, self.qT)
        dve.wait_ge(L["k_in_psum"], 2)
        self.rotate(dve, o, self.kT, (4, 5)).then_inc(L["qk_ready"], 1)
        self.att.vector(dve, 0)
        dve.wait_ge(L["y_in_psum"], 1)
        o.after(dve.tensor_tensor(net.x[:, :], net.x[:, :], L.ps[:, 6, 0:D], ALU.add))


class CausalAttention:

    def __init__(self, L):
        self.L, self.net, self.norm = L, L.net, NormRows(L)
        sb = L.sb
        self.qT, self.kT = sb("qT", [P, DC, S]), sb("kT", [P, DC, S])
        self.v, self.o = sb("v", [S, D]), sb("o", [S, D])
        self.oT = sb("oT", [P, DC, S])
        self.att = SelfAttention(L, DH, DH ** -0.5, True, 1, self.kT, self.v, self.o)
        self.attended = Transposed(L, "oT", self.o, DC, self.oT, 5)

    def w(self, name, **split):
        return self.net.w(self.L.name, name, **split)

    def sync(self, sp):
        self.net.load_weights(sp, LAYERS.index(self.L.name) + 1)

    def gpsimd(self, pool):
        self.norm.gpsimd(pool)

    def tensor(self, pe):
        L, xnT = self.L, self.norm.xnT
        self.norm.tensor(pe)
        self.net.wait_weights(pe, L.name)
        pe.wait_ge(L["xnT_ready"], 1)
        for part in range(2):
            for c in range(DC):
                at = part * D + c * P
                last = project_T(pe, L.ps[:, 4 + part, c * S:(c + 1) * S], xnT, self.w("Wqk", c=DC),
                                 slice(at, at + P))
            last.then_inc(L["qk_in_psum"], 1)
        project(pe, L.ps[:, 6, 0:D], xnT, self.w("Wv", c=DC), slice(0, D)).then_inc(L["v_in_psum"], 1)
        pe.wait_ge(L["kT_ready"], DC)
        pe.wait_ge(L["v_ready"], 1)
        self.att.tensor_scores(pe, 0)
        self.att.tensor_output(pe, 0)
        self.attended.tensor(pe, L["attended"])
        self.attended.wait(pe)
        project(pe, L.ps[:, 6, 0:D], self.oT, self.w("Wout", c=DC), slice(0, D)).then_inc(L["y_in_psum"], 1)

    def scalar(self, act):
        L = self.L
        self.norm.scalar(act)
        self.net.wait_weights(act, L.name)
        act.wait_ge(L["qk_in_psum"], 2)
        for c in range(DC):
            act.activation(self.kT[:, c, :], L.ps[:, 5, c * S:(c + 1) * S], ACT.Identity,
                           bias=self.w("bqk")[:, DC + c:DC + c + 1]).then_inc(L["kT_ready"], 1)
        self.att.scalar(act, 0)
        self.attended.scalar(act)

    def vector(self, dve):
        L, net = self.L, self.net
        self.norm.vector(dve)
        net.wait_weights(dve, L.name)
        o = L.order(dve, "latent_dve")
        dve.wait_ge(L["qk_in_psum"], 1)
        for c in range(DC):
            o.after(dve.tensor_scalar(self.qT[:, c, :], L.ps[:, 4, c * S:(c + 1) * S], self.w("bqk")[:, c:c + 1],
                                      None, ALU.add))
        self.att.spread_vector(dve, 0, self.qT)
        dve.wait_ge(L["v_in_psum"], 1)
        dve.tensor_tensor(self.v[:, :], L.ps[:, 6, 0:D], self.w("bv"), ALU.add).then_inc(L["v_ready"], 1)
        self.att.vector(dve, 0)
        dve.wait_ge(L["y_in_psum"], 1)
        o.after(dve.tensor_tensor(net.x[:, :], net.x[:, :], L.ps[:, 6, 0:D], ALU.add))
        o.after(dve.tensor_tensor(net.x[:, :], net.x[:, :], self.w("bout"), ALU.add))


class WideAttention:

    HEADS, WIDTH = 32, 32
    INNER = HEADS * WIDTH
    IC = INNER // P

    def __init__(self, L):
        self.L, self.net, self.norm = L, L.net, NormRows(L)
        sb, IC = L.sb, self.IC
        self.qT, self.kT = sb("qT", [P, IC, S]), sb("kT", [P, IC, S])
        self.v, self.o = sb("v", [S, self.INNER]), sb("o", [S, self.INNER])
        self.oT = sb("oT", [P, IC, S])
        self.y = sb("y", [S, D])
        self.y_stats = sb("y_stats", [S, 12])
        self.att = SelfAttention(L, self.WIDTH, self.WIDTH ** -0.5, False, 2, self.kT, self.v, self.o)
        self.attended = Transposed(L, "oT", self.o, IC, self.oT, 4)

    def w(self, name, **split):
        return self.net.w(self.L.name, name, **split)

    def sync(self, sp):
        self.net.load_weights(sp, LAYERS.index(self.L.name) + 1)

    def gpsimd(self, pool):
        L, st = self.L, self.y_stats
        self.norm.gpsimd(pool)
        pool.wait_ge(L["y_var_ready"], 1)
        pool.tensor_scalar(st[:, 8:9], st[:, 7:8], 1e-6, None, ALU.add).then_inc(L["y_rstd_ready"], 1)
        pool.wait_ge(L["y_rstd_ready"], 1)
        pool.tensor_tensor(st[:, 9:10], st[:, 8:9], self.net.const("neg_half"), ALU.pow)\
            .then_inc(L["y_rstd_ready"], 1)

    def tensor(self, pe):
        L, xnT, IC = self.L, self.norm.xnT, self.IC
        qkv = self.w("w_qkv", c=DC)
        self.norm.tensor(pe)
        self.net.wait_weights(pe, L.name)
        pe.wait_ge(L["xnT_ready"], 1)
        for bank in range(2 * IC // 4):
            for c in range(4):
                at = (bank * 4 + c) * P
                last = project_T(pe, L.ps[:, bank, c * S:(c + 1) * S], xnT, qkv, slice(at, at + P))
            last.then_inc(L["qk_in_psum"], 1)
        for b in range(2):
            at = 2 * self.INNER + b * BANK
            project(pe, L.ps[:, 4 + b, :], xnT, qkv, slice(at, at + BANK)).then_inc(L["v_in_psum"], 1)
        pe.wait_ge(L["qk_ready"], 4)
        pe.wait_ge(L["v_ready"], 2)
        for s in range(2):
            self.att.tensor_scores(pe, s)
            self.att.tensor_output(pe, s)
        self.attended.tensor(pe, L["attended"], 2)
        self.attended.wait(pe)
        project(pe, L.ps[:, 6, 0:D], self.oT, self.w("w_out", c=IC), slice(0, D)).then_inc(L["y_in_psum"], 1)

    def scalar(self, act):
        L = self.L
        self.norm.scalar(act)
        for b in (0, 2):
            act.wait_ge(L["qk_in_psum"], b + 1)
            dst = self.qT if b == 0 else self.kT
            act.activation(dst[:, 0:4, :], L.ps[:, b, :].rearrange("p (c n) -> p c n", c=4), ACT.Copy)\
               .then_inc(L["qk_ready"], 1)
        act.wait_ge(L["v_in_psum"], 1)
        act.activation(self.v[:, 0:BANK], L.ps[:, 4, :], ACT.Copy).then_inc(L["v_ready"], 1)
        for s in range(2):
            self.att.scalar(act, s)
        self.attended.scalar(act)

    def vector(self, dve):
        L, net, st = self.L, self.net, self.y_stats
        self.norm.vector(dve)
        for b in (1, 3):
            dve.wait_ge(L["qk_in_psum"], b + 1)
            dst = self.qT if b == 1 else self.kT
            dve.tensor_copy(dst[:, 4:8, :], L.ps[:, b, :].rearrange("p (c n) -> p c n", c=4)).then_inc(L["qk_ready"], 1)
        dve.wait_ge(L["v_in_psum"], 2)
        dve.tensor_copy(self.v[:, BANK:2 * BANK], L.ps[:, 5, :]).then_inc(L["v_ready"], 1)
        dve.wait_ge(L["qk_ready"], 4)
        for s in range(2):
            self.att.spread_vector(dve, s, self.qT)
            self.att.vector(dve, s)
        net.wait_weights(dve, L.name)
        o = L.order(dve, "latent_dve")
        dve.wait_ge(L["y_in_psum"], 1)
        o.after(dve.tensor_tensor(self.y[:, :], L.ps[:, 6, 0:D], self.w("b_out"), ALU.add))
        o.after(dve.bn_stats(st[:, 0:6], self.y[:, :]))
        dve.bn_aggr(st[:, 6:8], st[:, 0:6]).then_inc(L["y_var_ready"], 1)
        dve.wait_ge(L["y_rstd_ready"], 2)
        o.after(dve.tensor_scalar(self.y[:, :], self.y[:, :], st[:, 6:7], st[:, 9:10], ALU.subtract, ALU.mult))
        o.after(dve.tensor_tensor(self.y[:, :], self.y[:, :], self.w("ln_gamma"), ALU.mult))
        o.after(dve.tensor_tensor(self.y[:, :], self.y[:, :], self.w("ln_beta"), ALU.add))
        o.after(dve.tensor_tensor(net.x[:, :], net.x[:, :], self.y[:, :], ALU.add))




class QuantizedGatedLayer:

    I = 768
    IC = I // P
    BLOCK = 32

    def __init__(self, L):
        self.L, self.net, self.norm = L, L.net, NormRows(L)
        sb, I = L.sb, self.I
        nb = 6 * D // self.BLOCK
        self.blocks = sb("blocks", [P, 3, 2, nb])
        self.turned = {"w_gate": sb("w_gateT", [P, DC, I]), "w_up": sb("w_upT", [P, DC, I]),
                       "w_down": sb("w_downT", [P, self.IC, D])}
        self.xq = sb("xq", [S, D])
        self.xqT = sb("xqT", [P, DC, S])
        self.up, self.gate, self.sig = sb("up", [S, I]), sb("gate", [S, I]), sb("sig", [S, I])
        self.oT = sb("oT", [P, self.IC, S])
        self.scales = sb("scales", [P, 5, 4])
        self.x_turned = Transposed(L, "xqT", self.xq, DC, self.xqT, 0)
        self.o_turned = Transposed(L, "oT", self.gate, self.IC, self.oT, 4)

    SHAPES = (("w_gate", 6, 256), ("w_up", 6, 256), ("w_down", 2, 768))

    def sync(self, sp):
        self.net.load_weights(sp, LAYERS.index(self.L.name) + 1)

    def tensor(self, pe):
        L = self.L
        n = 0
        for name, row_blocks, width in self.SHAPES:
            pe.wait_ge(L["dequantized"], 1 + [s[0] for s in self.SHAPES].index(name))
            w = self.net.w(L.name, name, c=row_blocks)
            for k in range(3):
                if n >= 8:
                    pe.wait_ge(L["w_turned"], n - 7)
                for j in range(4):
                    r, c = self.block(name, 4 * k + j)
                    last = pe.transpose(L.ps[:, n % 8, j * P:(j + 1) * P], w[:, r, c * P:(c + 1) * P],
                                        self.net.const("identity"))
                last.then_inc(L["w_in_psum"], 1)
                n += 1
        pe.wait_ge(L["w_turned"], 9)
        self.x_turned.tensor(pe, L["quantized"], 1)
        self.x_turned.wait(pe)
        for bank, name in ((2, "w_up"), (4, "w_gate")):
            project(pe, L.ps[:, bank, :], self.xqT, self.turned[name], slice(0, BANK))
            project(pe, L.ps[:, bank + 1, 0:self.I - BANK], self.xqT, self.turned[name], slice(BANK, self.I))\
                .then_inc(L["up_gate_in_psum"], 1)
        self.o_turned.tensor(pe, L["quantized"], 5)
        self.o_turned.wait(pe)
        project(pe, L.ps[:, 6, 0:D], self.oT, self.turned["w_down"], slice(0, D)).then_inc(L["y_in_psum"], 1)

    def block(self, name, k):
        if name == "w_down":
            return k % 2, k // 2
        return k % 6, k // 6

    def scalar(self, act):
        L = self.L
        n = 0
        for name, _, _ in self.SHAPES:
            dst = self.turned[name][:, :, :].rearrange("p c n -> p (c n)")
            for k in range(3):
                act.wait_ge(L["w_in_psum"], n + 1)
                act.activation(dst[:, k * BANK:(k + 1) * BANK], L.ps[:, n % 8, :], ACT.Copy)\
                   .then_inc(L["w_turned"], 1)
                n += 1
        self.x_turned.scalar(act)
        act.wait_ge(L["quantized"], 3)
        act.activation(self.sig[:, :], self.gate[:, :], ACT.Sigmoid).then_inc(L["sigmoid_ready"], 1)
        self.o_turned.scalar(act)

    def gpsimd(self, pool):
        L = self.L
        self.norm.gpsimd(pool)
        for k in range(5):
            pool.wait_ge(L["row_absmax_ready"], k + 1)
            pool.partition_all_reduce(self.scales[:, k, 1:2], self.scales[:, k, 0:1], P, ABSMAX)\
                .then_inc(L["absmax_ready"], 1)

    def dequantize(self, dve, o, k):
        name = self.SHAPES[k][0]
        w = self.net.w(self.L.name, name).rearrange("p (b n) -> p b n", n=self.BLOCK)
        scale, inverse = self.blocks[:, k, 0, :], self.blocks[:, k, 1, :]
        o.after(dve.tensor_reduce(scale, w, AX_X, ALU.max, apply_absolute_value=True))
        o.after(dve.tensor_scalar(scale, scale, 1.0 / 7.0, 1e-12, ALU.mult, ALU.max))
        o.after(dve.reciprocal(inverse, scale))
        o.after(dve.tensor_tensor(w, w, wide(inverse, self.BLOCK), ALU.mult))
        o.after(dve.tensor_scalar(w, w, ROUND, -ROUND, ALU.add, ALU.add))
        o.after(dve.tensor_scalar(w, w, -8.0, 7.0, ALU.max, ALU.min))
        dve.tensor_tensor(w, w, wide(scale, self.BLOCK), ALU.mult).then_inc(self.L["dequantized"], 1)

    def quantize(self, dve, o, k, out, src):
        L, sc = self.L, self.scales
        dve.tensor_reduce(sc[:, k, 0:1], src, AX_X, ALU.max, apply_absolute_value=True)\
           .then_inc(L["row_absmax_ready"], 1)
        dve.wait_ge(L["absmax_ready"], k + 1)
        o.after(dve.tensor_scalar(sc[:, k, 2:3], sc[:, k, 1:2], 1.0 / 32767.0, 1e-12, ALU.mult, ALU.max))
        o.after(dve.reciprocal(sc[:, k, 3:4], sc[:, k, 2:3]))
        o.after(dve.tensor_scalar(out, src, sc[:, k, 3:4], ROUND, ALU.mult, ALU.add))
        o.after(dve.tensor_scalar(out, out, -ROUND, -32768.0, ALU.add, ALU.max))
        dve.tensor_scalar(out, out, 32767.0, sc[:, k, 2:3], ALU.min, ALU.mult).then_inc(L["quantized"], 1)

    def vector(self, dve):
        L, net, I = self.L, self.net, self.I
        o = L.order(dve, "gated_dve")
        net.wait_weights(dve, L.name)
        for k in range(3):
            self.dequantize(dve, o, k)
        self.norm_rows(dve)
        self.quantize(dve, o, 0, self.xq[:, :], self.norm.xn[:, :])
        for k, dst in ((1, self.up), (2, self.gate)):
            dve.wait_ge(L["up_gate_in_psum"], k)
            src = L.ps[:, 2 * k:2 * k + 2, :].rearrange("p b n -> p (b n)")[:, 0:I]
            self.quantize(dve, o, k, dst[:, :], src)
        dve.wait_ge(L["sigmoid_ready"], 1)
        sig = self.sig[:, :]
        o.after(dve.tensor_scalar(sig, sig, 65536.0, ROUND, ALU.mult, ALU.add))
        o.after(dve.tensor_scalar(sig, sig, -ROUND, 0.0, ALU.add, ALU.max))
        o.after(dve.tensor_scalar(sig, sig, 65535.0, 1.0 / 65536.0, ALU.min, ALU.mult))
        o.after(dve.tensor_tensor(self.gate[:, :], self.gate[:, :], sig, ALU.mult))
        self.quantize(dve, o, 3, self.gate[:, :], self.gate[:, :])
        dve.wait_ge(L["quantized"], 4)
        o.after(dve.tensor_tensor(self.gate[:, :], self.gate[:, :], self.up[:, :], ALU.mult))
        self.quantize(dve, o, 4, self.gate[:, :], self.gate[:, :])
        dve.wait_ge(L["y_in_psum"], 1)
        o.after(dve.tensor_tensor(net.x[:, :], net.x[:, :], L.ps[:, 6, 0:D], ALU.add))

    def norm_rows(self, dve):
        self.norm.vector(dve)
        dve.wait_ge(self.L["xn_ready"], 1)


class ExpertLayer:

    E, HID = 8, 1024
    HC = HID // P

    def __init__(self, L):
        self.L, self.net, self.norm = L, L.net, NormRows(L)
        sb, E = L.sb, self.E
        self.W1 = sb("W1", [P, E, DC, self.HID])
        self.W2 = sb("W2", [P, E, self.HC, D])
        self.hT = [sb(f"hT{c}", [P, self.HC, S]) for c in range(2)]
        self.route = sb("route", [S, 8, E])
        self.col = sb("col", [S, 4])
        self.route_T = sb("route_T", [E, S])

    def sync(self, sp):
        L, E, ins = self.L, self.E, self.net.ins
        w1 = ins["experts_W1"].rearrange("e (c p) n -> p e c n", p=P)
        w2 = ins["experts_W2"].rearrange("e (c p) n -> p e c n", p=P)
        for e in range(E):
            sp.dma_start(self.W1[:, e, :, :], w1[:, e, :, :]).then_inc(L[f"W1_loaded{e}"], 16)
            sp.dma_start(self.W2[:, e, :, :], w2[:, e, :, :]).then_inc(L[f"W2_loaded{e}"], 16)
        self.net.load_weights(sp, LAYERS.index(L.name) + 1)

    def gpsimd(self, pool):
        self.norm.gpsimd(pool)

    def tensor(self, pe):
        L, xnT, E = self.L, self.norm.xnT, self.E
        self.norm.tensor(pe)
        self.net.wait_weights(pe, L.name)
        pe.wait_ge(L["xnT_ready"], 1)
        project(pe, L.ps[:, 6, 0:E], xnT, self.net.w(L.name, "Wr", c=DC), slice(0, E)).then_inc(L["logits_in_psum"], 1)

        def hidden(e):
            pe.wait_ge(L[f"W1_loaded{e}"], 16)
            if e >= 2:
                pe.wait_ge(L["hidden_ready"], (e - 1) * self.HC)
            for b in range(self.HC):
                last = project_T(pe, L.ps[:, e % 2 * 2 + b // 4, b % 4 * S:(b % 4 + 1) * S], xnT,
                                 self.W1[:, e, :, :], slice(b * P, (b + 1) * P))
                if b % 4 == 3:
                    last.then_inc(L["hidden_in_psum"], 1)

        def output(e):
            pe.wait_ge(L[f"W2_loaded{e}"], 16)
            pe.wait_ge(L["hidden_ready"], (e + 1) * self.HC)
            if e >= 2:
                pe.wait_ge(L["expert_added"], e - 1)
            project(pe, L.ps[:, 4 + e % 2, 0:D], self.hT[e % 2], self.W2[:, e, :, :], slice(0, D))\
                .then_inc(L["expert_in_psum"], 1)

        hidden(0)
        pe.wait_ge(L["route_ready"], 1)
        pe.transpose(L.ps[0:E, 7, 0:S], self.route[:, 3, :], self.net.const("identity"))\
          .then_inc(L["route_T_in_psum"], 1)
        pe.wait_ge(L["route_T_ready"], 1)
        pe.matmul(L.ps[:, 6, 0:D], self.route_T[:, :], self.net.w(L.name, "b2")[0:E, :], start=True, stop=True)\
          .then_inc(L["b2_in_psum"], 1)
        for e in range(E):
            if e + 1 < E:
                hidden(e + 1)
            output(e)

    def scalar(self, act):
        L, E = self.L, self.E
        self.norm.scalar(act)
        self.net.wait_weights(act, L.name)
        act.wait_ge(L["logits_centred"], 1)
        act.activation(self.route[:, 3, :], self.route[:, 3, :], ACT.Exp).then_inc(L["route_exp_ready"], 1)
        act.wait_ge(L["route_T_in_psum"], 1)
        act.activation(self.route_T[:, :], L.ps[0:E, 7, 0:S], ACT.Copy).then_inc(L["route_T_ready"], 1)
        for e in range(E):
            if e >= 2:
                act.wait_ge(L["expert_in_psum"], e - 1)
            for b in range(self.HC):
                if b % 4 == 0:
                    act.wait_ge(L["hidden_in_psum"], 2 * e + b // 4 + 1)
                k = e * self.HC + b
                act.activation(self.hT[e % 2][:, b, :], L.ps[:, e % 2 * 2 + b // 4, b % 4 * S:(b % 4 + 1) * S],
                               ACT.Gelu, bias=self.net.w(L.name, "b1")[:, k:k + 1]).then_inc(L["hidden_ready"], 1)

    def vector(self, dve):
        L, net, E, r = self.L, self.net, self.E, self.route
        self.norm.vector(dve)
        net.wait_weights(dve, L.name)
        o = L.order(dve, "expert_dve")
        dve.wait_ge(L["logits_in_psum"], 1)
        o.after(dve.tensor_tensor(r[:, 0, :], L.ps[:, 6, 0:E], net.w(L.name, "br"), ALU.add))
        o.after(dve.max(r[:, 1, :], r[:, 0, :]))
        o.after(dve.tensor_scalar(r[:, 2, :], r[:, 0, :], r[:, 1, 1:2], None, ALU.is_ge))
        dve.tensor_scalar(r[:, 3, :], r[:, 0, :], r[:, 1, 0:1], None, ALU.subtract).then_inc(L["logits_centred"], 1)
        dve.wait_ge(L["route_exp_ready"], 1)
        o.after(dve.tensor_tensor(r[:, 4, :], r[:, 3, :], r[:, 2, :], ALU.mult))
        o.after(dve.tensor_reduce(self.col[:, 0:1], r[:, 4, :], AX_X, ALU.add))
        o.after(dve.reciprocal(self.col[:, 1:2], self.col[:, 0:1]))
        dve.tensor_scalar(r[:, 3, :], r[:, 4, :], self.col[:, 1:2], None, ALU.mult).then_inc(L["route_ready"], 1)
        dve.wait_ge(L["route_ready"], 1)
        dve.wait_ge(L["b2_in_psum"], 1)
        o.after(dve.tensor_tensor(net.x[:, :], net.x[:, :], L.ps[:, 6, 0:D], ALU.add))
        for e in range(E):
            dve.wait_ge(L["expert_in_psum"], e + 1)
            if e:
                dve.wait_ge(L["expert_added"], e)
            dve.scalar_tensor_tensor(net.x[:, :], L.ps[:, 4 + e % 2, 0:D], r[:, 3, e:e + 1], net.x[:, :], ALU.mult,
                                     ALU.add).then_inc(L["expert_added"], 1)


class FeatureAttention:

    M = 64
    TILES = 7
    CHUNKS = NT // TILES

    def __init__(self, L):
        self.L, self.net, self.norm = L, L.net, NormRows(L)
        sb, M = L.sb, self.M
        self.ctxT = [sb(f"ctxT{c}", [P, DC, self.TILES * P]) for c in range(2)]
        self.ctx = [sb(f"ctx{c}", [P, self.TILES, D + 1]) for c in range(2)]
        self.rf = [sb(f"rf{c}", [P, self.TILES * M]) for c in range(2)]
        self.kv = sb("kv", [M, D + 1])
        self.rf_q = sb("rf_q", [M, S])
        self.norm_col = sb("norm_col", [S, 2])
        self.y = sb("y", [S, D])

    def sync(self, sp):
        L, ins = self.L, self.net.ins
        ctxT = ins["ctxT"].rearrange("(c p) t -> p c t", p=P)
        ctx = ins["ctx"].rearrange("(j p) d -> p j d", p=P)
        n = self.TILES
        with sp.Fori(0, self.CHUNKS // 2) as i:
            for c in range(2):
                sp.wait_ge(L["logits_in_psum"], 2 * i + c + 1)
                sp.dma_start(self.ctxT[c][:, :, :], ctxT[:, :, bass.ds((2 * i + c) * n * P, n * P)])\
                  .then_inc(L[f"ctxT_loaded{c}"], 16)
                sp.wait_ge(L["chunk_summed"], 2 * i + c + 1)
                sp.dma_start(self.ctx[c][:, :, 0:D], ctx[:, bass.ds((2 * i + c) * n, n), :])\
                  .then_inc(L[f"ctx_loaded{c}"], 16)
        self.net.load_weights(sp, LAYERS.index(L.name) + 1)

    def gpsimd(self, pool):
        L = self.L
        for c in range(2):
            last = pool.memset(self.ctx[c][:, :, D:D + 1], 1.0)
        last.then_inc(L["ones_ready"], 1)
        self.norm.gpsimd(pool)

    def tensor(self, pe):
        L, M, proj = self.L, self.M, self.net.w(self.L.name, "projection", c=DC)
        pe.sem_inc(L["logits_in_psum"], 2)
        pe.sem_inc(L["chunk_summed"], 2)
        self.norm.tensor(pe)
        self.net.wait_weights(pe, L.name)
        pe.wait_ge(L["xnT_ready"], 1)
        for c in range(DC):
            last = pe.matmul(L.ps[0:M, 3, 0:S], proj[:, c, :], self.norm.xnT[:, c, :], start=c == 0, stop=c == 1)
        last.then_inc(L["q_in_psum"], 1)
        pe.matmul(L.ps[:, 2, :], self.net.zeros_bf[:, 0:P], self.net.zeros_bf[:, :], start=True, stop=True,
                  skip_group_check=True)
        pe.wait_ge(L["ones_ready"], 1)
        with pe.Fori(0, self.CHUNKS // 2) as i:
            for c in range(2):
                pe.wait_ge(L[f"ctxT_loaded{c}"], 16 * (i + 1))
                pe.wait_ge(L["rf_ready"], 2 * i + c + 1)
                for j in range(self.TILES):
                    for e in range(DC):
                        last = pe.matmul(L.ps[:, c, j * M:(j + 1) * M], self.ctxT[c][:, e, j * P:(j + 1) * P],
                                         proj[:, e, :], start=j == 0 and e == 0, stop=e == 1, skip_group_check=True)
                last.then_inc(L["logits_in_psum"], 1)
            for c in range(2):
                pe.wait_ge(L[f"ctx_loaded{c}"], 16 * (i + 1))
                pe.wait_ge(L["rf_ready"], 2 * i + c + 3)
                for j in range(self.TILES):
                    last = pe.matmul(L.ps[0:M, 2, 0:D + 1], self.rf[c][:, j * M:(j + 1) * M], self.ctx[c][:, j, :],
                                     start=False, stop=True, skip_group_check=True)
                last.then_inc(L["chunk_summed"], 1)
        pe.wait_ge(L["kv_ready"], 1)
        pe.wait_ge(L["rf_q_ready"], 2)
        pe.matmul(L.ps[:, 4, 0:D + 1], self.rf_q[:, :], self.kv[:, :], start=True, stop=True)\
          .then_inc(L["y_in_psum"], 1)

    def scalar(self, act):
        L, M = self.L, self.M
        act.sem_inc(L["rf_ready"], 2)
        self.norm.scalar(act)
        act.wait_ge(L["q_in_psum"], 1)
        act.activation(self.rf_q[:, :], L.ps[0:M, 3, 0:S], ACT.Exp, scale=D ** -0.5).then_inc(L["rf_q_ready"], 1)
        act.wait_ge(L["rf_q_ready"], 1)
        act.mul(self.rf_q[:, :], self.rf_q[:, :], M ** -0.5).then_inc(L["rf_q_ready"], 1)
        with act.Fori(0, self.CHUNKS // 2) as i:
            for c in range(2):
                act.wait_ge(L["logits_in_psum"], 2 * i + c + 3)
                act.wait_ge(L["chunk_summed"], 2 * i + c + 1)
                act.activation(self.rf[c][:, :], L.ps[:, c, 0:self.TILES * M], ACT.Exp, scale=D ** -0.5)\
                   .then_inc(L["rf_ready"], 1)

    def vector(self, dve):
        L, net = self.L, self.net
        self.norm.vector(dve)
        o = L.order(dve, "feature_dve")
        dve.wait_ge(L["chunk_summed"], self.CHUNKS + 2)
        dve.tensor_copy(self.kv[:, :], L.ps[0:self.M, 2, 0:D + 1]).then_inc(L["kv_ready"], 1)
        dve.wait_ge(L["y_in_psum"], 1)
        o.after(dve.tensor_scalar(self.norm_col[:, 0:1], L.ps[:, 4, D:D + 1], 1e-6, None, ALU.add))
        o.after(dve.reciprocal(self.norm_col[:, 1:2], self.norm_col[:, 0:1]))
        o.after(dve.scalar_tensor_tensor(net.x[:, :], L.ps[:, 4, 0:D], self.norm_col[:, 1:2], net.x[:, :], ALU.mult,
                                         ALU.add))


class Float8Layer:

    MOST = 448.0

    def __init__(self, L):
        self.L, self.net, self.norm = L, L.net, NormRows(L)
        sb = L.sb
        self.scales = sb("scales", [P, 2, 8])
        self.work = sb("work", [P, DC * D])
        self.unit = sb("unit", [P, DC * D])
        self.wq = sb("wq", [P, DC * D], BF16)
        self.xq = sb("xq", [P, DC * S], BF16)
        self.y16 = sb("y16", [S, D], BF16)
        self.y = sb("y", [S, D])

    def sync(self, sp):
        self.net.load_weights(sp, LAYERS.index(self.L.name) + 1)

    def gpsimd(self, pool):
        L = self.L
        self.norm.gpsimd(pool)
        for k in range(2):
            pool.wait_ge(L["row_absmax_ready"], k + 1)
            pool.partition_all_reduce(self.scales[:, k, 1:2], self.scales[:, k, 0:1], P, ABSMAX)\
                .then_inc(L["absmax_ready"], 1)

    def scalar(self, act):
        self.norm.scalar(act)

    def tensor(self, pe):
        L = self.L
        self.norm.tensor(pe)
        pe.wait_ge(L["quantized"], 2)
        xq = self.xq[:, :].rearrange("p (c n) -> p c n", c=DC)
        project(pe, L.ps[:, 0, 0:D], xq, self.wq[:, :].rearrange("p (c n) -> p c n", c=DC), slice(0, D))\
            .then_inc(L["y_in_psum"], 1)

    def quantize(self, dve, o, k, out, src):
        L, sc, n = self.L, self.scales, src.shape[1]
        work, unit = self.work[:, 0:n], self.unit[:, 0:n]
        dve.tensor_reduce(sc[:, k, 0:1], src, AX_X, ALU.max, apply_absolute_value=True)\
           .then_inc(L["row_absmax_ready"], 1)
        dve.wait_ge(L["absmax_ready"], k + 1)
        o.after(dve.tensor_scalar(sc[:, k, 2:3], sc[:, k, 1:2], 1e-12, None, ALU.max))
        o.after(dve.reciprocal(sc[:, k, 3:4], sc[:, k, 2:3]))
        o.after(dve.tensor_scalar(sc[:, k, 4:5], sc[:, k, 3:4], self.MOST, self.MOST, ALU.mult, ALU.min))
        o.after(dve.reciprocal(sc[:, k, 5:6], sc[:, k, 4:5]))
        o.after(dve.tensor_scalar(work, src, sc[:, k, 4:5], self.MOST, ALU.mult, ALU.min))
        o.after(dve.tensor_scalar(work, work, -self.MOST, None, ALU.max))
        o.after(dve.tensor_scalar(unit.bitcast(U32), work.bitcast(U32), 0x7F800000, None, ALU.bitwise_and))
        o.after(dve.tensor_scalar(unit, unit, 2.0 ** -6, 1.5 * 2.0 ** 20, ALU.max, ALU.mult))
        o.after(dve.tensor_tensor(work, work, unit, ALU.add))
        dve.tensor_tensor(out, work, unit, ALU.subtract).then_inc(L["quantized"], 1)

    def vector(self, dve):
        L, net, sc = self.L, self.net, self.scales
        self.norm.vector(dve)
        net.wait_weights(dve, L.name)
        o = L.order(dve, "float8_dve")
        self.quantize(dve, o, 0, self.wq[:, :], net.w(L.name, "weight"))
        dve.wait_ge(L["quantized"], 1)
        dve.wait_ge(L["xnT_ready"], 1)
        self.quantize(dve, o, 1, self.xq[:, :], self.norm.xnT[:, :, :].rearrange("p c n -> p (c n)"))
        o.after(dve.tensor_tensor(sc[:, 0, 6:7], sc[:, 0, 5:6], sc[:, 1, 5:6], ALU.mult))
        dve.wait_ge(L["y_in_psum"], 1)
        o.after(dve.scalar_tensor_tensor(self.y[:, :], L.ps[:, 0, 0:D], sc[:, 0, 6:7], net.w(L.name, "bias"),
                                         ALU.mult, ALU.add))
        o.after(dve.tensor_copy(self.y16[:, :], self.y[:, :]))
        o.after(dve.tensor_tensor(net.x[:, :], net.x[:, :], self.y16[:, :], ALU.add))


class LinearAttention:

    def __init__(self, L):
        self.L, self.net, self.norm = L, L.net, NormRows(L)
        sb = L.sb
        self.qkvT = sb("qkvT", [P, 3, DC, S])
        self.small = sb("small", [P, 2, DC, S])
        self.sums = sb("sums", [P, 2, DC])
        self.y = sb("y", [S, D])

    def sync(self, sp):
        self.net.load_weights(sp, LAYERS.index(self.L.name) + 1)

    def gpsimd(self, pool):
        self.norm.gpsimd(pool)

    def tensor(self, pe):
        L, xnT = self.L, self.norm.xnT
        self.norm.tensor(pe)
        self.net.wait_weights(pe, L.name)
        pe.wait_ge(L["xnT_ready"], 1)
        for k, name in enumerate(("Wq", "Wk", "Wv")):
            for c in range(DC):
                last = project_T(pe, L.ps[:, k, c * S:(c + 1) * S], xnT, self.net.w(L.name, name, c=DC),
                                 slice(c * P, (c + 1) * P))
            last.then_inc(L["qkv_in_psum"], 1)
        pe.wait_ge(L["attended"], 1)
        project(pe, L.ps[:, 3, 0:D], self.qkvT[:, 0, :, :], self.net.w(L.name, "Wo", c=DC), slice(0, D))\
            .then_inc(L["y_in_psum"], 1)

    def scalar(self, act):
        L = self.L
        self.norm.scalar(act)
        act.wait_ge(L["small_ready"], 1)
        act.activation(self.small[:, :, :, :], self.small[:, :, :, :], ACT.Exp).then_inc(L["small_exp_ready"], 1)
        act.wait_ge(L["y_ready"], 1)
        act.activation(self.y[:, :], self.y[:, :], ACT.Gelu_apprx_tanh).then_inc(L["gelu_ready"], 1)

    def vector(self, dve):
        L, net, t = self.L, self.net, self.qkvT
        self.norm.vector(dve)
        net.wait_weights(dve, L.name)
        o = L.order(dve, "linear_dve")
        for k in range(3):
            dve.wait_ge(L["qkv_in_psum"], k + 1)
            for c in range(DC):
                o.after(dve.tensor_scalar(t[:, k, c, :], L.ps[:, k, c * S:(c + 1) * S],
                                          net.w(L.name, "bqkv")[:, k * DC + c:k * DC + c + 1], None, ALU.add))
        dve.tensor_scalar(self.small[:, :, :, :], t[:, 0:2, :, :], 0.0, None, ALU.min).then_inc(L["small_ready"], 1)
        dve.wait_ge(L["small_exp_ready"], 1)
        flat = lambda a: a.rearrange("p k c n -> p (k c n)")
        o.after(dve.tensor_scalar(flat(self.small[:, :, :, :]), flat(self.small[:, :, :, :]), -1.0, None, ALU.add))
        o.after(dve.scalar_tensor_tensor(flat(t[:, 0:2, :, :]), flat(t[:, 0:2, :, :]), 0.0,
                                         flat(self.small[:, :, :, :]), ALU.max, ALU.add))
        o.after(dve.tensor_scalar(flat(t[:, 0:2, :, :]), flat(t[:, 0:2, :, :]), 1.0, None, ALU.add))
        o.after(dve.tensor_reduce(self.sums[:, 0, :], t[:, 1, :, :], AX_X, ALU.add))
        o.after(dve.tensor_tensor(t[:, 2, :, :], t[:, 1, :, :], t[:, 2, :, :], ALU.mult))
        o.after(dve.tensor_reduce(self.sums[:, 1, :], t[:, 2, :, :], AX_X, ALU.add))
        for c in range(DC):
            o.after(dve.tensor_scalar(t[:, 1, c, :], t[:, 0, c, :], self.sums[:, 0, c:c + 1], 1e-6, ALU.mult, ALU.add))
        o.after(dve.reciprocal(t[:, 1, :, :], t[:, 1, :, :]))
        for c in range(DC):
            last = dve.scalar_tensor_tensor(t[:, 0, c, :], t[:, 0, c, :], self.sums[:, 1, c:c + 1], t[:, 1, c, :],
                                            ALU.mult, ALU.mult)
        last.then_inc(L["attended"], 1)
        dve.wait_ge(L["y_in_psum"], 1)
        dve.tensor_tensor(self.y[:, :], L.ps[:, 3, 0:D], net.w(L.name, "bo"), ALU.add).then_inc(L["y_ready"], 1)
        dve.wait_ge(L["gelu_ready"], 1)
        o.after(dve.tensor_tensor(net.x[:, :], net.x[:, :], self.y[:, :], ALU.add))


class AdaptedExpertLayer:

    E, HID, R = 4, 1024, 4
    HC = HID // P

    def __init__(self, L):
        self.L, self.net, self.norm = L, L.net, NormRows(L)
        sb, E, F = L.sb, self.E, self.HID
        self.base = sb("base", [S, F])
        self.lowT = sb("lowT", [P, S])
        self.adapted = [sb(f"adapted{c}", [S, F]) for c in range(2)]
        self.weighted = [sb(f"weighted{c}", [S, F]) for c in range(2)]
        self.h = sb("h", [S, F])
        self.hT = sb("hT", [P, self.HC, S])
        self.route = sb("route", [S, 4, E])
        self.ahead = sb("ahead", [S, E, E])
        self.col = sb("col", [S, 4])
        self.h_turned = Transposed(L, "hT", self.h, self.HC, self.hT, 4)

    def w(self, name, **split):
        return self.net.w(self.L.name, name, **split)

    def sync(self, sp):
        pass

    def gpsimd(self, pool):
        L = self.L
        self.norm.gpsimd(pool)
        pool.memset(self.h[:, :], 0.0).then_inc(L["h_summed"], 1)
        for e in range(self.E):
            pool.wait_ge(L["weighted_ready"], e + 1)
            pool.wait_ge(L["h_summed"], e + 1)
            pool.tensor_tensor(self.h[:, :], self.h[:, :], self.weighted[e % 2][:, :], ALU.add)\
                .then_inc(L["h_summed"], 1)

    def tensor(self, pe):
        L, xnT, E = self.L, self.norm.xnT, self.E
        self.norm.tensor(pe)
        self.net.wait_weights(pe, L.name)
        pe.wait_ge(L["xnT_ready"], 1)
        project(pe, L.ps[:, 6, 0:E], xnT, self.w("Wg", c=DC), slice(0, E)).then_inc(L["logits_in_psum"], 1)
        project_T(pe, L.ps[:, 7, 0:S], xnT, self.w("A", c=DC), slice(0, P)).then_inc(L["low_in_psum"], 1)
        for b in range(2):
            project(pe, L.ps[:, 4 + b, :], xnT, self.w("Wi", c=DC), slice(b * BANK, (b + 1) * BANK))\
                .then_inc(L["base_in_psum"], 1)
        pe.wait_ge(L["lowT_ready"], 1)
        for e in range(E):
            if e >= 2:
                pe.wait_ge(L["adapted_ready"], e - 1)
            rows_e = slice(32 * e, 32 * e + self.R)
            for b in range(2):
                last = pe.matmul(L.ps[:, e % 2 * 2 + b, :], self.lowT[rows_e, :],
                                 self.w("B")[rows_e, b * BANK:(b + 1) * BANK], start=True, stop=True,
                                 tile_position=(32 * e, 0))
            last.then_inc(L["adapter_in_psum"], 1)
        self.h_turned.tensor(pe, L["h_summed"], E + 1)
        self.h_turned.wait(pe)
        project(pe, L.ps[:, 6, 0:D], self.hT, self.w("Wo", c=self.HC), slice(0, D)).then_inc(L["y_in_psum"], 1)

    def scalar(self, act):
        L = self.L
        self.norm.scalar(act)
        act.wait_ge(L["low_in_psum"], 1)
        act.activation(self.lowT[:, :], L.ps[:, 7, 0:S], ACT.Copy).then_inc(L["lowT_ready"], 1)
        act.wait_ge(L["logits_centred"], 1)
        act.activation(self.route[:, 1, :], self.route[:, 1, :], ACT.Exp).then_inc(L["route_exp_ready"], 1)
        act.wait_ge(L["base_in_psum"], 2)
        act.activation(self.base[:, :], L.ps[:, 4:6, :].rearrange("p b n -> p (b n)"), ACT.Copy)\
           .then_inc(L["base_ready"], 1)
        act.wait_ge(L["route_ready"], 1)
        for e in range(self.E):
            act.wait_ge(L["adapted_ready"], e + 1)
            if e >= 2:
                act.wait_ge(L["h_summed"], e)
            act.activation(self.weighted[e % 2][:, :], self.adapted[e % 2][:, :], ACT.Relu,
                           scale=self.route[:, 3, e:e + 1]).then_inc(L["weighted_ready"], 1)
        self.h_turned.scalar(act)

    def vector(self, dve):
        L, net, E, r = self.L, self.net, self.E, self.route
        self.norm.vector(dve)
        net.wait_weights(dve, L.name)
        o = L.order(dve, "adapted_dve")
        dve.wait_ge(L["logits_in_psum"], 1)
        o.after(dve.tensor_tensor(r[:, 0, :], L.ps[:, 6, 0:E], self.w("bg"), ALU.add))
        o.after(dve.tensor_reduce(self.col[:, 0:1], r[:, 0, :], AX_X, ALU.max))
        dve.tensor_scalar(r[:, 1, :], r[:, 0, :], self.col[:, 0:1], None, ALU.subtract)\
           .then_inc(L["logits_centred"], 1)
        dve.wait_ge(L["route_exp_ready"], 1)
        o.after(dve.tensor_reduce(self.col[:, 1:2], r[:, 1, :], AX_X, ALU.add))
        o.after(dve.reciprocal(self.col[:, 2:3], self.col[:, 1:2]))
        o.after(dve.tensor_scalar(r[:, 2, :], r[:, 1, :], self.col[:, 2:3], None, ALU.mult))
        o.after(dve.memset(self.ahead[:, :, :], 0.0))
        for e in range(E):
            if e:
                o.after(dve.tensor_scalar(self.ahead[:, e, 0:e], r[:, 2, 0:e], r[:, 2, e:e + 1], None, ALU.is_ge))
            if e < E - 1:
                o.after(dve.tensor_scalar(self.ahead[:, e, e + 1:E], r[:, 2, e + 1:E], r[:, 2, e:e + 1], None,
                                          ALU.is_gt))
        o.after(dve.tensor_reduce(r[:, 0, :], self.ahead[:, :, :], AX_X, ALU.add))
        dve.scalar_tensor_tensor(r[:, 3, :], r[:, 0, :], 1.5, r[:, 2, :], ALU.is_lt, ALU.mult)\
           .then_inc(L["route_ready"], 1)
        dve.wait_ge(L["base_ready"], 1)
        for e in range(E):
            dve.wait_ge(L["adapter_in_psum"], e + 1)
            if e >= 2:
                dve.wait_ge(L["weighted_ready"], e - 1)
            b = e % 2 * 2
            dve.tensor_tensor(self.adapted[e % 2][:, :], L.ps[:, b:b + 2, :].rearrange("p b n -> p (b n)"),
                              self.base[:, :], ALU.add).then_inc(L["adapted_ready"], 1)
        dve.wait_ge(L["y_in_psum"], 1)
        o.after(dve.tensor_tensor(net.x[:, :], net.x[:, :], L.ps[:, 6, 0:D], ALU.add))





def bass_perceiver_kernel(nc, ins, out):
    with ExitStack() as ctx:
        net = Net(nc, ctx, ins)
        with Layer(net, "setup") as L:
            block = L.ctx.enter_context(nc.Block())

            @block.sync
            def _(sp):
                sp.dma_start(net.const_sb[:, :], ins["consts"]).then_inc(net.first_loaded, 16)
                sp.dma_start(net.x[:, :], ins["x_rows"]).then_inc(net.first_loaded, 16)
                net.load_weights(sp, 0)
                sp.wait_ge(net.first_loaded, 32)

            @block.gpsimd
            def _(pool):
                pool.memset(net.zeros_bf[:, :], 0.0)

            @block.vector
            def _(dve):
                dve.wait_ge(net.first_loaded, 32)
                dve.tensor_copy(net.ident_bf[:, :], net.const("identity"))
                dve.tensor_copy(net.causal_bf[:, :, :], times(net.const("causal"), 4))
                dve.tensor_copy(net.causal_T_bf[:, :, :], times(net.const("causal_T"), 4))
                dve.tensor_copy(net.fill_bf[:, :], net.const("fill"))

        steps = {
            "L0_xattn": lambda L: CrossAttention(L, causal=True),
            "L0_attn": LatentAttention,
            "L0_ffn": QuantizedGatedLayer,
            "L1_xattn": lambda L: CrossAttention(L, masked=True),
            "L1_attn": WideAttention,
            "L1_ffn": ExpertLayer,
            "L2_xattn": FeatureAttention,
            "L2_attn": CausalAttention,
            "L2_ffn": Float8Layer,
            "L3_xattn": lambda L: CrossAttention(L, turned=True),
            "L3_attn": LinearAttention,
            "L3_ffn": AdaptedExpertLayer,
        }
        for name in LAYERS:
            with Layer(net, name) as L:
                step = steps[name](L)
                block = L.ctx.enter_context(nc.Block())
                block.sync(step.sync)
                block.gpsimd(step.gpsimd)
                block.scalar(step.scalar)
                block.vector(step.vector)
                block.tensor(step.tensor)

        with Layer(net, "end") as L:
            block = L.ctx.enter_context(nc.Block())

            @block.sync
            def _(sp):
                sp.dma_start(out, net.x[:, :]).then_inc(L["stored"], 16)
                sp.wait_ge(L["stored"], 16)




def rows(a):
    return a.reshape(a.shape[0] // P, P, -1).transpose(1, 0, 2).reshape(P, -1)


def cols(v):
    return v.reshape(-1, P).T


def each(v):
    return np.broadcast_to(v.reshape(1, -1), (P, v.size))


def padded(a):
    return np.concatenate([a, np.zeros((P - a.shape[0], a.shape[1]), a.dtype)])


def swapped_halves(w, half):
    order = np.arange(DH)
    order[:half], order[half:2 * half] = np.arange(half, 2 * half), np.arange(half)
    return w.reshape(w.shape[0], H, DH)[:, :, order].reshape(w.shape[0], D)


def packed(g):
    def xattn(n, turn):
        w = (lambda a: a) if n == "L0_xattn" else (lambda a: a.T)
        got = {k: rows(w(g(f"{n}_{k}"))) for k in ("Wq", "Wk", "Wv", "Wo")}
        got |= {"bq": cols(g(f"{n}_bq")), "bk": cols(g(f"{n}_bk")), "bv": each(g(f"{n}_bv")), "bo": each(g(f"{n}_bo"))}
        if turn:
            got |= {"Wq_swapped": rows(swapped_halves(w(g(f"{n}_Wq")), 1)),
                    "bq_swapped": cols(swapped_halves(g(f"{n}_bq")[None, :], 1)[0]),
                    "theta": cols(np.repeat(g(f"{n}_theta"), DH)), "gate": each(g(f"{n}_gate"))}
        return got

    a = lambda k: g(f"L0_attn_{k}")
    qkv = g("L2_attn_Wqkv").transpose(1, 0, 2)
    bqkv = g("L2_attn_bqkv")
    lora_A = np.zeros((D, P), np.float32).reshape(D, 4, 32)
    lora_A = np.concatenate([g("L3_ffn_A").transpose(2, 0, 1), lora_A[:, :, 4:]], axis=2).reshape(D, P)
    lora_B = g("L3_ffn_B").transpose(0, 2, 1)
    lora_B = np.concatenate([lora_B, np.zeros((4, 28, 1024), np.float32)], axis=1).reshape(P, 1024)
    r = lambda k: g(f"L3_attn_{k}")
    return {
        "L0_xattn": xattn("L0_xattn", False),
        "L0_attn": {"W_q": rows(a("W_q")), "W_q_swapped": rows(swapped_halves(a("W_q"), 8)),
                    "W_dkv": rows(a("W_dkv")), "W_uk": padded(a("W_uk")),
                    "W_uk_swapped": padded(swapped_halves(a("W_uk"), 8)), "W_uv": padded(a("W_uv")),
                    "W_o": rows(a("W_o")), "ln_gamma": each(a("ln_gamma")), "ln_beta": each(a("ln_beta"))},
        "L0_ffn": {k: rows(g(f"L0_ffn_{k}")) for k in ("w_gate", "w_up", "w_down")},
        "L1_xattn": xattn("L1_xattn", False),
        "L1_attn": {"w_qkv": rows(g("L1_attn_w_qkv")), "w_out": rows(g("L1_attn_w_out")),
                    "b_out": each(g("L1_attn_b_out")), "ln_gamma": each(g("L1_attn_ln_gamma")),
                    "ln_beta": each(g("L1_attn_ln_beta"))},
        "L1_ffn": {"Wr": rows(g("L1_ffn_Wr")), "br": each(g("L1_ffn_br")), "b1": cols(g("L1_ffn_b1").reshape(-1)),
                   "b2": padded(g("L1_ffn_b2"))},
        "L2_xattn": {"projection": rows(g("L2_xattn_projection").T)},
        "L2_attn": {"Wqk": rows(np.concatenate([qkv[:, :, 0:16].reshape(D, D), qkv[:, :, 16:32].reshape(D, D)], 1)),
                    "Wv": rows(qkv[:, :, 32:48].reshape(D, D)), "Wout": rows(g("L2_attn_Wout")),
                    "bqk": cols(np.concatenate([bqkv[:, 0:16].reshape(-1), bqkv[:, 16:32].reshape(-1)])),
                    "bv": each(bqkv[:, 32:48].reshape(-1)), "bout": each(g("L2_attn_bout"))},
        "L2_ffn": {"weight": rows(g("L2_ffn_weight").T), "bias": each(g("L2_ffn_bias"))},
        "L3_xattn": xattn("L3_xattn", True),
        "L3_attn": {"Wq": rows(r("Wq")), "Wk": rows(r("Wk")), "Wv": rows(r("Wv")), "Wo": rows(r("Wo")),
                    "bqkv": np.concatenate([cols(r("bq")), cols(r("bk")), cols(r("bv"))], 1), "bo": each(r("bo"))},
        "L3_ffn": {"Wg": rows(g("L3_ffn_Wg").T), "bg": each(g("L3_ffn_bg")), "Wi": rows(g("L3_ffn_Wi").T),
                   "Wo": rows(g("L3_ffn_Wo").T), "A": rows(lora_A), "B": lora_B},
    }


def laid_out(inputs):
    def g(name):
        return np.asarray(inputs[name])

    arrays = {}
    ctx_rows = g("ctx_1024").reshape(T, D)
    mask = g("mask_BxS2_bf1").reshape(T).view(np.uint8)
    arrays["ctxT"] = ctx_rows.T
    arrays["ctx"] = ctx_rows
    arrays["mask_row"] = mask[None, :]
    arrays["mask_cols"] = mask.reshape(NT, P).T
    arrays["x_rows"] = g("x").reshape(S, D)
    arrays["experts_W1"] = g("L1_ffn_W1")
    arrays["experts_W2"] = g("L1_ffn_W2")
    arrays["consts"] = constants()
    for layer, parts in packed(g).items():
        for name, n in PACKS[layer]:
            assert parts[name].shape == (P, n), (layer, name, parts[name].shape)
        arrays[f"pack_{layer}"] = np.concatenate([parts[name] for name, _ in PACKS[layer]], axis=1)
    return {k: np.ascontiguousarray(v) for k, v in arrays.items()}


def kernel(**inputs):
    import concourse.bacc as bacc
    from concourse.bass_utils import run_bass_kernel_spmd

    nc = bacc.Bacc("TRN2", target_bir_lowering=False, num_devices=1)
    arrays = {f"in_{k}": v for k, v in laid_out(inputs).items()}
    ins = {k[3:]: nc.dram_tensor(k, v.shape, mybir.dt.from_np(v.dtype), kind="ExternalInput").ap()
           for k, v in arrays.items()}
    out = nc.dram_tensor("out_rows", (S, D), F32, kind="ExternalOutput").ap()
    bass_perceiver_kernel(nc, ins, out)
    result = run_bass_kernel_spmd(nc, [arrays], core_ids=[0])
    return result.results[0]["out_rows"].reshape(1, S, D)
```

```python
from contextlib import ExitStack

import numpy as np

import concourse.bass as bass
from concourse import mybir

ALU = mybir.AluOpType
ACT = mybir.ActivationFunctionType
F32 = mybir.dt.float32
F32R = mybir.dt.float32r
BF16 = mybir.dt.bfloat16
U8 = mybir.dt.uint8
U32 = mybir.dt.uint32
AX_X = mybir.AxisListType.X
ABSMAX = bass.bass_isa.ReduceOp.absmax

P = 128
S = 128
D = 256
DC = D // P
T = 12544
H = 16
DH = D // H
HPB = P // DH
NT = T // P
BANK = 512
LARGEST = 3.0e38
NEG = -1.0e30
ROUND = 12582912.0

XATTN_PACK = [("Wq", DC * D), ("Wk", DC * D), ("Wv", DC * D), ("Wo", DC * D), ("bq", DC), ("bk", DC),
              ("bv", D), ("bo", D)]
PACKS = {
    "L0_xattn": XATTN_PACK,
    "L0_attn": [("W_q", DC * D), ("W_q_swapped", DC * D), ("W_dkv", DC * 64), ("W_uk", D), ("W_uk_swapped", D),
                ("W_uv", D), ("W_o", DC * D), ("ln_gamma", 64), ("ln_beta", 64)],
    "L0_ffn": [("w_gate", 6 * D), ("w_up", 6 * D), ("w_down", 2 * 768)],
    "L1_xattn": XATTN_PACK,
    "L1_attn": [("w_qkv", DC * 3072), ("w_out", 8 * D), ("b_out", D), ("ln_gamma", D), ("ln_beta", D)],
    "L1_ffn": [("Wr", DC * 8), ("br", 8), ("b1", 64), ("b2", D)],
    "L2_xattn": [("projection", DC * 64)],
    "L2_attn": [("Wqk", DC * 2 * D), ("Wv", DC * D), ("Wout", DC * D), ("bqk", 4), ("bv", D), ("bout", D)],
    "L2_ffn": [("weight", DC * D), ("bias", D)],
    "L3_xattn": XATTN_PACK + [("Wq_swapped", DC * D), ("bq_swapped", DC), ("theta", DC), ("gate", D)],
    "L3_attn": [("Wq", DC * D), ("Wk", DC * D), ("Wv", DC * D), ("Wo", DC * D), ("bqkv", 3 * DC), ("bo", D)],
    "L3_ffn": [("Wg", DC * 4), ("bg", 4), ("Wi", DC * 1024), ("Wo", 8 * D), ("A", DC * P), ("B", 1024)],
}
LAYERS = list(PACKS)
QUANTIZED = "L0_ffn"
CONSTS = [("identity", P), ("ones", P), ("causal", P), ("causal_T", P), ("rope_cos", S), ("rope_sin", S),
          ("head16", 8), ("head32", 4), ("neg_half", 1), ("fill", P), ("turned", 1), ("turn_sign", 1)]


def columns(pack):
    at, out = 0, {}
    for name, n in pack:
        out[name] = (at, at + n)
        at += n
    return out, at


def constants():
    p = np.arange(P)
    half = DH // 2
    inv_freq = (np.float32(1.0) / np.float32(10000.0) ** (np.arange(half, dtype=np.float32) / np.float32(half)))
    angle = np.arange(S, dtype=np.float32)[None, :] * inv_freq.astype(np.float32)[(p % DH) % half][:, None]
    sign = np.where(p % DH < half, -1.0, 1.0)[:, None]
    high = 390656.0 * 256
    fill = np.where(p == 0, high, np.where(p == 1, 1e8 - high, 0.0))[:, None] * np.ones((1, P))
    made = {
        "identity": np.eye(P), "ones": np.ones((P, P)), "fill": fill,
        "causal": np.where(p[None, :] > p[:, None], NEG, 0.0), "causal_T": np.where(p[:, None] > p[None, :], NEG, 0.0),
        "rope_cos": np.cos(angle), "rope_sin": np.sin(angle) * sign,
        "head16": p[:, None] // 16 == np.arange(8)[None, :], "head32": p[:, None] // 32 == np.arange(4)[None, :],
        "neg_half": np.full((P, 1), -0.5),
        "turned": (p % DH < 2)[:, None],
        "turn_sign": np.where(p % DH == 0, -1.0, np.where(p % DH == 1, 1.0, 0.0))[:, None],
    }
    return np.concatenate([np.asarray(made[n], np.float32) for n, _ in CONSTS], axis=1)


class Order:

    def __init__(self, eng, sem):
        self.eng, self.sem, self.n = eng, sem, 0

    def after(self, ins):
        self.n += 1
        ins.then_inc(self.sem, 1)
        self.eng.wait_ge(self.sem, self.n)


class Layer:

    def __init__(self, net, name):
        self.net, self.nc, self.name = net, net.nc, name
        self.sems = {}
        self.ctx = ExitStack()

    def __getitem__(self, name):
        if name not in self.sems:
            self.sems[name] = self.nc.alloc_semaphore(f"{self.name}_{name}")
        return self.sems[name]

    def sb(self, name, shape, dt=F32):
        return self.ctx.enter_context(self.nc.sbuf_tensor(f"{self.name}_{name}", shape, dt))

    def order(self, eng, name):
        return Order(eng, self[name])

    def __enter__(self):
        self.ps = self.ctx.enter_context(self.nc.psum_tensor(f"{self.name}_ps", [P, 8, BANK], F32))
        return self

    def __exit__(self, *exc):
        self.ctx.close()
        if exc[0] is None:
            self.nc.clear_and_free_semaphores(list(self.sems.values()))
            self.nc.all_engine_barrier()


class Net:

    def __init__(self, nc, ctx, ins):
        self.nc, self.ins = nc, ins
        self.const_at, n = columns(CONSTS)
        self.const_sb = ctx.enter_context(nc.sbuf_tensor("consts", [P, n], F32))
        self.ident_bf = ctx.enter_context(nc.sbuf_tensor("ident_bf", [P, P], BF16))
        self.causal_bf = ctx.enter_context(nc.sbuf_tensor("causal_bf", [P, 4, P], BF16))
        self.causal_T_bf = ctx.enter_context(nc.sbuf_tensor("causal_T_bf", [P, 4, P], BF16))
        self.zeros_bf = ctx.enter_context(nc.sbuf_tensor("zeros_bf", [P, BANK], BF16))
        self.x = ctx.enter_context(nc.sbuf_tensor("x_rows", [S, D], F32))
        sizes = [columns(PACKS[n])[1] for n in LAYERS]
        self.arena = [ctx.enter_context(nc.sbuf_tensor(f"weights_{k}", [P, max(sizes[k::2])], F32)) for k in range(2)]
        self.loaded = [nc.alloc_semaphore(f"{n}_weights_loaded") for n in LAYERS]
        self.first_loaded = nc.alloc_semaphore("x_and_consts_loaded")
        self.dequantized = nc.dram_tensor("dequantized", [P, columns(PACKS[QUANTIZED])[1]], F32, kind="Internal").ap()

    def const(self, name):
        a, b = self.const_at[name]
        return self.const_sb[:, a:b]

    def w(self, layer, name, **split):
        k = LAYERS.index(layer)
        a, b = columns(PACKS[layer])[0][name]
        v = self.arena[k % 2][:, a:b]
        return v.rearrange("p (c n) -> p c n", **split) if split else v

    def load_weights(self, eng, k):
        if k < len(LAYERS):
            n = columns(PACKS[LAYERS[k]])[1]
            source = self.dequantized if LAYERS[k] == QUANTIZED else self.ins[f"pack_{LAYERS[k]}"]
            eng.dma_start(self.arena[k % 2][:, 0:n], source).then_inc(self.loaded[k], 16)

    def wait_weights(self, eng, layer):
        eng.wait_ge(self.loaded[LAYERS.index(layer)], 16)




class NormRows:

    def __init__(self, L, bank=7):
        self.L, self.net, self.bank = L, L.net, bank
        self.stats = L.sb("stats", [S, 6])
        self.mv = L.sb("mean_var", [S, 2])
        self.rstd = L.sb("rstd", [S, 2])
        self.xn = L.sb("xn", [S, D])
        self.xnT = L.sb("xnT", [P, DC, S])

    def vector(self, dve):
        L, x = self.L, self.net.x
        o = L.order(dve, "norm_dve")
        o.after(dve.bn_stats(self.stats[:, :], x[:, :]))
        dve.bn_aggr(self.mv[:, :], self.stats[:, :]).then_inc(L["var_ready"], 1)
        dve.wait_ge(L["rstd_ready"], 2)
        dve.tensor_scalar(self.xn[:, :], x[:, :], self.mv[:, 0:1], self.rstd[:, 1:2], ALU.subtract,
                          ALU.mult).then_inc(L["xn_ready"], 1)

    def gpsimd(self, pool):
        L = self.L
        pool.wait_ge(L["var_ready"], 1)
        pool.tensor_scalar(self.rstd[:, 0:1], self.mv[:, 1:2], 1e-5, None, ALU.add).then_inc(L["rstd_ready"], 1)
        pool.wait_ge(L["rstd_ready"], 1)
        pool.tensor_tensor(self.rstd[:, 1:2], self.rstd[:, 0:1], self.net.const("neg_half"),
                           ALU.pow).then_inc(L["rstd_ready"], 1)

    def tensor(self, pe):
        L = self.L
        pe.wait_ge(L["xn_ready"], 1)
        for c in range(DC):
            last = pe.transpose(L.ps[:, self.bank, c * P:(c + 1) * P], self.xn[:, c * P:(c + 1) * P],
                                self.net.const("identity"))
        last.then_inc(L["xnT_in_psum"], 1)

    def scalar(self, act):
        L = self.L
        act.wait_ge(L["xnT_in_psum"], 1)
        act.activation(self.xnT[:, :, :], L.ps[:, self.bank, 0:DC * P].rearrange("p (c n) -> p c n", c=DC),
                       ACT.Copy).then_inc(L["xnT_ready"], 1)


class Transposed:

    def __init__(self, L, tag, src, C, dst, bank):
        self.L, self.tag, self.src, self.C, self.dst, self.bank = L, tag, src, C, dst, bank

    def tensor(self, pe, ready, n=1):
        L, C = self.L, self.C
        pe.wait_ge(ready, n)
        for c in range(C):
            last = pe.transpose(L.ps[:, self.bank + c // 4, c % 4 * P:(c % 4 + 1) * P],
                                self.src[:, c * P:(c + 1) * P], L.net.const("identity"))
        last.then_inc(L[f"{self.tag}_in_psum"], 1)

    def scalar(self, act):
        L, C = self.L, self.C
        act.wait_ge(L[f"{self.tag}_in_psum"], 1)
        for b in range(0, C, 4):
            k = min(4, C - b)
            last = act.activation(self.dst[:, b:b + k, :],
                                  L.ps[:, self.bank + b // 4, 0:k * P].rearrange("p (c n) -> p c n", c=k), ACT.Copy)
            last.then_inc(L[f"{self.tag}_ready"], 1)

    def wait(self, eng):
        eng.wait_ge(self.L[f"{self.tag}_ready"], -(-self.C // 4))


def project(pe, out, xT, W, cols, start=True, stop=True):
    C = W.shape[1]
    for c in range(C):
        last = pe.matmul(out, xT[:, c, :], W[:, c, cols], start=start and c == 0, stop=stop and c == C - 1)
    return last


def project_T(pe, out, xT, W, cols):
    C = W.shape[1]
    for c in range(C):
        last = pe.matmul(out, W[:, c, cols], xT[:, c, :], start=c == 0, stop=c == C - 1, skip_group_check=True)
    return last


def wide(ap, n):
    return ap.unsqueeze(2).broadcast_to([ap.shape[0], ap.shape[1], n])


def times(ap, m):
    return ap.unsqueeze(1).broadcast_to([ap.shape[0], m, ap.shape[1]])


class SelfAttention:

    HEADS = 8
    BANK_FREED = "attended"

    def __init__(self, L, dh, scale, causal, units, kT, v, out):
        self.L, self.dh, self.scale, self.causal, self.units = L, dh, scale, causal, units
        self.kT, self.v, self.out = kT, v, out
        self.q_heads = L.sb("q_heads", [P, 2, self.HEADS, S])
        self.p = L.sb("p", [S, 2, self.HEADS, S])
        self.pT = L.sb("pT", [S, 2, self.HEADS, S])
        self.mx = L.sb("score_max", [S, 2, self.HEADS])
        self.den = L.sb("den", [S, 2, 2, self.HEADS])
        self.blocks = self.HEADS * dh // P

    def scores_psum(self, u):
        b = u % 2 * 2
        return self.L.ps[:, b:b + 2, :].rearrange("p b (h n) -> p (b h) n", h=4)

    def spread_vector(self, dve, u, qT):
        L, per = self.L, P // self.dh
        if u >= 2:
            dve.wait_ge(L["scores_ready"], u - 1)
        mask = L.net.const("head16" if self.dh == 16 else "head32")
        for b in range(self.blocks):
            last = dve.tensor_tensor(self.q_heads[:, u % 2, b * per:(b + 1) * per, :],
                                     times(qT[:, u * self.blocks + b, :], per), wide(mask, S), ALU.mult)
        last.then_inc(L["q_heads_ready"], 1)

    def scores(self, pe, u):
        L, per, bank = self.L, P // self.dh, u % 2 * 2
        pe.wait_ge(L["q_heads_ready"], u + 1)
        if u >= 2:
            pe.wait_ge(L[self.BANK_FREED], u - 1)
        for g in range(2):
            if self.causal:
                pe.matmul(L.ps[:, bank + g, :], L.net.ident_bf[:, :],
                          L.net.causal_bf[:, :, :].rearrange("p a b -> p (a b)"), start=True, stop=False,
                          skip_group_check=True)
            for h in range(4 * g, 4 * g + 4):
                last = pe.matmul(L.ps[:, bank + g, h % 4 * S:(h % 4 + 1) * S], self.q_heads[:, u % 2, h, :],
                                 self.kT[:, u * self.blocks + h // per, :], start=h % 4 == 0 and not self.causal,
                                 stop=h % 4 == 3, skip_group_check=True)
        last.then_inc(L["scores_ready"], 1)

    def output(self, pe, u):
        L, dh = self.L, self.dh
        pe.wait_ge(L["pT_ready_act"], u + 1)
        pe.wait_ge(L["pT_ready_dve"], u + 1)
        for h in range(self.HEADS):
            at = (u * self.HEADS + h) * dh
            last = pe.matmul(L.ps[:, u % 2 * 2, h * dh:(h + 1) * dh], self.pT[:, u % 2, h, :], self.v[:, at:at + dh],
                             start=h == 0, stop=h == self.HEADS - 1, skip_group_check=True)
        last.then_inc(L["out_in_psum"], 1)

    def tensor(self, pe):
        L = self.L
        self.scores(pe, 0)
        self.scores(pe, 1)
        for u in range(self.units):
            pe.wait_ge(L["p_ready"], u + 1)
            if u >= 2:
                pe.wait_ge(L["pT_ready_act"], u - 1)
                pe.wait_ge(L["pT_ready_dve"], u - 1)
            for h in range(self.HEADS):
                last = pe.transpose(L.ps[:, 4 + u % 2 * 2 + h // 4, h % 4 * S:(h % 4 + 1) * S],
                                    self.p[:, u % 2, h, :], L.net.const("identity"))
            last.then_inc(L["pT_in_psum"], 1)
            if u:
                self.output(pe, u - 1)
                if u + 1 < self.units:
                    self.scores(pe, u + 1)
        self.output(pe, self.units - 1)

    def scalar(self, act):
        L = self.L
        for u in range(self.units + 1):
            if u < self.units:
                act.wait_ge(L["centred"], u + 1)
                p = self.p[:, u % 2, :, :]
                act.activation(p, p, ACT.Exp, scale=self.scale).then_inc(L["p_ready"], 1)
            if u:
                v, b = u - 1, 4 + (u - 1) % 2 * 2
                act.wait_ge(L["pT_in_psum"], v + 1)
                if v >= 2:
                    act.wait_ge(L["out_in_psum"], v - 1)
                act.activation(self.pT[:, v % 2, 0:4, :], L.ps[:, b, :].rearrange("p (h n) -> p h n", h=4),
                               ACT.Copy).then_inc(L["pT_ready_act"], 1)

    def divide(self, dve, u):
        L, dh, width = self.L, self.dh, self.HEADS * self.dh
        dve.wait_ge(L["out_in_psum"], u + 1)
        dve.tensor_tensor(self.out[:, u * width:(u + 1) * width].rearrange("p (h n) -> p h n", n=dh),
                          L.ps[:, u % 2 * 2, 0:width].rearrange("p (h n) -> p h n", n=dh),
                          wide(self.den[:, u % 2, 1, :], dh), ALU.mult).then_inc(L["attended"], 1)

    def vector(self, dve, qT):
        L, o = self.L, self.L.order(dve, "attention_dve")
        for u in range(self.units + 1):
            if u < self.units:
                dve.wait_ge(L["scores_ready"], u + 1)
                o.after(dve.tensor_reduce(self.mx[:, u % 2, :], self.scores_psum(u), AX_X, ALU.max))
                if u >= 2:
                    dve.wait_ge(L["pT_in_psum"], u - 1)
                dve.tensor_tensor(self.p[:, u % 2, :, :], self.scores_psum(u), wide(self.mx[:, u % 2, :], S),
                                  ALU.subtract).then_inc(L["centred"], 1)
                if u + 2 < self.units:
                    self.spread_vector(dve, u + 2, qT)
            if u:
                v, b = u - 1, 5 + (u - 1) % 2 * 2
                den = self.den[:, v % 2, :, :]
                dve.wait_ge(L["p_ready"], v + 1)
                o.after(dve.tensor_reduce(den[:, 0, :], self.p[:, v % 2, :, :], AX_X, ALU.add))
                o.after(dve.reciprocal(den[:, 1, :], den[:, 0, :]))
                dve.wait_ge(L["pT_in_psum"], v + 1)
                if v >= 2:
                    dve.wait_ge(L["out_in_psum"], v - 1)
                dve.tensor_copy(self.pT[:, v % 2, 4:8, :], L.ps[:, b, :].rearrange("p (h n) -> p h n", h=4))\
                   .then_inc(L["pT_ready_dve"], 1)
                self.divide(dve, v)


class TransposedSelfAttention(SelfAttention):

    BANK_FREED = "centred"

    def output(self, pe, u):
        L, dh = self.L, self.dh
        pe.wait_ge(L["pT_ready"], u + 1)
        for h in range(self.HEADS):
            at, q = (u * self.HEADS + h) * dh, h % 4 * dh
            last = pe.matmul(L.ps[q:q + dh, 4 + u % 2 * 2, h // 4 * S:(h // 4 + 1) * S], self.v[:, at:at + dh],
                             self.pT[:, u % 2, h, :], start=True, stop=True, skip_group_check=True)
        last.then_inc(L["out_in_psum"], 1)

    def tensor(self, pe):
        L = self.L
        self.scores(pe, 0)
        self.scores(pe, 1)
        for u in range(self.units):
            pe.wait_ge(L["p_divided"], u + 1)
            if u >= 2:
                pe.wait_ge(L["attended"], u - 1)
            for h in range(self.HEADS):
                last = pe.transpose(L.ps[:, 4 + u % 2 * 2 + h // 4, h % 4 * S:(h % 4 + 1) * S],
                                    self.p[:, u % 2, h, :], L.net.const("identity"))
            last.then_inc(L["pT_in_psum"], 1)
            if u + 2 < self.units:
                self.scores(pe, u + 2)
            self.output(pe, u)

    def scalar(self, act):
        L = self.L
        for u in range(self.units + 1):
            if u < self.units:
                act.wait_ge(L["centred"], u + 1)
                p = self.p[:, u % 2, :, :]
                act.activation(p, p, ACT.Exp, scale=self.scale).then_inc(L["p_ready"], 1)
            if u:
                v, b = u - 1, 4 + (u - 1) % 2 * 2
                act.wait_ge(L["pT_in_psum"], v + 1)
                if v >= 2:
                    act.wait_ge(L["out_in_psum"], v - 1)
                act.activation(self.pT[:, v % 2, :, :], L.ps[:, b:b + 2, :].rearrange("p b (h n) -> p (b h) n", h=4),
                               ACT.Copy).then_inc(L["pT_ready"], 1)
                act.wait_ge(L["out_in_psum"], v + 1)
                act.activation(self.out[:, 2 * v:2 * v + 2, :],
                               L.ps[:, b, 0:2 * S].rearrange("p (c n) -> p c n", c=2), ACT.Copy)\
                   .then_inc(L["attended"], 1)

    def vector(self, dve, qT):
        L, o = self.L, self.L.order(dve, "attention_dve")
        for u in range(self.units + 1):
            if u < self.units:
                dve.wait_ge(L["scores_ready"], u + 1)
                o.after(dve.tensor_reduce(self.mx[:, u % 2, :], self.scores_psum(u), AX_X, ALU.max))
                if u >= 2:
                    dve.wait_ge(L["pT_in_psum"], u - 1)
                dve.tensor_tensor(self.p[:, u % 2, :, :], self.scores_psum(u), wide(self.mx[:, u % 2, :], S),
                                  ALU.subtract).then_inc(L["centred"], 1)
                if u + 2 < self.units:
                    self.spread_vector(dve, u + 2, qT)
            if u:
                v = u - 1
                den, p = self.den[:, v % 2, :, :], self.p[:, v % 2, :, :]
                dve.wait_ge(L["p_ready"], v + 1)
                o.after(dve.tensor_reduce(den[:, 0, :], p, AX_X, ALU.add))
                o.after(dve.reciprocal(den[:, 1, :], den[:, 0, :]))
                dve.tensor_tensor(p, p, wide(den[:, 1, :], S), ALU.mult).then_inc(L["p_divided"], 1)




KEYS = 2 * P
NCHUNK = T // KEYS
BODY = 7
TURNS = NCHUNK // BODY
assert NCHUNK * KEYS == T and TURNS * BODY == NCHUNK

RING3 = (0, 1, 0, 1, 0, 1, 2)
RING4 = (0, 1, 2, 0, 1, 2, 3)
UNITS = 4 * BODY
BANKS = tuple(u % 3 for u in range(UNITS - 1)) + (1,)


def uses(ring, i, j):
    return ring.count(ring[j]) * i + ring[:j].count(ring[j])


def units_since(u):
    return next(k for k in range(1, UNITS) if BANKS[(u - k) % UNITS] == BANKS[u])


def turns(eng, count, body):
    with eng.Fori(0, count - 1) as i:
        body(i, False)
    body(count - 1, True)


class CrossAttention:

    PIECES = 9

    def __init__(self, L, causal=False, masked=False, turned=False, dequantizing=False):
        self.L, self.net, self.nc, self.dequantizing = L, L.net, L.nc, dequantizing
        self.causal, self.masked, self.turned = causal, masked, turned
        self.norm = NormRows(L)
        sb = L.sb
        self.w_halves = [sb(f"w_halves{h}", [P, 2, DC, D], F32R) for h in range(2)]
        self.qT = sb("qT", [P, DC, S])
        self.qT_halves = sb("qT_halves", [P, 2, DC, S], F32R)
        self.q_hi = sb("q_hi", [P, H, S], F32R)
        self.q_lo = sb("q_lo", [P, H, S], F32R)
        self.q_packed = sb("q_packed", [P, H, S], F32R)
        self.ctx_chunk = [sb(f"ctx_chunk{c}", [P, DC, KEYS]) for c in range(3)]
        self.ctx_halves = [sb(f"ctx_halves{c}", [P, 2, DC, KEYS], F32R) for c in range(3)]
        self.k_full = [sb(f"k_full{c}", [P, DC, KEYS]) for c in range(3)]
        self.k_halves = [sb(f"k_halves{c}", [P, 2, DC, KEYS], F32R) for c in range(3)]
        self.v_chunk = [sb(f"v_chunk{c}", [P, 2, H, DH + 1]) for c in range(3)]
        self.turn_max = sb("turn_max", [S, BODY, H])
        self.row_max = sb("row_max", [S, 2, H])
        self.minus_max = sb("minus_max", [S, 3, H], F32R)
        self.minus_max_T = sb("minus_max_T", [3 * H, S])
        self.k_packed = [sb(f"k_packed{c}", [P, H // 2, KEYS], F32R) for c in range(4)]
        self.v_group = [sb(f"v_group{c}", [P, 2, H, DH + 1]) for c in range(4)]
        self.p = [sb(f"p{c}", [P, H, S]) for c in range(2)]
        flat = [c[:, :, :].rearrange("p c t -> p (c t)") for c in self.ctx_chunk]
        self.sums = flat[0].rearrange("p (i n) -> p i n", n=S)
        self.o = flat[1][:, 0:D]
        self.oT = flat[2][:, 0:DC * S].rearrange("p (c n) -> p c n", n=S)
        self.rden = sb("rden", [S, H])
        self.attended = Transposed(L, "oT", self.o, DC, self.oT, 1)
        dram = self.nc.dram_tensor
        self.k_dram = dram(f"{L.name}_k", [NCHUNK, 2 * D, KEYS], F32, kind="Internal").ap()
        self.v_dram = dram(f"{L.name}_v", [T, H * (DH + 1)], F32, kind="Internal").ap()
        if dequantizing:
            self.block_scale = sb("block_scale", [P, 2, 16])
            self.pieces = [flat[c] for c in range(3)]
            self.pieces += [k[:, :, :].rearrange("p c t -> p (c t)") for k in self.k_full]
            self.pieces += [v[:, :, :, :].rearrange("p t h n -> p (t h n)")[:, 0:16 * 32] for v in self.v_chunk]
            assert columns(PACKS[QUANTIZED])[1] == self.PIECES * 16 * 32
        if masked:
            self.mask_u8 = sb("mask_u8", [NT, P], U8)
            self.mask_rows = self.v_group[3][0:NT, :, :, :].rearrange("p t h n -> p (t h n)")[:, 0:3 * P]\
                .rearrange("p (k n) -> p k n", k=3)
            self.mask_chunk = [sb(f"mask_chunk{c}", [P, KEYS]) for c in range(3)]
            self.fill_chunk = [sb(f"fill_chunk{c}", [P, KEYS]) for c in range(3)]
            self.mask_dram = dram(f"{L.name}_mask", [3, T], F32, kind="Internal").ap()
        if turned:
            self.turn = sb("turn", [P, 24])
            self.qT_swapped = sb("qT_swapped", [P, DC, S])

    def w(self, name, **split):
        return self.net.w(self.L.name, name, **split)


    def load_context(self, sp, n, j):
        L, c, at = self.L, RING3[j], bass.ds(n * KEYS, KEYS)
        ctxT = self.net.ins["ctxT"].rearrange("(c p) t -> p c t", p=P)
        sp.wait_ge(L["ctx_split"], n + 1)
        sp.dma_start(self.ctx_chunk[c][:, :, :], ctxT[:, :, at])\
          .then_inc(L[f"ctx_loaded{c}"], 16)

    def load_mask(self, sp, n, j):
        L, c, at = self.L, RING3[j], bass.ds(n * KEYS, KEYS)
        sp.wait_ge(L["k_full_ready"], n + 1)
        sp.dma_start(self.mask_chunk[c][:, :], self.mask_dram[0:1, at]
                     .broadcast_to([P, KEYS])).then_inc(L[f"mask_loaded{c}"], 16)

    def load_fill(self, sp, n, j):
        L, c, at = self.L, RING3[j], bass.ds(n * KEYS, KEYS)
        row = self.mask_dram[2:3, at].broadcast_to([P, KEYS])
        sp.wait_ge(L["unit_filled"], 4 * n + 4)
        sp.dma_start(self.fill_chunk[c][:, :], row).then_inc(L[f"fill_loaded{c}"], 16)

    def store_chunk(self, sp, n, j):
        L, c = self.L, RING3[j]
        v_rows = self.v_dram[bass.ds(n * KEYS, KEYS), :].rearrange("(t p) x -> p t x", p=P)
        sp.wait_ge(L["v_drained"], n + 2)
        sp.dma_start(v_rows, self.v_chunk[c][:, :, :, :].rearrange("p t h n -> p t (h n)"))\
          .then_inc(L[f"v_stored{c}"], 16)
        sp.wait_ge(L["k_lo_ready"], n + 3)
        sp.dma_start(self.k_dram[bass.ds(n, 1), :, :].rearrange("o (a p) t -> p (o a) t", p=P),
                     self.k_halves[c][:, :, :, :].rearrange("p a c t -> p (a c) t").bitcast(F32))\
          .then_inc(L[f"k_stored{c}"], 16)

    def load_group_mask(self, sp, n, j):
        L, c, at = self.L, RING4[j], bass.ds(n * KEYS, KEYS)
        for row in (99, 100):
            sp.dma_start(self.k_packed[c][row:row + 1, :, :].bitcast(F32),
                         self.mask_dram[1:2, at].unsqueeze(1).broadcast_to([1, H // 2, KEYS]))\
              .then_inc(L[f"group_loaded{c}"], 16)

    def load_group(self, sp, n, j):
        L, c, at = self.L, RING4[j], bass.ds(n * KEYS, KEYS)
        v_rows = self.v_dram[at, :].rearrange("(t p) x -> p t x", p=P)
        sp.wait_ge(L["unit_scored"], 4 * n + 4)
        for g, half in enumerate((0, 0, 1)):
            sp.dma_start(self.k_packed[c][32 * g:32 * g + 32, :, :].bitcast(F32),
                         self.k_dram[bass.ds(n, 1), half * D:(half + 1) * D, :]
                         .rearrange("o (j r) t -> r (o j) t", r=32))\
              .then_inc(L[f"group_loaded{c}"], 16)
        sp.wait_ge(L["tile_attended"], 2 * n + 2)
        sp.dma_start(self.v_group[c][:, :, :, :].rearrange("p t h n -> p t (h n)"), v_rows)\
          .then_inc(L[f"v_loaded{c}"], 16)

    def pack_queries(self, sp):
        L = self.L
        if self.masked:
            sp.wait_ge(L["q_packed_cleared"], 1)
            sp.dma_start(self.q_packed[99:101, :, :].bitcast(F32), times(self.net.const("fill")[0:2, :], H))\
              .then_inc(L["q_packed_ready"], 16)
        sp.wait_ge(L["q_heads_ready"], 2)
        for quarter in range(4):
            own = slice(32 * quarter, 32 * quarter + 32)
            for g, q in enumerate((self.q_hi, self.q_lo, self.q_hi)):
                def heads(a):
                    return a.rearrange("r (c h) n -> r c h n", c=DC)[:, :, 2 * quarter:2 * quarter + 2, :].bitcast(F32)
                sp.dma_start(heads(self.q_packed[32 * g:32 * g + 32, :, :]), heads(q[own, :, :]))\
                  .then_inc(L["q_packed_ready"], 16)

    def sync(self, sp):
        L, ins = self.L, self.net.ins
        if self.masked:
            sp.dma_start(self.mask_u8[:, :], ins["mask_rows"]).then_inc(L["mask_u8_loaded"], 16)
            sp.wait_ge(L["mask_rows_ready"], 3)
            for k in range(3):
                sp.dma_start(self.mask_dram[k].rearrange("(t n) -> t n", t=NT), self.mask_rows[:, k, :])\
                  .then_inc(L["mask_stored"], 16)
            sp.wait_ge(L["mask_stored"], 48)

        for j in range(3):
            self.load_context(sp, j, j)
        if self.masked:
            self.load_mask(sp, 0, 0)
            self.load_mask(sp, 1, 1)
            self.load_fill(sp, 0, 0)
            self.load_fill(sp, 1, 1)

        def chunk_turn(i, last):
            for j in range(BODY):
                n = BODY * i + j
                for ahead, load in ((3, self.load_context), (2, self.load_mask), (2, self.load_fill)):
                    if (self.masked or ahead == 3) and not (last and j + ahead >= BODY):
                        load(sp, n + ahead, (j + ahead) % BODY)
                if last and j == 0:
                    self.pack_queries(sp)
                if last and j == BODY - 3:
                    for s in range(3):
                        sp.wait_ge(L[f"k_stored{s}"], 16 * (RING3.count(s) + 1))
                        sp.wait_ge(L[f"v_stored{s}"], 16 * (RING3.count(s) + 1))
                    for m in range(3):
                        self.load_group(sp, m, m)
                self.store_chunk(sp, n, j)
        turns(sp, TURNS, chunk_turn)
        if self.masked:
            sp.wait_ge(L["k_packed_ones"], 4)
            for m in range(3):
                self.load_group_mask(sp, m, m)
        for s in range(3):
            sp.wait_ge(L[f"k_stored{s}"], 16 * (RING3.count(s) * TURNS + 1))
            sp.wait_ge(L[f"v_stored{s}"], 16 * (RING3.count(s) * TURNS + 1))
        if self.dequantizing:
            raw = self.net.ins[f"pack_{QUANTIZED}"].rearrange("p (k n) -> p k n", k=self.PIECES)
            sp.wait_ge(L["k_lo_ready"], NCHUNK + 2)
            for k in range(self.PIECES):
                sp.dma_start(self.pieces[k], raw[:, k, :]).then_inc(L[f"piece_loaded{k}"], 16)

        def group_turn(i, last):
            for j in range(BODY):
                if not (last and j + 3 >= BODY):
                    self.load_group(sp, BODY * i + j + 3, (j + 3) % BODY)
                    if self.masked:
                        self.load_group_mask(sp, BODY * i + j + 3, (j + 3) % BODY)
                if last and j == BODY - 3:
                    self.net.load_weights(sp, LAYERS.index(L.name) + 1)
                    if self.dequantizing:
                        made = self.net.dequantized.rearrange("p (k n) -> p k n", k=self.PIECES)
                        for k in range(self.PIECES):
                            sp.wait_ge(L["piece_ready"], k + 1)
                            sp.dma_start(made[:, k, :], self.pieces[k]).then_inc(L["pieces_stored"], 16)
        turns(sp, TURNS, group_turn)
        if self.dequantizing:
            sp.wait_ge(L["pieces_stored"], 16 * self.PIECES)


    def pe_queries(self, pe):
        L, xnT = self.L, self.norm.xnT
        pe.wait_ge(L["xnT_ready"], 1)
        for c in range(DC):
            last = project_T(pe, L.ps[:, 0, c * S:(c + 1) * S], xnT, self.w("Wq", c=DC), slice(c * P, (c + 1) * P))
        if self.turned:
            for c in range(DC):
                last = project_T(pe, L.ps[:, 1, c * S:(c + 1) * S], xnT, self.w("Wq_swapped", c=DC),
                                 slice(c * P, (c + 1) * P))
        last.then_inc(L["q_in_psum"], 1)

    def pe_keys_and_values(self, pe, n, c, part):
        L, x, (wk, wv) = self.L, self.ctx_halves[c], self.w_halves
        terms = [(a, b, e) for a, b in ((0, 0), (0, 1), (1, 0)) for e in range(DC)]
        if part == 0:
            pe.wait_ge(L["ctx_split"], n + 3)
            pe.wait_ge(L["k_full_ready"], n + 2)
        if part == 2:
            pe.wait_ge(L["v_drained"], n + 1)
        for a, b, e in terms:
            start, stop = (a, b, e) == terms[0], (a, b, e) == terms[-1]
            if part < 2:
                d = part
                last = pe.matmul(L.ps[:, 6, d * KEYS:(d + 1) * KEYS], wk[:, b, e, d * P:(d + 1) * P], x[:, a, e, :],
                                 start=start, stop=stop, skip_group_check=True)
            else:
                t = part - 2
                last = pe.matmul(L.ps[:, 7, t * D:(t + 1) * D], x[:, a, e, t * P:(t + 1) * P], wv[:, b, e, :],
                                 start=start, stop=stop, skip_group_check=True)
        if part % 2:
            last.then_inc(L["k_in_psum" if part == 1 else "v_in_psum"], 1)

    def pe_chunk_scores(self, pe, n, i, j, g, last_chunk):
        L, c, u = self.L, RING3[j], 4 * j + g
        if g == 0:
            pe.wait_ge(L["k_hi_ready"], n + 1)
        if self.masked:
            pe.wait_ge(L["unit_filled"], UNITS * i + u + 9)
        else:
            pe.wait_ge(L["unit_max_ready"], UNITS * i + u - units_since(u) + 5)
        for h in range(4 * g, 4 * g + 4):
            bank, at = 2 * BANKS[u] + h % 4 // 2, h % 2 * KEYS
            last = pe.matmul(L.ps[:, bank, at:at + KEYS], self.q_hi[:, h, :], self.k_halves[c][:, 0, h // HPB, :],
                             start=not self.masked, stop=not last_chunk, skip_group_check=True)
            if last_chunk:
                last = pe.matmul(L.ps[:, bank, at + P:at + KEYS], self.net.ident_bf[:, :],
                                 self.net.causal_bf[:, 0, :], start=False, stop=True, skip_group_check=True)
        last.then_inc(L["chunk_unit_scored"], 1)


    def pe_tile_scores(self, pe, i, j, half, masked_tile):
        L, c, n = self.L, RING4[j], BODY * i + j
        loads = 5 if self.masked else 3
        if half == 0:
            pe.wait_ge(L[f"group_loaded{c}"], 16 * loads * (uses(RING4, i, j) + 1))
        for v in range(2):
            u = 4 * j + 2 * half + v
            pe.wait_ge(L["unit_exp_ready"], UNITS * i + u - units_since(u) + 5)
            if masked_tile:
                for b in range(2):
                    pe.matmul(L.ps[:, 2 * BANKS[u] + b, :], self.net.ident_bf[:, :],
                              self.net.causal_T_bf[:, :, :].rearrange("p a b -> p (a b)"), start=True, stop=False,
                              skip_group_check=True)
            for k in range(4):
                pair = 4 * v + k
                last = pe.matmul(L.ps[:, 2 * BANKS[u] + k // 2, k % 2 * 2 * S:(k % 2 + 1) * 2 * S],
                                 self.k_packed[c][:, pair, half * P:(half + 1) * P],
                                 self.q_packed[:, 2 * pair:2 * pair + 2, :].rearrange("p h n -> p (h n)"),
                                 start=not masked_tile, stop=True, skip_group_check=True)
            last.then_inc(L["unit_scored"], 1)

    def pe_attend(self, pe, i, j, half):
        L, c, t = self.L, RING4[j], 2 * (BODY * i + j) + half
        if half == 0:
            pe.wait_ge(L[f"v_loaded{c}"], 16 * (uses(RING4, i, j) + 1))
        for h in range(H):
            if h % 8 == 0:
                pe.wait_ge(L["unit_exp_ready"], 2 * t + h // 8 + 5)
            q, col = h % 4 * 32, h // 4 * S
            last = pe.matmul(L.ps[q:q + DH + 1, 6, col:col + S], self.v_group[c][:, half, h, :],
                             self.p[half][:, h, :], start=False, stop=True, skip_group_check=True)
        last.then_inc(L["tile_attended"], 1)

    def tensor(self, pe):
        L = self.L
        self.norm.tensor(pe)
        self.net.wait_weights(pe, L.name)
        pe.sem_inc(L["v_in_psum"], 2)
        pe.sem_inc(L["unit_scored"], 12)
        pe.sem_inc(L["tile_attended"], 6)
        pe.sem_inc(L["chunk_unit_scored"], 8)
        self.pe_queries(pe)
        pe.wait_ge(L["w_halves_ready"], 2)
        for part in range(4):
            self.pe_keys_and_values(pe, 0, 0, part)
        pe.wait_ge(L["q_heads_ready"], 1)
        if self.masked:
            for bank in range(6):
                last = pe.matmul(L.ps[:, bank, :], self.net.zeros_bf[:, 0:P], self.net.zeros_bf[:, :], start=True,
                                 stop=True, skip_group_check=True)
            last.then_inc(L["banks_marked"], 1)

        def chunk_turn(i, last):
            for j in range(BODY):
                n = BODY * i + j
                final = last and j == BODY - 1
                for g in range(4):
                    if not final:
                        self.pe_keys_and_values(pe, n + 1, RING3[(j + 1) % BODY], g)
                    self.pe_chunk_scores(pe, n, i, j, g, final and self.causal)
        turns(pe, TURNS, chunk_turn)
        pe.wait_ge(L["minus_max_ready"], 3)
        pe.transpose(L.ps[0:3 * H, 0, 0:S], self.minus_max[:, :, :].rearrange("p a h -> p (a h)").bitcast(F32),
                     self.net.const("identity")).then_inc(L["minus_max_in_psum"], 1)
        pe.wait_ge(L["k_full_ready"], NCHUNK + 2)
        pe.matmul(L.ps[:, 6, :], self.net.zeros_bf[:, 0:P], self.net.zeros_bf[:, :], start=True, stop=True,
                  skip_group_check=True)
        pe.wait_ge(L["minus_max_drained"], 1)
        pe.wait_ge(L["k_packed_ones"], 4)
        pe.wait_ge(L["q_packed_ready"], 16 * (13 if self.masked else 12))
        pe.wait_ge(L["minus_max_loaded"], 16)
        self.pe_tile_scores(pe, 0, 0, 0, False)

        def tile_turn(i, last):
            for j in range(BODY):
                for half in range(2):
                    final = last and j == BODY - 1
                    if half == 0:
                        self.pe_tile_scores(pe, i, j, 1, self.causal and final)
                    elif not final:
                        carry, nxt = divmod(j + 1, BODY)
                        self.pe_tile_scores(pe, i + carry, nxt, 0, False)
                    self.pe_attend(pe, i, j, half)
        turns(pe, TURNS, tile_turn)
        pe.wait_ge(L["sums_ready"], 1)
        for i in range(4):
            last = pe.transpose(L.ps[:, 0, i * S:(i + 1) * S], self.sums[:, i, :], self.net.const("identity"))
        last.then_inc(L["sums_in_psum"], 1)
        self.attended.tensor(pe, L["o_ready"])
        self.attended.wait(pe)
        project(pe, L.ps[:, 2, 0:D], self.oT, self.w("Wo", c=DC), slice(0, D)).then_inc(L["y_in_psum"], 1)

    def act_fill(self, act, i, j):
        L, c = self.L, RING3[j]
        act.wait_ge(L[f"fill_loaded{c}"], 16 * (uses(RING3, i, j) + 1))
        for u in range(4 * j, 4 * j + 4):
            bank = 2 * BANKS[u]
            act.wait_ge(L["unit_max_ready"], UNITS * i + u - units_since(u) + 5)
            act.activation(L.ps[:, bank:bank + 2, :].rearrange("p b (h n) -> p (b h) n", h=2),
                           times(self.fill_chunk[c][:, :], 4), ACT.Copy).then_inc(L["unit_filled"], 1)

    def act_drain_k(self, act, n, i, j):
        L, c = self.L, RING3[j]
        act.wait_ge(L["k_lo_ready"], n + 1)
        act.wait_ge(L["chunk_unit_scored"], 4 * n + 4)
        act.wait_ge(L[f"k_stored{c}"], 16 * (uses(RING3, i, j) + 1))
        if self.masked:
            act.wait_ge(L["k_full_ready"], n + 3)
            act.activation(self.k_halves[c][:, 0, :, :], self.k_full[c][:, :, :], ACT.Copy)\
               .then_inc(L["k_hi_ready"], 1)
        else:
            act.wait_ge(L["k_in_psum"], n + 1)
            for d in range(DC):
                rounded = act.activation(self.k_halves[c][:, 0, d, :], L.ps[:, 6, d * KEYS:(d + 1) * KEYS],
                                         ACT.Identity, bias=self.w("bk")[:, d:d + 1])
            rounded.then_inc(L["k_hi_ready"], 1)
            for d in range(DC):
                full = act.activation(self.k_full[c][:, d, :], L.ps[:, 6, d * KEYS:(d + 1) * KEYS],
                                      ACT.Identity, bias=self.w("bk")[:, d:d + 1])
            full.then_inc(L["k_full_ready"], 1)

    def act_drain_v(self, act, n, i, j):
        L, c = self.L, RING3[j]
        act.wait_ge(L[f"v_stored{c}"], 16 * (uses(RING3, i, j) + 1))
        act.wait_ge(L["v_in_psum"], n + 3)
        act.activation(self.v_chunk[c][:, :, :, 0:DH].rearrange("p t h n -> p (t h) n"),
                       L.ps[:, 7, :].rearrange("p (m n) -> p m n", n=DH), ACT.Copy)\
           .then_inc(L["v_drained"], 1)

    def scalar(self, act):
        L = self.L
        for c in range(3):
            act.sem_inc(L[f"k_stored{c}"], 16)
            act.sem_inc(L[f"v_stored{c}"], 16)
        act.sem_inc(L["v_drained"], 1)
        if not self.masked:
            act.sem_inc(L["k_full_ready"], 2)
        act.sem_inc(L["unit_exp_ready"], 4)
        self.norm.scalar(act)
        self.net.wait_weights(act, L.name)
        if self.turned:
            act.wait_ge(L["turn_angles"], 1)
            act.activation(self.turn[:, 4:8], self.turn[:, 0:4], ACT.Sin).then_inc(L["sines_ready"], 1)
            act.wait_ge(L["gate_mean_ready"], 1)
            act.activation(self.turn[:, 9:10], self.turn[:, 8:9], ACT.Exp, scale=-1.0 / D)\
               .then_inc(L["gate_exp_ready"], 1)
        act.wait_ge(L["v_ones_ready"], 1)

        if self.masked:
            act.sem_inc(L["unit_filled"], 8)
            act.wait_ge(L["banks_marked"], 1)
            self.act_drain_k(act, 0, 0, 0)
            self.act_drain_v(act, 0, 0, 0)

        def chunk_turn(i, last):
            for j in range(BODY):
                if self.masked:
                    final = last and j == BODY - 1
                    carry, nxt = divmod(j + 1, BODY)
                    self.act_fill(act, i, j)
                    if not final:
                        self.act_drain_k(act, BODY * i + j + 1, i + carry, nxt)
                        self.act_drain_v(act, BODY * i + j + 1, i + carry, nxt)
                else:
                    self.act_drain_k(act, BODY * i + j, i, j)
                    self.act_drain_v(act, BODY * i + j, i, j)
        turns(act, TURNS, chunk_turn)
        act.wait_ge(L["minus_max_in_psum"], 1)
        act.activation(self.minus_max_T[:, :], L.ps[0:3 * H, 0, 0:S], ACT.Copy).then_inc(L["minus_max_drained"], 1)
        act.wait_ge(L["minus_max_drained"], 1)
        act.wait_ge(L["q_packed_cleared"], 1)
        act.dma_start(self.q_packed[96:99, :, :].bitcast(F32), self.minus_max_T[:, :])\
           .then_inc(L["minus_max_loaded"], 16)

        def tile_turn(i, last):
            for j in range(BODY):
                for half in range(2):
                    t = 2 * (BODY * i + j) + half
                    act.wait_ge(L["tile_attended"], t + 5)
                    for v in range(2):
                        bank = 2 * BANKS[4 * j + 2 * half + v]
                        act.wait_ge(L["unit_scored"], 2 * t + v + 13)
                        act.activation(self.p[half][:, 8 * v:8 * v + 8, :],
                                       L.ps[:, bank:bank + 2, :].rearrange("p b (h n) -> p (b h) n", h=4),
                                       ACT.Exp).then_inc(L["unit_exp_ready"], 1)
        turns(act, TURNS, tile_turn)
        self.attended.scalar(act)

    def gpsimd(self, pool):
        L, ones = self.L, self.net.const("ones")
        pool.sem_inc(L["ctx_split"], 2)
        pool.sem_inc(L["k_lo_ready"], 2)
        for c in range(3):
            last = pool.memset(self.v_chunk[c][:, :, :, DH:DH + 1], 1.0)
        last.then_inc(L["v_ones_ready"], 1)
        self.norm.gpsimd(pool)

        def split_context(n, i, j):
            c = RING3[j]
            hi, lo = self.ctx_halves[c][:, 0, :, :], self.ctx_halves[c][:, 1, :, :]
            pool.wait_ge(L[f"ctx_loaded{c}"], 16 * (uses(RING3, i, j) + 1))
            pool.wait_ge(L["v_in_psum"], n + 1)
            pool.tensor_tensor(hi, self.ctx_chunk[c][:, :, :], wide(ones[:, 0:DC], KEYS), ALU.mult)\
                .then_inc(L["ctx_hi_ready"], 1)
            pool.wait_ge(L["ctx_hi_ready"], n + 1)
            pool.tensor_tensor(lo, self.ctx_chunk[c][:, :, :], hi.bitcast(F32), ALU.subtract)\
                .then_inc(L["ctx_split"], 1)

        split_context(0, 0, 0)
        split_context(1, 0, 1)
        tail = slice(96, P)

        pool.wait_ge(L["ctx_split"], 4)
        pool.memset(self.q_packed[tail, :, :].bitcast(F32), 0.0).then_inc(L["q_packed_cleared"], 1)
        pool.wait_ge(L["q_packed_cleared"], 1)

        def chunk_turn(i, last):
            for j in range(BODY):
                n, c = BODY * i + j, RING3[j]
                carry, ahead = divmod(j + 2, BODY)
                if not (last and carry):
                    split_context(n + 2, i + carry, ahead)
                pool.wait_ge(L["k_full_ready"], n + 3)
                pool.wait_ge(L["k_hi_ready"], n + 1)
                pool.tensor_tensor(self.k_halves[c][:, 1, :, :], self.k_full[c][:, :, :],
                                   self.k_halves[c][:, 0, :, :].bitcast(F32), ALU.subtract)\
                    .then_inc(L["k_lo_ready"], 1)
        turns(pool, TURNS, chunk_turn)
        pool.wait_ge(L["k_lo_ready"], NCHUNK + 2)
        for c in range(4):
            pool.memset(self.k_packed[c][tail, :, :].bitcast(F32), 1.0).then_inc(L["k_packed_ones"], 1)
            pool.wait_ge(L["k_packed_ones"], c + 1)

    def dequantize(self, dve, o, w):
        scale, inverse = self.block_scale[:, 0, :], self.block_scale[:, 1, :]
        o.after(dve.tensor_reduce(scale, w, AX_X, ALU.max, apply_absolute_value=True))
        o.after(dve.tensor_scalar(scale, scale, 1.0 / 7.0, 1e-12, ALU.mult, ALU.max))
        o.after(dve.reciprocal(inverse, scale))
        o.after(dve.tensor_tensor(w, w, wide(inverse, 32), ALU.mult))
        o.after(dve.tensor_scalar(w, w, ROUND, -ROUND, ALU.add, ALU.add))
        o.after(dve.tensor_scalar(w, w, -8.0, 7.0, ALU.max, ALU.min))
        dve.tensor_tensor(w, w, wide(scale, 32), ALU.mult).then_inc(self.L["piece_ready"], 1)

    def turn_angles(self, dve, o):
        L, tn, net = self.L, self.turn, self.net
        two_pi = 2.0 * np.pi
        hi = float(np.float32(6.28125))
        mid = float(np.float32(two_pi - hi))
        lo = float(two_pi - hi - mid)
        theta = self.w("theta")
        dve.tensor_reduce(tn[:, 8:9], self.w("gate"), AX_X, ALU.add).then_inc(L["gate_mean_ready"], 1)
        for k, quarter in ((0, 0.0), (2, 0.25)):
            o.after(dve.tensor_scalar(tn[:, 12 + k:14 + k], theta, 1.0 / two_pi, quarter, ALU.mult, ALU.add))
            o.after(dve.tensor_scalar(tn[:, 12 + k:14 + k], tn[:, 12 + k:14 + k], ROUND, -ROUND, ALU.add, ALU.add))
            o.after(dve.tensor_scalar(tn[:, k:k + 2], tn[:, 12 + k:14 + k], -hi, None, ALU.mult))
            o.after(dve.tensor_tensor(tn[:, k:k + 2], tn[:, k:k + 2], theta, ALU.add))
            for part in (-mid, -lo):
                o.after(dve.tensor_scalar(tn[:, 16:18], tn[:, 12 + k:14 + k], part, None, ALU.mult))
                o.after(dve.tensor_tensor(tn[:, k:k + 2], tn[:, k:k + 2], tn[:, 16:18], ALU.add))
            if k:
                o.after(dve.tensor_scalar(tn[:, 2:4], tn[:, 2:4], float(np.pi / 2), None, ALU.add))
        dve.tensor_scalar(tn[:, 0:4], tn[:, 0:4], 3.1415925, -3.1415925, ALU.min, ALU.max)\
           .then_inc(L["turn_angles"], 1)

    def turn_factors(self, dve, o):
        L, tn, net = self.L, self.turn, self.net
        dve.wait_ge(L["gate_exp_ready"], 1)
        o.after(dve.tensor_scalar(tn[:, 10:11], tn[:, 9:10], 1.0, None, ALU.add))
        o.after(dve.reciprocal(tn[:, 10:11], tn[:, 10:11]))
        dve.wait_ge(L["sines_ready"], 1)
        o.after(dve.tensor_scalar(tn[:, 20:22], tn[:, 4:6], tn[:, 10:11], net.const("turn_sign"), ALU.mult, ALU.mult))
        o.after(dve.tensor_scalar(tn[:, 22:24], tn[:, 6:8], -1.0, tn[:, 10:11], ALU.add, ALU.mult))
        o.after(dve.tensor_scalar(tn[:, 22:24], tn[:, 22:24], net.const("turned"), 1.0, ALU.mult, ALU.add))

    def turn_queries(self, dve, o):
        tn = self.turn
        for c in range(DC):
            o.after(dve.tensor_scalar(self.qT_swapped[:, c, :], self.qT_swapped[:, c, :], tn[:, 20 + c:21 + c], None,
                                      ALU.mult))
            o.after(dve.scalar_tensor_tensor(self.qT[:, c, :], self.qT[:, c, :], tn[:, 22 + c:23 + c],
                                             self.qT_swapped[:, c, :], ALU.mult, ALU.add))

    def vector(self, dve):
        L, net = self.L, self.net
        dve.sem_inc(L["unit_max_ready"], 4)
        if self.masked:
            dve.sem_inc(L["k_full_ready"], 2)
            dve.wait_ge(L["mask_u8_loaded"], 16)
            dve.tensor_scalar(self.mask_rows[:, 0, :], self.mask_u8[:, :], 0.0, None, ALU.add)\
               .then_inc(L["mask_rows_ready"], 1)
            dve.tensor_scalar(self.mask_rows[:, 1, :], self.mask_u8[:, :], -1.0, None, ALU.add)\
               .then_inc(L["mask_rows_ready"], 1)
            dve.tensor_scalar(self.mask_rows[:, 2, :], self.mask_u8[:, :], -1.0, 1e8, ALU.add, ALU.mult)\
               .then_inc(L["mask_rows_ready"], 1)
        self.norm.vector(dve)
        self.net.wait_weights(dve, L.name)
        o = L.order(dve, "mid_dve")
        if self.turned:
            self.turn_angles(dve, o)
        for halves, name in zip(self.w_halves, ("Wk", "Wv")):
            o.after(dve.tensor_copy(halves[:, 0, :, :], self.w(name, c=DC)))
            dve.tensor_tensor(halves[:, 1, :, :], self.w(name, c=DC), halves[:, 0, :, :].bitcast(F32), ALU.subtract)\
               .then_inc(L["w_halves_ready"], 1)
        o.after(dve.memset(self.row_max[:, 0, :], -LARGEST))
        if self.turned:
            self.turn_factors(dve, o)
        dve.wait_ge(L["q_in_psum"], 1)
        for c in range(DC):
            o.after(dve.tensor_scalar(self.qT[:, c, :], L.ps[:, 0, c * S:(c + 1) * S], self.w("bq")[:, c:c + 1],
                                      DH ** -0.5, ALU.add, ALU.mult))
        if self.turned:
            for c in range(DC):
                o.after(dve.tensor_scalar(self.qT_swapped[:, c, :], L.ps[:, 1, c * S:(c + 1) * S],
                                          self.w("bq_swapped")[:, c:c + 1], DH ** -0.5, ALU.add, ALU.mult))
            self.turn_queries(dve, o)
        o.after(dve.tensor_copy(self.qT_halves[:, 0, :, :], self.qT[:, :, :]))
        o.after(dve.tensor_tensor(self.qT_halves[:, 1, :, :], self.qT[:, :, :],
                                  self.qT_halves[:, 0, :, :].bitcast(F32), ALU.subtract))
        for half, q in enumerate((self.q_hi, self.q_lo)):
            for c in range(DC):
                last = dve.tensor_tensor(q[:, c * HPB:(c + 1) * HPB, :],
                                         times(self.qT_halves[:, half, c, :].bitcast(F32), HPB),
                                         wide(net.const("head16"), S), ALU.mult)
            last.then_inc(L["q_heads_ready"], 1)

        def masked_keys(n, i, j):
            c = RING3[j]
            dve.wait_ge(L["k_in_psum"], n + 1)
            dve.wait_ge(L["k_lo_ready"], n + 1)
            dve.wait_ge(L[f"mask_loaded{c}"], 16 * (uses(RING3, i, j) + 1))
            for d in range(DC):
                last = dve.scalar_tensor_tensor(self.k_full[c][:, d, :], L.ps[:, 6, d * KEYS:(d + 1) * KEYS],
                                                self.w("bk")[:, d:d + 1], self.mask_chunk[c][:, :], ALU.add, ALU.mult)
            last.then_inc(L["k_full_ready"], 1)

        if self.masked:
            masked_keys(0, 0, 0)

        def chunk_turn(i, last):
            for j in range(BODY):
                n = BODY * i + j
                for g in range(4):
                    if self.masked and g == 1 and not (last and j == BODY - 1):
                        carry, nxt = divmod(j + 1, BODY)
                        masked_keys(n + 1, i + carry, nxt)
                    b = 2 * BANKS[4 * j + g]
                    dve.wait_ge(L["chunk_unit_scored"], 4 * n + g + 9)
                    dve.tensor_reduce(self.turn_max[:, j, 4 * g:4 * g + 4],
                                      L.ps[:, b:b + 2, :].rearrange("p b (h n) -> p (b h) n", h=2), AX_X,
                                      ALU.max).then_inc(L["unit_max_ready"], 1)
            dve.wait_ge(L["unit_max_ready"], UNITS * (i + 1) + 4)
            dve.tensor_reduce(self.row_max[:, 1, :], self.turn_max[:, :, :].rearrange("p j h -> p h j"), AX_X,
                              ALU.max).then_inc(L["row_max_ready"], 1)
            dve.wait_ge(L["row_max_ready"], 2 * i + 1)
            dve.tensor_tensor(self.row_max[:, 0, :], self.row_max[:, 0, :], self.row_max[:, 1, :], ALU.max)\
               .then_inc(L["row_max_ready"], 1)
            dve.wait_ge(L["row_max_ready"], 2 * i + 2)
        turns(dve, TURNS, chunk_turn)
        most, rest = self.row_max[:, 0, :], self.row_max[:, 1, :]
        o.after(dve.tensor_scalar(most, most, -1.0, None, ALU.mult))
        for k in range(3):
            part = self.minus_max[:, k, :]
            dve.tensor_copy(part, most if k == 0 else rest).then_inc(L["minus_max_ready"], 1)
            dve.wait_ge(L["minus_max_ready"], k + 1)
            if k < 2:
                o.after(dve.tensor_tensor(rest, most if k == 0 else rest, part.bitcast(F32), ALU.subtract))
        if self.dequantizing:
            for k in range(self.PIECES):
                dve.wait_ge(L[f"piece_loaded{k}"], 16)
                if k:
                    dve.wait_ge(L["piece_ready"], k)
                self.dequantize(dve, o, self.pieces[k].rearrange("p (b n) -> p b n", n=32))
            dve.wait_ge(L["pieces_stored"], 16 * self.PIECES)
        dve.wait_ge(L["tile_attended"], NT + 6)
        dve.tensor_copy(self.sums[:, :, :], L.ps[:, 6, :].rearrange("p (i n) -> p i n", i=4))\
           .then_inc(L["sums_ready"], 1)
        dve.wait_ge(L["sums_in_psum"], 1)
        sums = L.ps[:, 0, :].rearrange("p (h n) -> p h n", n=32)
        o.after(dve.reciprocal(self.rden[:, :], sums[:, :, DH]))
        o.after(dve.tensor_tensor(self.o[:, :].rearrange("p (h n) -> p h n", n=DH), sums[:, :, 0:DH],
                                  wide(self.rden[:, :], DH), ALU.mult))
        dve.tensor_tensor(self.o[:, :], self.o[:, :], self.w("bv"), ALU.add).then_inc(L["o_ready"], 1)
        o.after(dve.tensor_tensor(net.x[:, :], net.x[:, :], self.w("bo"), ALU.add))
        dve.wait_ge(L["y_in_psum"], 1)
        o.after(dve.tensor_tensor(net.x[:, :], net.x[:, :], L.ps[:, 2, 0:D], ALU.add))





class LatentAttention:

    RANK = 64

    def __init__(self, L):
        self.L, self.net, self.norm = L, L.net, NormRows(L)
        sb = L.sb
        self.qT, self.kT = sb("qT", [P, DC, S]), sb("kT", [P, DC, S])
        self.turned_part = sb("turned_part", [P, DC, S])
        self.lat = sb("lat", [S, self.RANK])
        self.latT = sb("latT", [self.RANK, S])
        self.lat_stats = sb("lat_stats", [S, 12])
        self.v, self.o = sb("v", [S, D]), sb("o", [S, D])
        self.oT = sb("oT", [P, DC, S])
        self.att = SelfAttention(L, DH, DH ** -0.5, True, 2, self.kT, self.v, self.o)
        self.attended = Transposed(L, "oT", self.o, DC, self.oT, 5)

    def w(self, name, **split):
        return self.net.w(self.L.name, name, **split)

    def sync(self, sp):
        self.net.load_weights(sp, LAYERS.index(self.L.name) + 1)

    def tensor(self, pe):
        L, xnT, n = self.L, self.norm.xnT, self.RANK
        self.norm.tensor(pe)
        self.net.wait_weights(pe, L.name)
        pe.wait_ge(L["xnT_ready"], 1)
        project(pe, L.ps[:, 0, 0:n], xnT, self.w("W_dkv", c=DC), slice(0, n)).then_inc(L["lat_in_psum"], 1)
        for bank, name in ((1, "W_q"), (2, "W_q_swapped")):
            for c in range(DC):
                last = project_T(pe, L.ps[:, bank, c * S:(c + 1) * S], xnT, self.w(name, c=DC),
                                 slice(c * P, (c + 1) * P))
            last.then_inc(L["q_in_psum"], 1)
        pe.wait_ge(L["lat_ready"], 1)
        pe.transpose(L.ps[0:n, 3, 0:S], self.lat[:, :], self.net.const("identity")).then_inc(L["latT_in_psum"], 1)
        pe.wait_ge(L["latT_ready"], 1)
        for bank, name in ((4, "W_uk"), (5, "W_uk_swapped")):
            for c in range(DC):
                last = pe.matmul(L.ps[:, bank, c * S:(c + 1) * S], self.w(name)[0:n, c * P:(c + 1) * P],
                                 self.latT[:, :], start=c == 0, stop=c == 1, skip_group_check=True)
            last.then_inc(L["k_in_psum"], 1)
        pe.matmul(L.ps[:, 6, 0:D], self.latT[:, :], self.w("W_uv")[0:n, :], start=True, stop=True)\
          .then_inc(L["v_in_psum"], 1)
        pe.wait_ge(L["qk_ready"], 2)
        pe.wait_ge(L["v_ready"], 1)
        self.att.tensor(pe)
        self.attended.tensor(pe, L["attended"], self.att.units)
        self.attended.wait(pe)
        project(pe, L.ps[:, 6, 0:D], self.oT, self.w("W_o", c=DC), slice(0, D)).then_inc(L["y_in_psum"], 1)

    def scalar(self, act):
        L = self.L
        self.norm.scalar(act)
        act.wait_ge(L["latT_in_psum"], 1)
        act.activation(self.latT[:, :], L.ps[0:self.RANK, 3, 0:S], ACT.Copy).then_inc(L["latT_ready"], 1)
        act.wait_ge(L["v_in_psum"], 1)
        act.activation(self.v[:, :], L.ps[:, 6, 0:D], ACT.Copy).then_inc(L["v_ready"], 1)
        self.att.scalar(act)
        self.attended.scalar(act)

    def gpsimd(self, pool):
        L, st = self.L, self.lat_stats
        self.norm.gpsimd(pool)
        pool.wait_ge(L["lat_var_ready"], 1)
        pool.tensor_scalar(st[:, 8:9], st[:, 7:8], 1e-5, None, ALU.add).then_inc(L["lat_rstd_ready"], 1)
        pool.wait_ge(L["lat_rstd_ready"], 1)
        pool.tensor_tensor(st[:, 9:10], st[:, 8:9], self.net.const("neg_half"), ALU.pow)\
            .then_inc(L["lat_rstd_ready"], 1)

    def rotate(self, dve, o, out, banks):
        ps, net = self.L.ps, self.net
        straight = ps[:, banks[0], 0:DC * S].rearrange("p (c n) -> p c n", c=DC)
        swapped = ps[:, banks[1], 0:DC * S].rearrange("p (c n) -> p c n", c=DC)
        o.after(dve.tensor_tensor(self.turned_part[:, :, :], swapped, times(net.const("rope_sin"), DC), ALU.mult))
        o.after(dve.tensor_tensor(out[:, :, :], straight, times(net.const("rope_cos"), DC), ALU.mult))
        return dve.tensor_tensor(out[:, :, :], out[:, :, :], self.turned_part[:, :, :], ALU.add)

    def vector(self, dve):
        L, net, st = self.L, self.net, self.lat_stats
        self.norm.vector(dve)
        net.wait_weights(dve, L.name)
        o = L.order(dve, "latent_dve")
        dve.wait_ge(L["lat_in_psum"], 1)
        o.after(dve.tensor_copy(self.lat[:, :], L.ps[:, 0, 0:self.RANK]))
        o.after(dve.bn_stats(st[:, 0:6], self.lat[:, :]))
        dve.bn_aggr(st[:, 6:8], st[:, 0:6]).then_inc(L["lat_var_ready"], 1)
        dve.wait_ge(L["lat_rstd_ready"], 2)
        o.after(dve.tensor_scalar(self.lat[:, :], self.lat[:, :], st[:, 6:7], st[:, 9:10], ALU.subtract, ALU.mult))
        o.after(dve.tensor_tensor(self.lat[:, :], self.lat[:, :], self.w("ln_gamma"), ALU.mult))
        dve.tensor_tensor(self.lat[:, :], self.lat[:, :], self.w("ln_beta"), ALU.add).then_inc(L["lat_ready"], 1)
        dve.wait_ge(L["q_in_psum"], 2)
        self.rotate(dve, o, self.qT, (1, 2)).then_inc(L["qk_ready"], 1)
        dve.wait_ge(L["qk_ready"], 1)
        for u in range(2):
            self.att.spread_vector(dve, u, self.qT)
        dve.wait_ge(L["k_in_psum"], 2)
        self.rotate(dve, o, self.kT, (4, 5)).then_inc(L["qk_ready"], 1)
        self.att.vector(dve, self.qT)
        dve.wait_ge(L["y_in_psum"], 1)
        o.after(dve.tensor_tensor(net.x[:, :], net.x[:, :], L.ps[:, 6, 0:D], ALU.add))


class CausalAttention:

    def __init__(self, L):
        self.L, self.net, self.norm = L, L.net, NormRows(L)
        sb = L.sb
        self.qT, self.kT = sb("qT", [P, DC, S]), sb("kT", [P, DC, S])
        self.v, self.o = sb("v", [S, D]), sb("o", [S, D])
        self.oT = sb("oT", [P, DC, S])
        self.att = SelfAttention(L, DH, DH ** -0.5, True, 2, self.kT, self.v, self.o)
        self.attended = Transposed(L, "oT", self.o, DC, self.oT, 5)

    def w(self, name, **split):
        return self.net.w(self.L.name, name, **split)

    def sync(self, sp):
        self.net.load_weights(sp, LAYERS.index(self.L.name) + 1)

    def gpsimd(self, pool):
        self.norm.gpsimd(pool)

    def tensor(self, pe):
        L, xnT = self.L, self.norm.xnT
        self.norm.tensor(pe)
        self.net.wait_weights(pe, L.name)
        pe.wait_ge(L["xnT_ready"], 1)
        for part in range(2):
            for c in range(DC):
                at = part * D + c * P
                last = project_T(pe, L.ps[:, 4 + part, c * S:(c + 1) * S], xnT, self.w("Wqk", c=DC),
                                 slice(at, at + P))
            last.then_inc(L["qk_in_psum"], 1)
        project(pe, L.ps[:, 6, 0:D], xnT, self.w("Wv", c=DC), slice(0, D)).then_inc(L["v_in_psum"], 1)
        pe.wait_ge(L["kT_ready"], DC)
        pe.wait_ge(L["v_ready"], 1)
        self.att.tensor(pe)
        self.attended.tensor(pe, L["attended"], self.att.units)
        self.attended.wait(pe)
        project(pe, L.ps[:, 6, 0:D], self.oT, self.w("Wout", c=DC), slice(0, D)).then_inc(L["y_in_psum"], 1)

    def scalar(self, act):
        L = self.L
        self.norm.scalar(act)
        self.net.wait_weights(act, L.name)
        act.wait_ge(L["qk_in_psum"], 2)
        for c in range(DC):
            act.activation(self.kT[:, c, :], L.ps[:, 5, c * S:(c + 1) * S], ACT.Identity,
                           bias=self.w("bqk")[:, DC + c:DC + c + 1]).then_inc(L["kT_ready"], 1)
        self.att.scalar(act)
        self.attended.scalar(act)

    def vector(self, dve):
        L, net = self.L, self.net
        self.norm.vector(dve)
        net.wait_weights(dve, L.name)
        o = L.order(dve, "latent_dve")
        dve.wait_ge(L["qk_in_psum"], 1)
        for c in range(DC):
            o.after(dve.tensor_scalar(self.qT[:, c, :], L.ps[:, 4, c * S:(c + 1) * S], self.w("bqk")[:, c:c + 1],
                                      None, ALU.add))
        for u in range(2):
            self.att.spread_vector(dve, u, self.qT)
        dve.wait_ge(L["v_in_psum"], 1)
        dve.tensor_tensor(self.v[:, :], L.ps[:, 6, 0:D], self.w("bv"), ALU.add).then_inc(L["v_ready"], 1)
        self.att.vector(dve, self.qT)
        dve.wait_ge(L["y_in_psum"], 1)
        o.after(dve.tensor_tensor(net.x[:, :], net.x[:, :], L.ps[:, 6, 0:D], ALU.add))
        o.after(dve.tensor_tensor(net.x[:, :], net.x[:, :], self.w("bout"), ALU.add))


class WideAttention:

    HEADS, WIDTH = 32, 32
    INNER = HEADS * WIDTH
    IC = INNER // P

    def __init__(self, L):
        self.L, self.net, self.norm = L, L.net, NormRows(L)
        sb, IC = L.sb, self.IC
        self.qT, self.kT = sb("qT", [P, IC, S]), sb("kT", [P, IC, S])
        self.v = sb("v", [S, self.INNER])
        self.oT = sb("oT", [P, IC, S])
        self.y = sb("y", [S, D])
        self.y_stats = sb("y_stats", [S, 12])
        self.att = TransposedSelfAttention(L, self.WIDTH, self.WIDTH ** -0.5, False, 4, self.kT, self.v, self.oT)

    def w(self, name, **split):
        return self.net.w(self.L.name, name, **split)

    def sync(self, sp):
        self.net.load_weights(sp, LAYERS.index(self.L.name) + 1)

    def gpsimd(self, pool):
        L, st = self.L, self.y_stats
        self.norm.gpsimd(pool)
        pool.wait_ge(L["y_var_ready"], 1)
        pool.tensor_scalar(st[:, 8:9], st[:, 7:8], 1e-6, None, ALU.add).then_inc(L["y_rstd_ready"], 1)
        pool.wait_ge(L["y_rstd_ready"], 1)
        pool.tensor_tensor(st[:, 9:10], st[:, 8:9], self.net.const("neg_half"), ALU.pow)\
            .then_inc(L["y_rstd_ready"], 1)

    def tensor(self, pe):
        L, xnT, IC = self.L, self.norm.xnT, self.IC
        qkv = self.w("w_qkv", c=DC)
        self.norm.tensor(pe)
        self.net.wait_weights(pe, L.name)
        pe.wait_ge(L["xnT_ready"], 1)
        for bank in range(2 * IC // 4):
            for c in range(4):
                at = (bank * 4 + c) * P
                last = project_T(pe, L.ps[:, bank, c * S:(c + 1) * S], xnT, qkv, slice(at, at + P))
            last.then_inc(L["qk_in_psum"], 1)
        for b in range(2):
            at = 2 * self.INNER + b * BANK
            project(pe, L.ps[:, 4 + b, :], xnT, qkv, slice(at, at + BANK)).then_inc(L["v_in_psum"], 1)
        pe.wait_ge(L["qk_ready"], 4)
        pe.wait_ge(L["v_ready"], 2)
        self.att.tensor(pe)
        pe.wait_ge(L["attended"], self.att.units)
        project(pe, L.ps[:, 6, 0:D], self.oT, self.w("w_out", c=IC), slice(0, D)).then_inc(L["y_in_psum"], 1)

    def scalar(self, act):
        L = self.L
        self.norm.scalar(act)
        for b in (0, 2):
            act.wait_ge(L["qk_in_psum"], b + 1)
            dst = self.qT if b == 0 else self.kT
            act.activation(dst[:, 0:4, :], L.ps[:, b, :].rearrange("p (c n) -> p c n", c=4), ACT.Copy)\
               .then_inc(L["qk_ready"], 1)
        act.wait_ge(L["v_in_psum"], 1)
        act.activation(self.v[:, 0:BANK], L.ps[:, 4, :], ACT.Copy).then_inc(L["v_ready"], 1)
        self.att.scalar(act)

    def vector(self, dve):
        L, net, st = self.L, self.net, self.y_stats
        self.norm.vector(dve)
        for b in (1, 3):
            dve.wait_ge(L["qk_in_psum"], b + 1)
            dst = self.qT if b == 1 else self.kT
            dve.tensor_copy(dst[:, 4:8, :], L.ps[:, b, :].rearrange("p (c n) -> p c n", c=4)).then_inc(L["qk_ready"], 1)
        dve.wait_ge(L["v_in_psum"], 2)
        dve.tensor_copy(self.v[:, BANK:2 * BANK], L.ps[:, 5, :]).then_inc(L["v_ready"], 1)
        dve.wait_ge(L["qk_ready"], 4)
        for u in range(2):
            self.att.spread_vector(dve, u, self.qT)
        self.att.vector(dve, self.qT)
        net.wait_weights(dve, L.name)
        o = L.order(dve, "latent_dve")
        dve.wait_ge(L["y_in_psum"], 1)
        o.after(dve.tensor_tensor(self.y[:, :], L.ps[:, 6, 0:D], self.w("b_out"), ALU.add))
        o.after(dve.bn_stats(st[:, 0:6], self.y[:, :]))
        dve.bn_aggr(st[:, 6:8], st[:, 0:6]).then_inc(L["y_var_ready"], 1)
        dve.wait_ge(L["y_rstd_ready"], 2)
        o.after(dve.tensor_scalar(self.y[:, :], self.y[:, :], st[:, 6:7], st[:, 9:10], ALU.subtract, ALU.mult))
        o.after(dve.tensor_tensor(self.y[:, :], self.y[:, :], self.w("ln_gamma"), ALU.mult))
        o.after(dve.tensor_tensor(self.y[:, :], self.y[:, :], self.w("ln_beta"), ALU.add))
        o.after(dve.tensor_tensor(net.x[:, :], net.x[:, :], self.y[:, :], ALU.add))




class QuantizedGatedLayer:

    I = 768
    IC = I // P

    def __init__(self, L):
        self.L, self.net, self.norm = L, L.net, NormRows(L)
        sb, I = L.sb, self.I
        self.turned = {"w_gate": sb("w_gateT", [P, DC, I]), "w_up": sb("w_upT", [P, DC, I]),
                       "w_down": sb("w_downT", [P, self.IC, D])}
        self.xq = sb("xq", [S, D])
        self.xqT = sb("xqT", [P, DC, S])
        self.up, self.gate, self.sig = sb("up", [S, I]), sb("gate", [S, I]), sb("sig", [S, I])
        self.oT = sb("oT", [P, self.IC, S])
        self.scales = sb("scales", [P, 5, 4])
        self.x_turned = Transposed(L, "xqT", self.xq, DC, self.xqT, 0)
        self.o_turned = Transposed(L, "oT", self.gate, self.IC, self.oT, 4)

    SHAPES = (("w_gate", 6), ("w_up", 6), ("w_down", 2))

    def sync(self, sp):
        self.net.load_weights(sp, LAYERS.index(self.L.name) + 1)

    def tensor(self, pe):
        L = self.L
        self.net.wait_weights(pe, L.name)
        n = 0
        for name, row_blocks in self.SHAPES:
            w = self.net.w(L.name, name, c=row_blocks)
            for k in range(3):
                if n >= 8:
                    pe.wait_ge(L["w_turned"], n - 7)
                for j in range(4):
                    r, c = self.block(name, 4 * k + j)
                    last = pe.transpose(L.ps[:, n % 8, j * P:(j + 1) * P], w[:, r, c * P:(c + 1) * P],
                                        self.net.const("identity"))
                last.then_inc(L["w_in_psum"], 1)
                n += 1
        pe.wait_ge(L["w_turned"], 9)
        self.x_turned.tensor(pe, L["quantized"], 1)
        self.x_turned.wait(pe)
        for bank, name in ((2, "w_up"), (4, "w_gate")):
            project(pe, L.ps[:, bank, :], self.xqT, self.turned[name], slice(0, BANK))
            project(pe, L.ps[:, bank + 1, 0:self.I - BANK], self.xqT, self.turned[name], slice(BANK, self.I))\
                .then_inc(L["up_gate_in_psum"], 1)
        self.o_turned.tensor(pe, L["quantized"], 5)
        self.o_turned.wait(pe)
        project(pe, L.ps[:, 6, 0:D], self.oT, self.turned["w_down"], slice(0, D)).then_inc(L["y_in_psum"], 1)

    def block(self, name, k):
        if name == "w_down":
            return k % 2, k // 2
        return k % 6, k // 6

    def scalar(self, act):
        L = self.L
        n = 0
        for name, _ in self.SHAPES:
            dst = self.turned[name][:, :, :].rearrange("p c n -> p (c n)")
            for k in range(3):
                act.wait_ge(L["w_in_psum"], n + 1)
                act.activation(dst[:, k * BANK:(k + 1) * BANK], L.ps[:, n % 8, :], ACT.Copy)\
                   .then_inc(L["w_turned"], 1)
                n += 1
        self.x_turned.scalar(act)
        act.wait_ge(L["quantized"], 3)
        act.activation(self.sig[:, :], self.gate[:, :], ACT.Sigmoid).then_inc(L["sigmoid_ready"], 1)
        self.o_turned.scalar(act)

    def gpsimd(self, pool):
        L = self.L
        self.norm.gpsimd(pool)
        for k in range(5):
            pool.wait_ge(L["row_absmax_ready"], k + 1)
            pool.partition_all_reduce(self.scales[:, k, 1:2], self.scales[:, k, 0:1], P, ABSMAX)\
                .then_inc(L["absmax_ready"], 1)

    def quantize(self, dve, o, k, out, src):
        L, sc = self.L, self.scales
        dve.tensor_reduce(sc[:, k, 0:1], src, AX_X, ALU.max, apply_absolute_value=True)\
           .then_inc(L["row_absmax_ready"], 1)
        dve.wait_ge(L["absmax_ready"], k + 1)
        o.after(dve.tensor_scalar(sc[:, k, 2:3], sc[:, k, 1:2], 1.0 / 32767.0, 1e-12, ALU.mult, ALU.max))
        o.after(dve.reciprocal(sc[:, k, 3:4], sc[:, k, 2:3]))
        o.after(dve.tensor_scalar(out, src, sc[:, k, 3:4], ROUND, ALU.mult, ALU.add))
        o.after(dve.tensor_scalar(out, out, -ROUND, -32768.0, ALU.add, ALU.max))
        dve.tensor_scalar(out, out, 32767.0, sc[:, k, 2:3], ALU.min, ALU.mult).then_inc(L["quantized"], 1)

    def vector(self, dve):
        L, net, I = self.L, self.net, self.I
        o = L.order(dve, "gated_dve")
        self.norm_rows(dve)
        self.quantize(dve, o, 0, self.xq[:, :], self.norm.xn[:, :])
        for k, dst in ((1, self.up), (2, self.gate)):
            dve.wait_ge(L["up_gate_in_psum"], k)
            src = L.ps[:, 2 * k:2 * k + 2, :].rearrange("p b n -> p (b n)")[:, 0:I]
            self.quantize(dve, o, k, dst[:, :], src)
        dve.wait_ge(L["sigmoid_ready"], 1)
        sig = self.sig[:, :]
        o.after(dve.tensor_scalar(sig, sig, 65536.0, ROUND, ALU.mult, ALU.add))
        o.after(dve.tensor_scalar(sig, sig, -ROUND, 0.0, ALU.add, ALU.max))
        o.after(dve.tensor_scalar(sig, sig, 65535.0, 1.0 / 65536.0, ALU.min, ALU.mult))
        o.after(dve.tensor_tensor(self.gate[:, :], self.gate[:, :], sig, ALU.mult))
        self.quantize(dve, o, 3, self.gate[:, :], self.gate[:, :])
        dve.wait_ge(L["quantized"], 4)
        o.after(dve.tensor_tensor(self.gate[:, :], self.gate[:, :], self.up[:, :], ALU.mult))
        self.quantize(dve, o, 4, self.gate[:, :], self.gate[:, :])
        dve.wait_ge(L["y_in_psum"], 1)
        o.after(dve.tensor_tensor(net.x[:, :], net.x[:, :], L.ps[:, 6, 0:D], ALU.add))

    def norm_rows(self, dve):
        self.norm.vector(dve)
        dve.wait_ge(self.L["xn_ready"], 1)


class ExpertLayer:

    E, HID = 8, 1024
    HC = HID // P

    def __init__(self, L):
        self.L, self.net, self.norm = L, L.net, NormRows(L)
        sb, E = L.sb, self.E
        self.W1 = sb("W1", [P, E, DC, self.HID])
        self.W2 = sb("W2", [P, E, self.HC, D])
        self.hT = [sb(f"hT{c}", [P, self.HC, S]) for c in range(2)]
        self.route = sb("route", [S, 8, E])
        self.col = sb("col", [S, 4])
        self.route_T = sb("route_T", [E, S])

    def sync(self, sp):
        L, E, ins = self.L, self.E, self.net.ins
        w1 = ins["experts_W1"].rearrange("e (c p) n -> p e c n", p=P)
        w2 = ins["experts_W2"].rearrange("e (c p) n -> p e c n", p=P)
        for e in range(E):
            sp.dma_start(self.W1[:, e, :, :], w1[:, e, :, :]).then_inc(L[f"W1_loaded{e}"], 16)
            sp.dma_start(self.W2[:, e, :, :], w2[:, e, :, :]).then_inc(L[f"W2_loaded{e}"], 16)
        self.net.load_weights(sp, LAYERS.index(L.name) + 1)

    def gpsimd(self, pool):
        self.norm.gpsimd(pool)

    def tensor(self, pe):
        L, xnT, E = self.L, self.norm.xnT, self.E
        self.norm.tensor(pe)
        self.net.wait_weights(pe, L.name)
        pe.wait_ge(L["xnT_ready"], 1)
        project(pe, L.ps[:, 6, 0:E], xnT, self.net.w(L.name, "Wr", c=DC), slice(0, E)).then_inc(L["logits_in_psum"], 1)

        def hidden(e):
            pe.wait_ge(L[f"W1_loaded{e}"], 16)
            if e >= 2:
                pe.wait_ge(L["hidden_ready"], (e - 1) * self.HC)
            for b in range(self.HC):
                last = project_T(pe, L.ps[:, e % 2 * 2 + b // 4, b % 4 * S:(b % 4 + 1) * S], xnT,
                                 self.W1[:, e, :, :], slice(b * P, (b + 1) * P))
                if b % 4 == 3:
                    last.then_inc(L["hidden_in_psum"], 1)

        def output(e):
            pe.wait_ge(L[f"W2_loaded{e}"], 16)
            pe.wait_ge(L["hidden_ready"], (e + 1) * self.HC)
            if e >= 2:
                pe.wait_ge(L["expert_added"], e - 1)
            project(pe, L.ps[:, 4 + e % 2, 0:D], self.hT[e % 2], self.W2[:, e, :, :], slice(0, D))\
                .then_inc(L["expert_in_psum"], 1)

        hidden(0)
        pe.wait_ge(L["route_ready"], 1)
        pe.transpose(L.ps[0:E, 7, 0:S], self.route[:, 3, :], self.net.const("identity"))\
          .then_inc(L["route_T_in_psum"], 1)
        pe.wait_ge(L["route_T_ready"], 1)
        pe.matmul(L.ps[:, 6, 0:D], self.route_T[:, :], self.net.w(L.name, "b2")[0:E, :], start=True, stop=True)\
          .then_inc(L["b2_in_psum"], 1)
        for e in range(E):
            if e + 1 < E:
                hidden(e + 1)
            output(e)

    def scalar(self, act):
        L, E = self.L, self.E
        self.norm.scalar(act)
        self.net.wait_weights(act, L.name)
        act.wait_ge(L["logits_centred"], 1)
        act.activation(self.route[:, 3, :], self.route[:, 3, :], ACT.Exp).then_inc(L["route_exp_ready"], 1)
        act.wait_ge(L["route_T_in_psum"], 1)
        act.activation(self.route_T[:, :], L.ps[0:E, 7, 0:S], ACT.Copy).then_inc(L["route_T_ready"], 1)
        for e in range(E):
            if e >= 2:
                act.wait_ge(L["expert_in_psum"], e - 1)
            for b in range(self.HC):
                if b % 4 == 0:
                    act.wait_ge(L["hidden_in_psum"], 2 * e + b // 4 + 1)
                k = e * self.HC + b
                act.activation(self.hT[e % 2][:, b, :], L.ps[:, e % 2 * 2 + b // 4, b % 4 * S:(b % 4 + 1) * S],
                               ACT.Gelu, bias=self.net.w(L.name, "b1")[:, k:k + 1]).then_inc(L["hidden_ready"], 1)

    def vector(self, dve):
        L, net, E, r = self.L, self.net, self.E, self.route
        self.norm.vector(dve)
        net.wait_weights(dve, L.name)
        o = L.order(dve, "expert_dve")
        dve.wait_ge(L["logits_in_psum"], 1)
        o.after(dve.tensor_tensor(r[:, 0, :], L.ps[:, 6, 0:E], net.w(L.name, "br"), ALU.add))
        o.after(dve.max(r[:, 1, :], r[:, 0, :]))
        o.after(dve.tensor_scalar(r[:, 2, :], r[:, 0, :], r[:, 1, 1:2], None, ALU.is_ge))
        dve.tensor_scalar(r[:, 3, :], r[:, 0, :], r[:, 1, 0:1], None, ALU.subtract).then_inc(L["logits_centred"], 1)
        dve.wait_ge(L["route_exp_ready"], 1)
        o.after(dve.tensor_tensor(r[:, 4, :], r[:, 3, :], r[:, 2, :], ALU.mult))
        o.after(dve.tensor_reduce(self.col[:, 0:1], r[:, 4, :], AX_X, ALU.add))
        o.after(dve.reciprocal(self.col[:, 1:2], self.col[:, 0:1]))
        dve.tensor_scalar(r[:, 3, :], r[:, 4, :], self.col[:, 1:2], None, ALU.mult).then_inc(L["route_ready"], 1)
        dve.wait_ge(L["route_ready"], 1)
        dve.wait_ge(L["b2_in_psum"], 1)
        o.after(dve.tensor_tensor(net.x[:, :], net.x[:, :], L.ps[:, 6, 0:D], ALU.add))
        for e in range(E):
            dve.wait_ge(L["expert_in_psum"], e + 1)
            if e:
                dve.wait_ge(L["expert_added"], e)
            dve.scalar_tensor_tensor(net.x[:, :], L.ps[:, 4 + e % 2, 0:D], r[:, 3, e:e + 1], net.x[:, :], ALU.mult,
                                     ALU.add).then_inc(L["expert_added"], 1)


class FeatureAttention:

    M = 64
    TILES = 7
    CHUNKS = NT // TILES
    TURNS = CHUNKS // BODY
    BANK_OF = (0, 1, 5)

    def __init__(self, L):
        self.L, self.net, self.norm = L, L.net, NormRows(L)
        sb, M = L.sb, self.M
        self.ctxT = [sb(f"ctxT{c}", [P, DC, self.TILES * P]) for c in range(4)]
        self.ctx = [sb(f"ctx{c}", [P, self.TILES, D + 1]) for c in range(4)]
        self.rf = [sb(f"rf{c}", [P, self.TILES * M]) for c in range(3)]
        self.kv = sb("kv", [M, D + 1])
        self.rf_q = sb("rf_q", [M, S])
        self.norm_col = sb("norm_col", [S, 2])
        self.y = sb("y", [S, D])

    def sync(self, sp):
        L, ins = self.L, self.net.ins
        ctxT = ins["ctxT"].rearrange("(c p) t -> p c t", p=P)
        ctx = ins["ctx"].rearrange("(j p) d -> p j d", p=P)
        n = self.TILES

        def turn(i, last):
            for j in range(BODY):
                m, c = BODY * i + j, RING4[j]
                sp.wait_ge(L["logits_in_psum"], m + 1)
                sp.dma_start(self.ctxT[c][:, :, :], ctxT[:, :, bass.ds(m * n * P, n * P)])\
                  .then_inc(L[f"ctxT_loaded{c}"], 16)
                sp.wait_ge(L["chunk_summed"], m + 1)
                sp.dma_start(self.ctx[c][:, :, 0:D], ctx[:, bass.ds(m * n, n), :])\
                  .then_inc(L[f"ctx_loaded{c}"], 16)
        turns(sp, self.TURNS, turn)
        self.net.load_weights(sp, LAYERS.index(L.name) + 1)

    def gpsimd(self, pool):
        L = self.L
        for c in range(4):
            last = pool.memset(self.ctx[c][:, :, D:D + 1], 1.0)
        last.then_inc(L["ones_ready"], 1)
        self.norm.gpsimd(pool)

    def tensor(self, pe):
        L, M, proj = self.L, self.M, self.net.w(self.L.name, "projection", c=DC)
        pe.sem_inc(L["logits_in_psum"], 3)
        pe.sem_inc(L["chunk_summed"], 3)
        self.norm.tensor(pe)
        self.net.wait_weights(pe, L.name)
        pe.wait_ge(L["xnT_ready"], 1)
        for c in range(DC):
            last = pe.matmul(L.ps[0:M, 3, 0:S], proj[:, c, :], self.norm.xnT[:, c, :], start=c == 0, stop=c == 1)
        last.then_inc(L["q_in_psum"], 1)
        pe.matmul(L.ps[:, 2, :], self.net.zeros_bf[:, 0:P], self.net.zeros_bf[:, :], start=True, stop=True,
                  skip_group_check=True)
        pe.wait_ge(L["ones_ready"], 1)

        def logits(n, i, j):
            c, bank = RING4[j], self.BANK_OF[RING3[j]]
            pe.wait_ge(L[f"ctxT_loaded{c}"], 16 * (uses(RING4, i, j) + 1))
            pe.wait_ge(L["rf_ready"], n + 1)
            for k in range(self.TILES):
                for e in range(DC):
                    last = pe.matmul(L.ps[:, bank, k * M:(k + 1) * M], self.ctxT[c][:, e, k * P:(k + 1) * P],
                                     proj[:, e, :], start=k == 0 and e == 0, stop=e == 1, skip_group_check=True)
            last.then_inc(L["logits_in_psum"], 1)

        logits(0, 0, 0)

        def turn(i, last):
            for j in range(BODY):
                n, c = BODY * i + j, RING4[j]
                if not (last and j == BODY - 1):
                    carry, nxt = divmod(j + 1, BODY)
                    logits(n + 1, i + carry, nxt)
                pe.wait_ge(L[f"ctx_loaded{c}"], 16 * (uses(RING4, i, j) + 1))
                pe.wait_ge(L["rf_ready"], n + 3)
                for k in range(self.TILES):
                    add = pe.matmul(L.ps[0:M, 2, 0:D + 1], self.rf[RING3[j]][:, k * M:(k + 1) * M],
                                    self.ctx[c][:, k, :], start=False, stop=True, skip_group_check=True)
                add.then_inc(L["chunk_summed"], 1)
        turns(pe, self.TURNS, turn)
        pe.wait_ge(L["kv_ready"], 1)
        pe.wait_ge(L["rf_q_ready"], 2)
        pe.matmul(L.ps[:, 4, 0:D + 1], self.rf_q[:, :], self.kv[:, :], start=True, stop=True)\
          .then_inc(L["y_in_psum"], 1)

    def scalar(self, act):
        L, M = self.L, self.M
        act.sem_inc(L["rf_ready"], 2)
        self.norm.scalar(act)
        act.wait_ge(L["q_in_psum"], 1)
        act.activation(self.rf_q[:, :], L.ps[0:M, 3, 0:S], ACT.Exp, scale=D ** -0.5).then_inc(L["rf_q_ready"], 1)
        act.wait_ge(L["rf_q_ready"], 1)
        act.mul(self.rf_q[:, :], self.rf_q[:, :], M ** -0.5).then_inc(L["rf_q_ready"], 1)

        def turn(i, last):
            for j in range(BODY):
                n, c = BODY * i + j, RING3[j]
                act.wait_ge(L["logits_in_psum"], n + 4)
                act.wait_ge(L["chunk_summed"], n + 2)
                act.activation(self.rf[c][:, :], L.ps[:, self.BANK_OF[c], 0:self.TILES * M], ACT.Exp,
                               scale=D ** -0.5).then_inc(L["rf_ready"], 1)
        turns(act, self.TURNS, turn)

    def vector(self, dve):
        L, net = self.L, self.net
        self.norm.vector(dve)
        o = L.order(dve, "feature_dve")
        dve.wait_ge(L["chunk_summed"], self.CHUNKS + 3)
        dve.tensor_copy(self.kv[:, :], L.ps[0:self.M, 2, 0:D + 1]).then_inc(L["kv_ready"], 1)
        dve.wait_ge(L["y_in_psum"], 1)
        o.after(dve.tensor_scalar(self.norm_col[:, 0:1], L.ps[:, 4, D:D + 1], 1e-6, None, ALU.add))
        o.after(dve.reciprocal(self.norm_col[:, 1:2], self.norm_col[:, 0:1]))
        o.after(dve.scalar_tensor_tensor(net.x[:, :], L.ps[:, 4, 0:D], self.norm_col[:, 1:2], net.x[:, :], ALU.mult,
                                         ALU.add))


class Float8Layer:

    MOST = 448.0

    def __init__(self, L):
        self.L, self.net, self.norm = L, L.net, NormRows(L)
        sb = L.sb
        self.scales = sb("scales", [P, 2, 8])
        self.work = sb("work", [P, DC * D])
        self.unit = sb("unit", [P, DC * D])
        self.wq = sb("wq", [P, DC * D], BF16)
        self.xq = sb("xq", [P, DC * S], BF16)
        self.y16 = sb("y16", [S, D], BF16)
        self.y = sb("y", [S, D])

    def sync(self, sp):
        self.net.load_weights(sp, LAYERS.index(self.L.name) + 1)

    def gpsimd(self, pool):
        L = self.L
        self.norm.gpsimd(pool)
        for k in range(2):
            pool.wait_ge(L["row_absmax_ready"], k + 1)
            pool.partition_all_reduce(self.scales[:, k, 1:2], self.scales[:, k, 0:1], P, ABSMAX)\
                .then_inc(L["absmax_ready"], 1)

    def scalar(self, act):
        self.norm.scalar(act)

    def tensor(self, pe):
        L = self.L
        self.norm.tensor(pe)
        pe.wait_ge(L["quantized"], 2)
        xq = self.xq[:, :].rearrange("p (c n) -> p c n", c=DC)
        project(pe, L.ps[:, 0, 0:D], xq, self.wq[:, :].rearrange("p (c n) -> p c n", c=DC), slice(0, D))\
            .then_inc(L["y_in_psum"], 1)

    def quantize(self, dve, o, k, out, src):
        L, sc, n = self.L, self.scales, src.shape[1]
        work, unit = self.work[:, 0:n], self.unit[:, 0:n]
        dve.tensor_reduce(sc[:, k, 0:1], src, AX_X, ALU.max, apply_absolute_value=True)\
           .then_inc(L["row_absmax_ready"], 1)
        dve.wait_ge(L["absmax_ready"], k + 1)
        o.after(dve.tensor_scalar(sc[:, k, 2:3], sc[:, k, 1:2], 1e-12, None, ALU.max))
        o.after(dve.reciprocal(sc[:, k, 3:4], sc[:, k, 2:3]))
        o.after(dve.tensor_scalar(sc[:, k, 4:5], sc[:, k, 3:4], self.MOST, self.MOST, ALU.mult, ALU.min))
        o.after(dve.reciprocal(sc[:, k, 5:6], sc[:, k, 4:5]))
        o.after(dve.tensor_scalar(work, src, sc[:, k, 4:5], self.MOST, ALU.mult, ALU.min))
        o.after(dve.tensor_scalar(work, work, -self.MOST, None, ALU.max))
        o.after(dve.tensor_scalar(unit.bitcast(U32), work.bitcast(U32), 0x7F800000, None, ALU.bitwise_and))
        o.after(dve.tensor_scalar(unit, unit, 2.0 ** -6, 1.5 * 2.0 ** 20, ALU.max, ALU.mult))
        o.after(dve.tensor_tensor(work, work, unit, ALU.add))
        dve.tensor_tensor(out, work, unit, ALU.subtract).then_inc(L["quantized"], 1)

    def vector(self, dve):
        L, net, sc = self.L, self.net, self.scales
        self.norm.vector(dve)
        net.wait_weights(dve, L.name)
        o = L.order(dve, "float8_dve")
        self.quantize(dve, o, 0, self.wq[:, :], net.w(L.name, "weight"))
        dve.wait_ge(L["quantized"], 1)
        dve.wait_ge(L["xnT_ready"], 1)
        self.quantize(dve, o, 1, self.xq[:, :], self.norm.xnT[:, :, :].rearrange("p c n -> p (c n)"))
        o.after(dve.tensor_tensor(sc[:, 0, 6:7], sc[:, 0, 5:6], sc[:, 1, 5:6], ALU.mult))
        dve.wait_ge(L["y_in_psum"], 1)
        o.after(dve.scalar_tensor_tensor(self.y[:, :], L.ps[:, 0, 0:D], sc[:, 0, 6:7], net.w(L.name, "bias"),
                                         ALU.mult, ALU.add))
        o.after(dve.tensor_copy(self.y16[:, :], self.y[:, :]))
        o.after(dve.tensor_tensor(net.x[:, :], net.x[:, :], self.y16[:, :], ALU.add))


class LinearAttention:

    def __init__(self, L):
        self.L, self.net, self.norm = L, L.net, NormRows(L)
        sb = L.sb
        self.qkvT = sb("qkvT", [P, 3, DC, S])
        self.small = sb("small", [P, 2, DC, S])
        self.sums = sb("sums", [P, 2, DC])
        self.y = sb("y", [S, D])

    def sync(self, sp):
        self.net.load_weights(sp, LAYERS.index(self.L.name) + 1)

    def gpsimd(self, pool):
        self.norm.gpsimd(pool)

    def tensor(self, pe):
        L, xnT = self.L, self.norm.xnT
        self.norm.tensor(pe)
        self.net.wait_weights(pe, L.name)
        pe.wait_ge(L["xnT_ready"], 1)
        for k, name in enumerate(("Wq", "Wk", "Wv")):
            for c in range(DC):
                last = project_T(pe, L.ps[:, k, c * S:(c + 1) * S], xnT, self.net.w(L.name, name, c=DC),
                                 slice(c * P, (c + 1) * P))
            last.then_inc(L["qkv_in_psum"], 1)
        pe.wait_ge(L["attended"], 1)
        project(pe, L.ps[:, 3, 0:D], self.qkvT[:, 0, :, :], self.net.w(L.name, "Wo", c=DC), slice(0, D))\
            .then_inc(L["y_in_psum"], 1)

    def scalar(self, act):
        L = self.L
        self.norm.scalar(act)
        act.wait_ge(L["small_ready"], 1)
        act.activation(self.small[:, :, :, :], self.small[:, :, :, :], ACT.Exp).then_inc(L["small_exp_ready"], 1)
        act.wait_ge(L["y_ready"], 1)
        act.activation(self.y[:, :], self.y[:, :], ACT.Gelu_apprx_tanh).then_inc(L["gelu_ready"], 1)

    def vector(self, dve):
        L, net, t = self.L, self.net, self.qkvT
        self.norm.vector(dve)
        net.wait_weights(dve, L.name)
        o = L.order(dve, "linear_dve")
        for k in range(3):
            dve.wait_ge(L["qkv_in_psum"], k + 1)
            for c in range(DC):
                o.after(dve.tensor_scalar(t[:, k, c, :], L.ps[:, k, c * S:(c + 1) * S],
                                          net.w(L.name, "bqkv")[:, k * DC + c:k * DC + c + 1], None, ALU.add))
        dve.tensor_scalar(self.small[:, :, :, :], t[:, 0:2, :, :], 0.0, None, ALU.min).then_inc(L["small_ready"], 1)
        dve.wait_ge(L["small_exp_ready"], 1)
        flat = lambda a: a.rearrange("p k c n -> p (k c n)")
        o.after(dve.tensor_scalar(flat(self.small[:, :, :, :]), flat(self.small[:, :, :, :]), -1.0, None, ALU.add))
        o.after(dve.scalar_tensor_tensor(flat(t[:, 0:2, :, :]), flat(t[:, 0:2, :, :]), 0.0,
                                         flat(self.small[:, :, :, :]), ALU.max, ALU.add))
        o.after(dve.tensor_scalar(flat(t[:, 0:2, :, :]), flat(t[:, 0:2, :, :]), 1.0, None, ALU.add))
        o.after(dve.tensor_reduce(self.sums[:, 0, :], t[:, 1, :, :], AX_X, ALU.add))
        o.after(dve.tensor_tensor(t[:, 2, :, :], t[:, 1, :, :], t[:, 2, :, :], ALU.mult))
        o.after(dve.tensor_reduce(self.sums[:, 1, :], t[:, 2, :, :], AX_X, ALU.add))
        for c in range(DC):
            o.after(dve.tensor_scalar(t[:, 1, c, :], t[:, 0, c, :], self.sums[:, 0, c:c + 1], 1e-6, ALU.mult, ALU.add))
        o.after(dve.reciprocal(t[:, 1, :, :], t[:, 1, :, :]))
        for c in range(DC):
            last = dve.scalar_tensor_tensor(t[:, 0, c, :], t[:, 0, c, :], self.sums[:, 1, c:c + 1], t[:, 1, c, :],
                                            ALU.mult, ALU.mult)
        last.then_inc(L["attended"], 1)
        dve.wait_ge(L["y_in_psum"], 1)
        dve.tensor_tensor(self.y[:, :], L.ps[:, 3, 0:D], net.w(L.name, "bo"), ALU.add).then_inc(L["y_ready"], 1)
        dve.wait_ge(L["gelu_ready"], 1)
        o.after(dve.tensor_tensor(net.x[:, :], net.x[:, :], self.y[:, :], ALU.add))


class AdaptedExpertLayer:

    E, HID, R = 4, 1024, 4
    HC = HID // P

    def __init__(self, L):
        self.L, self.net, self.norm = L, L.net, NormRows(L)
        sb, E, F = L.sb, self.E, self.HID
        self.base = sb("base", [S, F])
        self.lowT = sb("lowT", [P, S])
        self.adapted = [sb(f"adapted{c}", [S, F]) for c in range(2)]
        self.weighted = [sb(f"weighted{c}", [S, F]) for c in range(2)]
        self.h = sb("h", [S, F])
        self.hT = sb("hT", [P, self.HC, S])
        self.route = sb("route", [S, 4, E])
        self.ahead = sb("ahead", [S, E, E])
        self.col = sb("col", [S, 4])
        self.h_turned = Transposed(L, "hT", self.h, self.HC, self.hT, 4)

    def w(self, name, **split):
        return self.net.w(self.L.name, name, **split)

    def sync(self, sp):
        pass

    def gpsimd(self, pool):
        L = self.L
        self.norm.gpsimd(pool)
        pool.memset(self.h[:, :], 0.0).then_inc(L["h_summed"], 1)
        for e in range(self.E):
            pool.wait_ge(L["weighted_ready"], e + 1)
            pool.wait_ge(L["h_summed"], e + 1)
            pool.tensor_tensor(self.h[:, :], self.h[:, :], self.weighted[e % 2][:, :], ALU.add)\
                .then_inc(L["h_summed"], 1)

    def tensor(self, pe):
        L, xnT, E = self.L, self.norm.xnT, self.E
        self.norm.tensor(pe)
        self.net.wait_weights(pe, L.name)
        pe.wait_ge(L["xnT_ready"], 1)
        project(pe, L.ps[:, 6, 0:E], xnT, self.w("Wg", c=DC), slice(0, E)).then_inc(L["logits_in_psum"], 1)
        project_T(pe, L.ps[:, 7, 0:S], xnT, self.w("A", c=DC), slice(0, P)).then_inc(L["low_in_psum"], 1)
        for b in range(2):
            project(pe, L.ps[:, 4 + b, :], xnT, self.w("Wi", c=DC), slice(b * BANK, (b + 1) * BANK))\
                .then_inc(L["base_in_psum"], 1)
        pe.wait_ge(L["lowT_ready"], 1)
        for e in range(E):
            if e >= 2:
                pe.wait_ge(L["adapted_ready"], e - 1)
            rows_e = slice(32 * e, 32 * e + self.R)
            for b in range(2):
                last = pe.matmul(L.ps[:, e % 2 * 2 + b, :], self.lowT[rows_e, :],
                                 self.w("B")[rows_e, b * BANK:(b + 1) * BANK], start=True, stop=True,
                                 tile_position=(32 * e, 0))
            last.then_inc(L["adapter_in_psum"], 1)
        self.h_turned.tensor(pe, L["h_summed"], E + 1)
        self.h_turned.wait(pe)
        project(pe, L.ps[:, 6, 0:D], self.hT, self.w("Wo", c=self.HC), slice(0, D)).then_inc(L["y_in_psum"], 1)

    def scalar(self, act):
        L = self.L
        self.norm.scalar(act)
        act.wait_ge(L["low_in_psum"], 1)
        act.activation(self.lowT[:, :], L.ps[:, 7, 0:S], ACT.Copy).then_inc(L["lowT_ready"], 1)
        act.wait_ge(L["logits_centred"], 1)
        act.activation(self.route[:, 1, :], self.route[:, 1, :], ACT.Exp).then_inc(L["route_exp_ready"], 1)
        act.wait_ge(L["base_in_psum"], 2)
        act.activation(self.base[:, :], L.ps[:, 4:6, :].rearrange("p b n -> p (b n)"), ACT.Copy)\
           .then_inc(L["base_ready"], 1)
        act.wait_ge(L["route_ready"], 1)
        for e in range(self.E):
            act.wait_ge(L["adapted_ready"], e + 1)
            if e >= 2:
                act.wait_ge(L["h_summed"], e)
            act.activation(self.weighted[e % 2][:, :], self.adapted[e % 2][:, :], ACT.Relu,
                           scale=self.route[:, 3, e:e + 1]).then_inc(L["weighted_ready"], 1)
        self.h_turned.scalar(act)

    def vector(self, dve):
        L, net, E, r = self.L, self.net, self.E, self.route
        self.norm.vector(dve)
        net.wait_weights(dve, L.name)
        o = L.order(dve, "adapted_dve")
        dve.wait_ge(L["logits_in_psum"], 1)
        o.after(dve.tensor_tensor(r[:, 0, :], L.ps[:, 6, 0:E], self.w("bg"), ALU.add))
        o.after(dve.tensor_reduce(self.col[:, 0:1], r[:, 0, :], AX_X, ALU.max))
        dve.tensor_scalar(r[:, 1, :], r[:, 0, :], self.col[:, 0:1], None, ALU.subtract)\
           .then_inc(L["logits_centred"], 1)
        dve.wait_ge(L["route_exp_ready"], 1)
        o.after(dve.tensor_reduce(self.col[:, 1:2], r[:, 1, :], AX_X, ALU.add))
        o.after(dve.reciprocal(self.col[:, 2:3], self.col[:, 1:2]))
        o.after(dve.tensor_scalar(r[:, 2, :], r[:, 1, :], self.col[:, 2:3], None, ALU.mult))
        o.after(dve.memset(self.ahead[:, :, :], 0.0))
        for e in range(E):
            if e:
                o.after(dve.tensor_scalar(self.ahead[:, e, 0:e], r[:, 2, 0:e], r[:, 2, e:e + 1], None, ALU.is_ge))
            if e < E - 1:
                o.after(dve.tensor_scalar(self.ahead[:, e, e + 1:E], r[:, 2, e + 1:E], r[:, 2, e:e + 1], None,
                                          ALU.is_gt))
        o.after(dve.tensor_reduce(r[:, 0, :], self.ahead[:, :, :], AX_X, ALU.add))
        dve.scalar_tensor_tensor(r[:, 3, :], r[:, 0, :], 1.5, r[:, 2, :], ALU.is_lt, ALU.mult)\
           .then_inc(L["route_ready"], 1)
        dve.wait_ge(L["base_ready"], 1)
        for e in range(E):
            dve.wait_ge(L["adapter_in_psum"], e + 1)
            if e >= 2:
                dve.wait_ge(L["weighted_ready"], e - 1)
            b = e % 2 * 2
            dve.tensor_tensor(self.adapted[e % 2][:, :], L.ps[:, b:b + 2, :].rearrange("p b n -> p (b n)"),
                              self.base[:, :], ALU.add).then_inc(L["adapted_ready"], 1)
        dve.wait_ge(L["y_in_psum"], 1)
        o.after(dve.tensor_tensor(net.x[:, :], net.x[:, :], L.ps[:, 6, 0:D], ALU.add))





def bass_perceiver_kernel(nc, ins, out):
    with ExitStack() as ctx:
        net = Net(nc, ctx, ins)
        with Layer(net, "setup") as L:
            block = L.ctx.enter_context(nc.Block())

            @block.sync
            def _(sp):
                sp.dma_start(net.const_sb[:, :], ins["consts"]).then_inc(net.first_loaded, 16)
                sp.dma_start(net.x[:, :], ins["x_rows"]).then_inc(net.first_loaded, 16)
                net.load_weights(sp, 0)
                sp.wait_ge(net.first_loaded, 32)

            @block.gpsimd
            def _(pool):
                pool.memset(net.zeros_bf[:, :], 0.0)

            @block.vector
            def _(dve):
                dve.wait_ge(net.first_loaded, 32)
                dve.tensor_copy(net.ident_bf[:, :], net.const("identity"))
                dve.tensor_copy(net.causal_bf[:, :, :], times(net.const("causal"), 4))
                dve.tensor_copy(net.causal_T_bf[:, :, :], times(net.const("causal_T"), 4))

        steps = {
            "L0_xattn": lambda L: CrossAttention(L, causal=True, dequantizing=True),
            "L0_attn": LatentAttention,
            "L0_ffn": QuantizedGatedLayer,
            "L1_xattn": lambda L: CrossAttention(L, masked=True),
            "L1_attn": WideAttention,
            "L1_ffn": ExpertLayer,
            "L2_xattn": FeatureAttention,
            "L2_attn": CausalAttention,
            "L2_ffn": Float8Layer,
            "L3_xattn": lambda L: CrossAttention(L, turned=True),
            "L3_attn": LinearAttention,
            "L3_ffn": AdaptedExpertLayer,
        }
        for name in LAYERS:
            with Layer(net, name) as L:
                step = steps[name](L)
                block = L.ctx.enter_context(nc.Block())
                block.sync(step.sync)
                block.gpsimd(step.gpsimd)
                block.scalar(step.scalar)
                block.vector(step.vector)
                block.tensor(step.tensor)

        with Layer(net, "end") as L:
            block = L.ctx.enter_context(nc.Block())

            @block.sync
            def _(sp):
                sp.dma_start(out, net.x[:, :]).then_inc(L["stored"], 16)
                sp.wait_ge(L["stored"], 16)




def rows(a):
    return a.reshape(a.shape[0] // P, P, -1).transpose(1, 0, 2).reshape(P, -1)


def cols(v):
    return v.reshape(-1, P).T


def each(v):
    return np.broadcast_to(v.reshape(1, -1), (P, v.size))


def padded(a):
    return np.concatenate([a, np.zeros((P - a.shape[0], a.shape[1]), a.dtype)])


def swapped_halves(w, half):
    order = np.arange(DH)
    order[:half], order[half:2 * half] = np.arange(half, 2 * half), np.arange(half)
    return w.reshape(w.shape[0], H, DH)[:, :, order].reshape(w.shape[0], D)


def packed(g):
    def xattn(n, turn):
        w = (lambda a: a) if n == "L0_xattn" else (lambda a: a.T)
        got = {k: rows(w(g(f"{n}_{k}"))) for k in ("Wq", "Wk", "Wv", "Wo")}
        got |= {"bq": cols(g(f"{n}_bq")), "bk": cols(g(f"{n}_bk")), "bv": each(g(f"{n}_bv")), "bo": each(g(f"{n}_bo"))}
        if turn:
            got |= {"Wq_swapped": rows(swapped_halves(w(g(f"{n}_Wq")), 1)),
                    "bq_swapped": cols(swapped_halves(g(f"{n}_bq")[None, :], 1)[0]),
                    "theta": cols(np.repeat(g(f"{n}_theta"), DH)), "gate": each(g(f"{n}_gate"))}
        return got

    a = lambda k: g(f"L0_attn_{k}")
    qkv = g("L2_attn_Wqkv").transpose(1, 0, 2)
    bqkv = g("L2_attn_bqkv")
    lora_A = np.zeros((D, P), np.float32).reshape(D, 4, 32)
    lora_A = np.concatenate([g("L3_ffn_A").transpose(2, 0, 1), lora_A[:, :, 4:]], axis=2).reshape(D, P)
    lora_B = g("L3_ffn_B").transpose(0, 2, 1)
    lora_B = np.concatenate([lora_B, np.zeros((4, 28, 1024), np.float32)], axis=1).reshape(P, 1024)
    r = lambda k: g(f"L3_attn_{k}")
    return {
        "L0_xattn": xattn("L0_xattn", False),
        "L0_attn": {"W_q": rows(a("W_q")), "W_q_swapped": rows(swapped_halves(a("W_q"), 8)),
                    "W_dkv": rows(a("W_dkv")), "W_uk": padded(a("W_uk")),
                    "W_uk_swapped": padded(swapped_halves(a("W_uk"), 8)), "W_uv": padded(a("W_uv")),
                    "W_o": rows(a("W_o")), "ln_gamma": each(a("ln_gamma")), "ln_beta": each(a("ln_beta"))},
        "L0_ffn": {k: rows(g(f"L0_ffn_{k}")) for k in ("w_gate", "w_up", "w_down")},
        "L1_xattn": xattn("L1_xattn", False),
        "L1_attn": {"w_qkv": rows(g("L1_attn_w_qkv")), "w_out": rows(g("L1_attn_w_out")),
                    "b_out": each(g("L1_attn_b_out")), "ln_gamma": each(g("L1_attn_ln_gamma")),
                    "ln_beta": each(g("L1_attn_ln_beta"))},
        "L1_ffn": {"Wr": rows(g("L1_ffn_Wr")), "br": each(g("L1_ffn_br")), "b1": cols(g("L1_ffn_b1").reshape(-1)),
                   "b2": padded(g("L1_ffn_b2"))},
        "L2_xattn": {"projection": rows(g("L2_xattn_projection").T)},
        "L2_attn": {"Wqk": rows(np.concatenate([qkv[:, :, 0:16].reshape(D, D), qkv[:, :, 16:32].reshape(D, D)], 1)),
                    "Wv": rows(qkv[:, :, 32:48].reshape(D, D)), "Wout": rows(g("L2_attn_Wout")),
                    "bqk": cols(np.concatenate([bqkv[:, 0:16].reshape(-1), bqkv[:, 16:32].reshape(-1)])),
                    "bv": each(bqkv[:, 32:48].reshape(-1)), "bout": each(g("L2_attn_bout"))},
        "L2_ffn": {"weight": rows(g("L2_ffn_weight").T), "bias": each(g("L2_ffn_bias"))},
        "L3_xattn": xattn("L3_xattn", True),
        "L3_attn": {"Wq": rows(r("Wq")), "Wk": rows(r("Wk")), "Wv": rows(r("Wv")), "Wo": rows(r("Wo")),
                    "bqkv": np.concatenate([cols(r("bq")), cols(r("bk")), cols(r("bv"))], 1), "bo": each(r("bo"))},
        "L3_ffn": {"Wg": rows(g("L3_ffn_Wg").T), "bg": each(g("L3_ffn_bg")), "Wi": rows(g("L3_ffn_Wi").T),
                   "Wo": rows(g("L3_ffn_Wo").T), "A": rows(lora_A), "B": lora_B},
    }


def laid_out(inputs):
    def g(name):
        return np.asarray(inputs[name])

    arrays = {}
    ctx_rows = g("ctx_1024").reshape(T, D)
    mask = g("mask_BxS2_bf1").reshape(T).view(np.uint8)
    arrays["ctxT"] = ctx_rows.T
    arrays["ctx"] = ctx_rows
    arrays["mask_rows"] = mask.reshape(NT, P)
    arrays["x_rows"] = g("x").reshape(S, D)
    arrays["experts_W1"] = g("L1_ffn_W1")
    arrays["experts_W2"] = g("L1_ffn_W2")
    arrays["consts"] = constants()
    for layer, parts in packed(g).items():
        for name, n in PACKS[layer]:
            assert parts[name].shape == (P, n), (layer, name, parts[name].shape)
        arrays[f"pack_{layer}"] = np.concatenate([parts[name] for name, _ in PACKS[layer]], axis=1)
    return {k: np.ascontiguousarray(v) for k, v in arrays.items()}


def kernel(**inputs):
    import concourse.bacc as bacc
    from concourse.bass_utils import run_bass_kernel_spmd

    nc = bacc.Bacc("TRN2", target_bir_lowering=False, num_devices=1)
    arrays = {f"in_{k}": v for k, v in laid_out(inputs).items()}
    ins = {k[3:]: nc.dram_tensor(k, v.shape, mybir.dt.from_np(v.dtype), kind="ExternalInput").ap()
           for k, v in arrays.items()}
    out = nc.dram_tensor("out_rows", (S, D), F32, kind="ExternalOutput").ap()
    bass_perceiver_kernel(nc, ins, out)
    result = run_bass_kernel_spmd(nc, [arrays], core_ids=[0])
    return result.results[0]["out_rows"].reshape(1, S, D)
```
